# Optimizing a Trainium2 kernel written in Bass

```python
import numpy as np
import jax
import jax.numpy as jnp

def _softmax(x, axis=-1):
    return jax.nn.softmax(x, axis=axis)

def _gelu(x):
    return jax.nn.gelu(x, approximate=True)

def _silu(x):
    return jax.nn.silu(x)

def _sigmoid(x):
    return jax.nn.sigmoid(x)

def _layernorm(x, axis=-1, eps=1e-05):
    m = jnp.mean(x, axis=axis, keepdims=True)
    v = jnp.var(x, axis=axis, keepdims=True)
    return (x - m) / jnp.sqrt(v + eps)

def _scatter_add(tgt, idx, src, axis=0):
    return tgt.at[idx].add(src)

def _segment_sum(src, seg, n):
    return jax.ops.segment_sum(src, seg, n)
kernel_name = 'mk_prb_d1_jaxref_r4_463ead'

def setup_inputs(seed: int=0):
    np.random.seed(seed)
    _w = jnp.asarray

    def _L0_attn_setup():
        import jax, jax.numpy as jnp
        import numpy as np
        B, S, D, DV = (1, 1024, 256, 256)
        key = jax.random.key(seed)
        kq, kk, kv, ks, kp = jax.random.split(key, 5)
        return {'q': jax.random.normal(kq, (B, S, D), dtype=jnp.float32), 'k': jax.random.normal(kk, (B, S, D), dtype=jnp.float32), 'v': jax.random.normal(kv, (B, S, DV), dtype=jnp.float32), 'scale_factor': jax.random.normal(ks, (1,), dtype=jnp.float32), 'dropout_p': jax.random.uniform(kp, (1,), dtype=jnp.float32)}
    _L0_attn_in = _L0_attn_setup()

    def _L0_ffn_setup():
        import jax, jax.numpy as jnp
        import numpy as np
        import math
        N_EMBD = 256
        HIDDEN = 4 * N_EMBD
        N_EXPERTS = 8
        TOP_K = 2
        B, T = (4, 512)

        def new_gelu(x):
            c = math.sqrt(2.0 / math.pi)
            return 0.5 * x * (1.0 + jnp.tanh(c * (x + 0.044715 * x * x * x)))

        def _moe_forward(x, Wfc_s, bfc_s, Wproj_s, bproj_s, Wr, Wfc, bfc, Wproj, bproj):
            Bb, Tt, C = x.shape
            xf = x.reshape(Bb * Tt, C)
            N = Bb * Tt
            shared = new_gelu(xf @ Wfc_s + bfc_s) @ Wproj_s + bproj_s
            logits = xf @ Wr
            probs = jax.nn.softmax(logits, axis=-1)
            topk_p, topk_i = jax.lax.top_k(probs, TOP_K)
            topk_p = topk_p / jnp.sum(topk_p, axis=-1, keepdims=True)
            gate = jnp.zeros((N, N_EXPERTS), dtype=xf.dtype)
            gate = gate.at[jnp.arange(N)[:, None], topk_i].add(topk_p)
            routed = jnp.zeros_like(xf)
            for e in range(N_EXPERTS):
                h = new_gelu(xf @ Wfc[e] + bfc[e]) @ Wproj[e] + bproj[e]
                routed = routed + h * gate[:, e:e + 1]
            return (shared + routed).reshape(Bb, Tt, C)
        key = jax.random.key(seed)
        ks = jax.random.split(key, 10)
        s = 0.02
        return {'x': jax.random.normal(ks[0], (B, T, N_EMBD), dtype=jnp.float32), 'Wfc_s': jax.random.normal(ks[1], (N_EMBD, HIDDEN), dtype=jnp.float32) * s, 'bfc_s': jnp.zeros((HIDDEN,), dtype=jnp.float32), 'Wproj_s': jax.random.normal(ks[2], (HIDDEN, N_EMBD), dtype=jnp.float32) * s, 'bproj_s': jnp.zeros((N_EMBD,), dtype=jnp.float32), 'Wr': jax.random.normal(ks[3], (N_EMBD, N_EXPERTS), dtype=jnp.float32) * s, 'Wfc': jax.random.normal(ks[4], (N_EXPERTS, N_EMBD, HIDDEN), dtype=jnp.float32) * s, 'bfc': jnp.zeros((N_EXPERTS, HIDDEN), dtype=jnp.float32), 'Wproj': jax.random.normal(ks[5], (N_EXPERTS, HIDDEN, N_EMBD), dtype=jnp.float32) * s, 'bproj': jnp.zeros((N_EXPERTS, N_EMBD), dtype=jnp.float32)}
    _L0_ffn_in = _L0_ffn_setup()
    _d = {'L0_attn_q': _L0_attn_in['q'], 'L0_attn_k': _L0_attn_in['k'], 'L0_attn_v': _L0_attn_in['v'], 'L0_attn_scale_factor': _L0_attn_in['scale_factor'], 'L0_attn_dropout_p': _L0_attn_in['dropout_p'], 'L0_ffn_Wfc_s': _L0_ffn_in['Wfc_s'], 'L0_ffn_bfc_s': _L0_ffn_in['bfc_s'], 'L0_ffn_Wproj_s': _L0_ffn_in['Wproj_s'], 'L0_ffn_bproj_s': _L0_ffn_in['bproj_s'], 'L0_ffn_Wr': _L0_ffn_in['Wr'], 'L0_ffn_Wfc': _L0_ffn_in['Wfc'], 'L0_ffn_bfc': _L0_ffn_in['bfc'], 'L0_ffn_Wproj': _L0_ffn_in['Wproj'], 'L0_ffn_bproj': _L0_ffn_in['bproj']}
    _x0 = _d['L0_attn_q']
    _d['L0_attn_q'] = jax.random.normal(jax.random.fold_in(jax.random.key(seed), 1), (8, 512, 256), dtype=_x0.dtype)
    del _x0
    return _d

def reference(L0_attn_q, L0_attn_k, L0_attn_v, L0_attn_scale_factor, L0_attn_dropout_p, L0_ffn_Wfc_s, L0_ffn_bfc_s, L0_ffn_Wproj_s, L0_ffn_bproj_s, L0_ffn_Wr, L0_ffn_Wfc, L0_ffn_bfc, L0_ffn_Wproj, L0_ffn_bproj):

    def _L0_attn_ref(q, k, v, scale_factor, dropout_p):
        import jax, jax.numpy as jnp
        import numpy as np
        B, S, D, DV = (1, 1024, 256, 256)
        b, s, d = q.shape
        step = s // 4
        scale = q[:, ::step].reshape(b, -1)
        qk = jnp.einsum('bsd,btd->bst', q, k)
        scaled_qk = qk * scale[:, None, :]
        softmax_qk = jax.nn.softmax(scaled_qk, axis=-1)
        return jnp.einsum('bst,btv->bsv', softmax_qk, v)

    def _L0_ffn_ref(x, Wfc_s, bfc_s, Wproj_s, bproj_s, Wr, Wfc, bfc, Wproj, bproj):
        import jax, jax.numpy as jnp
        import numpy as np
        import math
        N_EMBD = 256
        HIDDEN = 4 * N_EMBD
        N_EXPERTS = 8
        TOP_K = 2
        B, T = (4, 512)

        def new_gelu(x):
            c = math.sqrt(2.0 / math.pi)
            return 0.5 * x * (1.0 + jnp.tanh(c * (x + 0.044715 * x * x * x)))

        def _moe_forward(x, Wfc_s, bfc_s, Wproj_s, bproj_s, Wr, Wfc, bfc, Wproj, bproj):
            Bb, Tt, C = x.shape
            xf = x.reshape(Bb * Tt, C)
            N = Bb * Tt
            shared = new_gelu(xf @ Wfc_s + bfc_s) @ Wproj_s + bproj_s
            logits = xf @ Wr
            probs = jax.nn.softmax(logits, axis=-1)
            topk_p, topk_i = jax.lax.top_k(probs, TOP_K)
            topk_p = topk_p / jnp.sum(topk_p, axis=-1, keepdims=True)
            gate = jnp.zeros((N, N_EXPERTS), dtype=xf.dtype)
            gate = gate.at[jnp.arange(N)[:, None], topk_i].add(topk_p)
            routed = jnp.zeros_like(xf)
            for e in range(N_EXPERTS):
                h = new_gelu(xf @ Wfc[e] + bfc[e]) @ Wproj[e] + bproj[e]
                routed = routed + h * gate[:, e:e + 1]
            return (shared + routed).reshape(Bb, Tt, C)
        return _moe_forward(x, Wfc_s, bfc_s, Wproj_s, bproj_s, Wr, Wfc, bfc, Wproj, bproj)
    x = L0_attn_q
    xn = _layernorm(x, axis=-1)
    x = x + _L0_attn_ref(xn, L0_attn_k, L0_attn_v, L0_attn_scale_factor, L0_attn_dropout_p) + _L0_ffn_ref(xn, L0_ffn_Wfc_s, L0_ffn_bfc_s, L0_ffn_Wproj_s, L0_ffn_bproj_s, L0_ffn_Wr, L0_ffn_Wfc, L0_ffn_bfc, L0_ffn_Wproj, L0_ffn_bproj)
    return x

_drawn_inputs = setup_inputs


def setup_inputs(seed=0):
    import zlib

    import numpy as np

    out = dict(_drawn_inputs(seed))
    spreads = {'L0_ffn_bfc_s': (0.0, 0.305),
     'L0_ffn_bproj_s': (0.0, 0.1),
     'L0_ffn_bfc': (0.0, 0.444),
     'L0_ffn_bproj': (0.0, 0.1)}
    factors = {}
    for name, (base, spread) in spreads.items():
        noise = np.random.default_rng([zlib.crc32(name.encode()), seed]).standard_normal(out[name].shape)
        drawn = base * np.exp(spread * noise) if base else spread * noise
        out[name] = jnp.asarray(drawn.astype(out[name].dtype))
    for name, factor in factors.items():
        out[name] = (out[name] * factor).astype(out[name].dtype)
    return out
```

```python
from contextlib import ExitStack, contextmanager

import concourse.bass as bass
from concourse import mybir

TOKENS, D = 4096, 256
BATCH, QLEN, KEYS = 8, 512, 1024
HID, EXPERTS, TOP = 1024, 8, 2
P = 128
TILE = 256
SUB = TILE // P
DC = D // P
HC = HID // P
BANKS = 4
SHARED = TOKENS // TILE
BLK_SHIFT = 8
ROUTED = (TOKENS * TOP + EXPERTS * (TILE - 1)) // TILE
CAP = TOKENS + TILE
SPARE = EXPERTS * CAP
QT = TOKENS // P
KC = KEYS // P
WS = 256.0
EPS = 1e-5
ROW = 2 * D


def moe_attention_block(nc, q, k, v, wfc_s, bfc_s, wproj_s, bproj_s, wr, wfc, bfc, wproj, bproj, out):
    f32, f16 = mybir.dt.float32, mybir.dt.float16
    i32, u32 = mybir.dt.int32, mybir.dt.uint32
    ALU = mybir.AluOpType
    ACT = mybir.ActivationFunctionType
    AX = mybir.AxisListType.X
    ds = bass.ds

    x_rows = q.rearrange("b s d -> (b s) d")
    out_rows = out.rearrange("b s d -> (b s) d")
    k_rows = k.rearrange("b s d -> (b s) d")
    v_rows = v.rearrange("b s d -> (b s) d")
    wfc_rows = wfc.rearrange("e c n -> (e c) n")
    wproj_rows = wproj.rearrange("e h n -> (e h) n")
    bfc_rows = bfc.rearrange("e (h p) -> (e h) p", p=P)
    bfc_s_rows = bfc_s.rearrange("(h p) -> h p", p=P)

    def dram(name, shape, dt):
        return nc.dram_tensor(name, shape, dt, kind="Internal").ap()

    slots_x = dram("slots_x", (SPARE + TILE, ROW), f16)
    slots_y = dram("slots_y", (ROUTED * TILE, D), f32)
    shared_y = dram("shared_y", (TOKENS, D), f32)
    xt_d = dram("xt_d", (SHARED * P, 2 * DC * TILE), f16)
    key_scale = dram("key_scale", (SHARED, SUB * D), f32)
    wpack = dram("wpack", (EXPERTS * P, 4 * 2048), f16)
    bfct_d = dram("bfct_d", (P, EXPERTS * HC), f32)

    ctx = ExitStack()
    with ctx:
        def sb(name, shape, dt):
            return ctx.enter_context(nc.sbuf_tensor(name, shape, dt))

        def sem(name):
            return ctx.enter_context(nc.semaphore(name))

        def sem2(name):
            return [sem(name + "_even"), sem(name + "_odd")]

        def sb2(name, shape, dt):
            return [sb(name + str(n), shape, dt) for n in range(2)]

        ident_h = sb("ident_h", [P, P], f16)
        ident_f = sb("ident_f", [P, P], f32)
        before = sb("before", [P, P], f16)
        ones_h = sb("ones_h", [P, P], f16)
        iota_e = sb("iota_e", [P, EXPERTS], f32)
        region = sb("region", [P, EXPERTS], f32)
        step_no = sb("step_no", [1, ROUTED], f32)
        neg_half = sb("neg_half", [P, SUB], f32)
        zeros = sb("zeros", [P, SUB, ROW], f16)
        one_row = sb("one_row", [P, EXPERTS], f32)
        x_in = sb2("x_in", [P, SUB, D], f32)
        stats = sb("stats", [P, SUB, 6], f32)
        mean_var = sb2("mean_var", [P, SUB, 2], f32)
        var_eps = sb2("var_eps", [P, SUB], f32)
        rstd = sb2("rstd", [P, SUB], f32)
        xn = sb2("xn", [P, SUB, D], f32)
        x_split = sb2("x_split", [P, SUB, ROW], f16)
        x_t = sb2("x_t", [P, 2 * DC, TILE], f16)
        wr32 = sb("wr32", [P, DC, EXPERTS], f32)
        wr_s = sb("wr_s", [P, DC, 2 * EXPERTS], f16)
        logits = sb("logits", [P, SUB, EXPERTS], f32)
        top_v = sb("top_v", [P, SUB, 8], f32)
        top_i = sb("top_i", [P, SUB, 8], u32)
        top_f = sb("top_f", [P, SUB, TOP], f32)
        chosen = sb("chosen", [P, SUB, TOP, EXPERTS], f32)
        mask = sb2("mask", [P, SUB, EXPERTS], f16)
        mask_sum = sb("mask_sum", [P, EXPERTS], f16)
        slot_of = sb("slot_of", [P, SUB, EXPERTS], f32)
        picked = sb("picked", [P, SUB, TOP, EXPERTS], f32)
        pos_f = sb("pos_f", [P, SUB * TOP], f32)
        pos_i = sb2("pos_i", [P, SUB * TOP], i32)
        pos_all = sb("pos_all", [P, QT * TOP], f32)
        exp_all = sb("exp_all", [P, QT * TOP], f32)
        match_e = sb("match_e", [P, QT * TOP, EXPERTS], f32)
        shift_e = sb("shift_e", [P, EXPERTS], f32)
        shift_t = sb("shift_t", [P, QT * TOP], f32)
        y_row_all = sb("y_row_all", [P, QT * TOP], i32)
        gap_all = sb("gap_all", [P, QT], f32)
        w_stage = sb2("w_stage", [P, 2048], f32)
        w_split = sb2("w_split", [P, 4096], f16)
        w_shared = sb2("w_shared", [P, 4096], f16)
        w_fc = sb2("w_fc", [P, 4096], f16)
        w_pj = sb2("w_pj", [P, 4096], f16)
        b_rows = sb("b_rows", [EXPERTS * HC + HC, P], f32)
        b_t = sb("b_t", [P, EXPERTS * HC + HC], f32)
        b_fc = sb2("b_fc", [P, HC], f32)
        b_pj = sb2("b_pj", [P, D], f32)
        b_pj_s = sb("b_pj_s", [P, D], f32)
        h32 = sb("h32", [P, HC, TILE], f32)
        h_split = sb2("h_split", [P, 2, HC, TILE], f16)
        y_sb = sb2("y_sb", [P, SUB, D], f32)
        cnt = sb("cnt", [P, EXPERTS], f32)
        cnt_i = sb("cnt_i", [P, EXPERTS], i32)
        blk_i = sb("blk_i", [P, EXPERTS], i32)
        blk = sb("blk", [P, EXPERTS], f32)
        blk_end = sb("blk_end", [P, EXPERTS], f32)
        past = sb("past", [1, ROUTED, EXPERTS], f32)
        past_blk = sb("past_blk", [1, ROUTED, EXPERTS], f32)
        step_e = sb("step_e", [1, ROUTED], f32)
        step_b = sb("step_b", [1, ROUTED], f32)
        step_r = sb("step_r", [1, ROUTED], f32)
        tab_e = sb("tab_e", [1, ROUTED], i32)
        tab_x = sb("tab_x", [1, ROUTED], i32)
        tab_pad = sb("tab_pad", [1, EXPERTS], i32)
        k_t = sb("k_t", [P, 2 * DC, KEYS], f16)
        v_split = sb("v_split", [P, 2, KC, D], f16)
        q_t = sb2("q_t", [P, 2 * DC, TILE], f16)
        scale_b = sb2("scale_b", [P, KEYS], f32)
        prob = sb2("prob", [P, KEYS], f32)
        row_max = sb2("row_max", [P, 1], f32)
        neg_max = sb2("neg_max", [P, 1], f32)
        row_sum = sb2("row_sum", [P, 1], f32)
        inv_sum = sb2("inv_sum", [P, 1], f32)
        p_t = sb2("p_t", [P, 2, KC, P], f16)
        gap_exp = sb("gap_exp", [P, QT], f32)
        gap_den = sb("gap_den", [P, QT], f32)
        gates = sb("gates", [P, QT, TOP], f32)
        gate_u = sb2("gate_u", [P, TOP], f32)
        pos_u = sb2("pos_u", [P, TOP], i32)
        y_rows = sb2("y_rows", [P, TOP, D], f32)
        base_y = sb2("base_y", [P, D], f32)
        base_x = sb2("base_x", [P, D], f32)
        o_sb = sb2("o_sb", [P, D], f32)

        ps_h = ctx.enter_context(nc.psum_tensor("ps_h", [P, BANKS * 512], f32))
        ps_y = [ctx.enter_context(nc.psum_tensor(f"ps_y{a}", [P, 512], f32)) for a in range(2)]
        ps_t = ctx.enter_context(nc.psum_tensor("ps_t", [P, 1024], f32))
        tr16 = ps_t[:, 0:512].bitcast(f16)
        misc = ps_t[:, 512:1024]
        lg_ps = misc[:, 0:SUB * 2 * EXPERTS]
        rk_ps = misc[:, 32:32 + SUB * EXPERTS]
        cn_ps = misc[:, 48:48 + EXPERTS]
        bt_ps = misc[:, 128:128 + EXPERTS * HC + HC]

        s_const = sem("s_const")
        s_bias_in = sem("s_bias_in")
        s_wr_in = sem("s_wr_in")
        s_bpj_in = sem("s_bpj_in")
        s_x_in = sem2("s_x_in")
        s_row_out = sem2("s_row_out")
        s_xt_out = sem2("s_xt_out")
        s_w_in = sem2("s_w_in")
        s_w_out = sem2("s_w_out")
        s_bt_out = sem("s_bt_out")
        s_scat = sem2("s_scat")
        s_y_out = sem2("s_y_out")
        s_pad = sem("s_pad")
        s_xs_in = sem2("s_xs_in")
        s_wfc_in = sem2("s_wfc_in")
        s_bfc_in = sem2("s_bfc_in")
        s_wpj_in = sem2("s_wpj_in")
        s_bpjx_in = sem2("s_bpjx_in")
        s_kv_in = sem2("s_kv_in")
        s_q_in = sem2("s_q_in")
        s_sc_in = sem2("s_sc_in")
        s_by_in = sem2("s_by_in")
        s_bx_in = sem2("s_bx_in")
        s_gat = sem2("s_gat")
        s_out = sem2("s_out")
        s_iota = sem("s_iota")
        s_bt_tr = sem("s_bt_tr")
        s_bt = sem("s_bt")
        s_wr = sem("s_wr")
        s_lna = sem("s_lna")
        s_rstd = sem("s_rstd")
        s_lnb = sem("s_lnb")
        s_tr = sem("s_tr")
        s_xt = sem("s_xt")
        s_logit = sem("s_logit")
        s_ra = sem("s_ra")
        s_rank = sem("s_rank")
        s_rb = sem("s_rb")
        s_msum0 = sem("s_msum0")
        s_count = sem("s_count")
        s_table = sem("s_table")
        s_y_rows = sem("s_y_rows")
        s_wsc = sem("s_wsc")
        s_whi = sem("s_whi")
        s_wlo = sem("s_wlo")
        s_mm1 = sem("s_mm1")
        s_gelu = sem("s_gelu")
        s_hhi = sem("s_hhi")
        s_hlo = sem("s_hlo")
        s_mm2 = sem("s_mm2")
        s_ev = sem("s_ev")
        s_kv_hi = sem("s_kv_hi")
        s_kv_lo = sem("s_kv_lo")
        s_k_tr = sem("s_k_tr")
        s_k_t = sem("s_k_t")
        s_gexp = sem("s_gexp")
        s_gate = sem("s_gate")
        s_qk = sem("s_qk")
        s_mul = sem("s_mul")
        s_nm = sem("s_nm")
        s_exp = sem("s_exp")
        s_pt = sem("s_pt")
        s_phi = sem("s_phi")
        s_plo = sem("s_plo")
        s_pv = sem("s_pv")
        s_meta = sem("s_meta")
        s_base = sem("s_base")
        s_fin = sem("s_fin")

        LNA, LNB, RA, RB, TABLE, Y_ROWS, FIN = 5, 4, 10, 7, 17, 6, 4
        CONSTS = 10
        PREPS = 2 + SHARED

        def chain(eng, s, start):
            at = [start]

            def link(ins, wait=False):
                ins.then_inc(s, 1)
                at[0] = at[0] + 1
                if wait:
                    wait_ge(eng, s, at[0])
            return link

        def wait_ge(eng, s, value):
            eng.wait_ge(s, value)
            eng.nop(nofuse=True)

        @contextmanager
        def pairs(eng, first, end):
            with eng.Fori(0, (end - first) // 2) as m:
                yield eng.snap(m * 2 + first)

        def nth(n, par, each=16):
            return (n - par) * (each // 2) + each

        def rows(ap, first, n):
            return ap[ds(first, n), :].rearrange("(a p) d -> p a d", p=P)

        block = ctx.enter_context(nc.Block())

        @block.sync
        def _(sp):
            def load_x(i, par, first=False):
                if not first:
                    wait_ge(sp, s_lnb, (i - 1) * LNB)
                sp.dma_start(x_in[par][:, :, :], rows(x_rows, i * TILE, TILE)).then_inc(s_x_in[par], 16)

            def load_w(n, par, fc_src, pj_src, first=False):
                if not first:
                    wait_ge(sp, s_wlo, n - 1)
                dst = w_stage[par]
                if par == 0:
                    sp.dma_start(dst[:, :].rearrange("p (c n) -> p c n", c=DC),
                                 fc_src.rearrange("(c p) n -> p c n", p=P)).then_inc(s_w_in[0], 16)
                else:
                    sp.dma_start(dst[:, :].rearrange("p (c n) -> p c n", c=HC),
                                 pj_src.rearrange("(c p) n -> p c n", p=P)).then_inc(s_w_in[1], 16)

            def load_expert(i, par):
                load_w(i + 2, par, wfc_rows[ds((i - par) * (D // 2), D), :],
                       wproj_rows[ds((i - par) * (HID // 2), HID), :])

            def store_w(i, par):
                wait_ge(sp, s_wlo, i + 3)
                sp.dma_start(wpack[ds((i - par) * (P // 2), P), par * 4096:(par + 1) * 4096],
                             w_split[par][:, :]).then_inc(s_w_out[par], 16)

            def store_row(i, par):
                wait_ge(sp, s_lnb, i * LNB + 2)
                sp.dma_start(key_scale[ds(i, 1), :], xn[par][0:1, :, :].rearrange("p a d -> p (a d)")
                             ).then_inc(s_row_out[par], 16)

            def store_xt(i, par):
                wait_ge(sp, s_xt, i + 1)
                sp.dma_start(xt_d[ds(i * P, P), :], x_t[par][:, :, :].rearrange("p c n -> p (c n)")
                             ).then_inc(s_xt_out[par], 16)

            def store_shared(i, par):
                wait_ge(sp, s_ev, 2 * i + 2)
                sp.dma_start(rows(shared_y, i * TILE, TILE), y_sb[par][:, :, :]).then_inc(s_y_out[par], 16)

            load_x(0, 0, first=True)
            load_w(0, 0, wfc_s, wproj_s, first=True)
            sp.dma_start(wr32[:, :, :], wr.rearrange("(c p) e -> p c e", p=P)).then_inc(s_wr_in, 16)
            sp.dma_start(b_rows[0:EXPERTS * HC, :], bfc_rows).then_inc(s_bias_in, 16)
            sp.dma_start(b_rows[EXPERTS * HC:, :], bfc_s_rows).then_inc(s_bias_in, 16)
            load_x(1, 1, first=True)
            load_w(1, 1, wfc_s, wproj_s, first=True)
            sp.dma_start(b_pj_s[:, :], bproj_s.partition_broadcast(P)).then_inc(s_bpj_in, 16)
            store_row(0, 0)
            store_xt(0, 0)
            load_x(2, 0)
            load_expert(0, 0)
            load_expert(1, 1)
            store_row(1, 1)
            wait_ge(sp, s_bt, 1)
            sp.dma_start(bfct_d, b_t[:, 0:EXPERTS * HC]).then_inc(s_bt_out, 16)
            store_w(0, 0)
            store_xt(1, 1)

            def body1(i, par, last=False):
                if not last:
                    load_x(i + 2, par)
                load_expert(i + 1, 1 - par)
                store_row(i + 1, 1 - par)
                store_w(i, par)
                store_xt(i + 1, 1 - par)
                store_shared(i - 1, 1 - par)

            with pairs(sp, 1, SHARED - 3) as i:
                body1(i, 1)
                body1(i + 1, 0)
            body1(SHARED - 3, 1)
            body1(SHARED - 2, 0, last=True)
            wait_ge(sp, s_wlo, PREPS - 1)
            sp.dma_start(w_stage[0][:, :].rearrange("p (c n) -> p c n", c=KC),
                         k_rows.rearrange("(c p) n -> p c n", p=P)).then_inc(s_kv_in[0], 16)
            store_w(SHARED - 1, 1)
            sp.dma_start(w_stage[1][:, :].rearrange("p (c n) -> p c n", c=KC),
                         v_rows.rearrange("(c p) n -> p c n", p=P)).then_inc(s_kv_in[1], 16)
            wait_ge(sp, s_table, TABLE)
            for e in range(EXPERTS):
                pad = sp.value_load(tab_pad[0:1, e:e + 1], min_val=0, max_val=SPARE - TILE)
                sp.dma_start(rows(slots_x, pad, TILE), zeros[:, :, :]).then_inc(s_pad, 16)
            sp.dma_start(rows(slots_x, SPARE, TILE), zeros[:, :, :]).then_inc(s_pad, 16)
            wait_ge(sp, s_w_out[0], 8 * SHARED)
            wait_ge(sp, s_w_out[1], 8 * SHARED)
            wait_ge(sp, s_bt_out, 16)

            def load_fc(j, par, first=False):
                if not first:
                    wait_ge(sp, s_mm1, BANKS * (SHARED + j - 1))
                e = sp.value_load(tab_e[0:1, ds(j, 1)], min_val=0, max_val=EXPERTS - 1)
                sp.dma_start(w_fc[par][:, :], wpack[ds(e * P, P), 0:4096]).then_inc(s_wfc_in[par], 16)
                if not first:
                    wait_ge(sp, s_gelu, BANKS * (SHARED + j - 1))
                sp.dma_start(b_fc[par][:, :], bfct_d[:, ds(e * HC, HC)]).then_inc(s_bfc_in[par], 16)

            def load_pj(j, par, first=False):
                if not first:
                    wait_ge(sp, s_mm2, 2 * (SHARED + j - 1))
                e = sp.value_load(tab_e[0:1, ds(j, 1)], min_val=0, max_val=EXPERTS - 1)
                sp.dma_start(w_pj[par][:, :], wpack[ds(e * P, P), 4096:8192]).then_inc(s_wpj_in[par], 16)
                if not first:
                    wait_ge(sp, s_ev, 2 * (SHARED + j - 1))
                sp.dma_start(b_pj[par][:, :], bproj[ds(e, 1), :].rearrange("e n -> (e n)").partition_broadcast(P)
                             ).then_inc(s_bpjx_in[par], 16)

            def load_slots(j, par):
                wait_ge(sp, s_tr, SHARED + j - 1)
                r = sp.value_load(tab_x[0:1, ds(j, 1)], min_val=0, max_val=SPARE)
                sp.dma_start(x_split[par][:, :, :], rows(slots_x, r, TILE)).then_inc(s_xs_in[par], 16)

            def store_slots(j, par):
                wait_ge(sp, s_ev, 2 * (SHARED + j) + 2)
                sp.dma_start(rows(slots_y, j * TILE, TILE), y_sb[par][:, :, :]).then_inc(s_y_out[par], 16)

            load_fc(0, 0, first=True)
            load_fc(1, 1, first=True)
            load_pj(0, 0, first=True)
            wait_ge(sp, s_scat[0], 32 * SHARED)
            wait_ge(sp, s_scat[1], 32 * SHARED)
            wait_ge(sp, s_pad, 16 * (EXPERTS + 1))
            load_slots(0, 0)
            load_slots(1, 1)
            store_shared(SHARED - 2, 0)
            store_shared(SHARED - 1, 1)

            load_fc(2, 0)
            load_slots(3, 1)
            load_slots(2, 0)
            load_pj(1, 1, first=True)

            def body2(j, par, tail=0):
                if tail < 2:
                    load_fc(j + 1, 1 - par)
                if tail < 1:
                    load_slots(j + 2, par)
                load_pj(j, par)
                store_slots(j - 2, par)

            body2(2, 0, tail=1)
            load_slots(4, 0)
            with pairs(sp, 3, ROUTED - 4) as j:
                body2(j, 1)
                body2(j + 1, 0)
            body2(ROUTED - 4, 1)
            body2(ROUTED - 3, 0)
            body2(ROUTED - 2, 1, tail=1)
            body2(ROUTED - 1, 0, tail=2)
            store_slots(ROUTED - 2, 1)
            store_slots(ROUTED - 1, 0)

            def load_q(m, par, first=False):
                if not first:
                    wait_ge(sp, s_qk, 2 * m - 2)
                sp.dma_start(q_t[par][:, :, :].rearrange("p c n -> p (c n)"), xt_d[ds(m * P, P), :]
                             ).then_inc(s_q_in[par], 16)

            def load_scale(b, par, first=False):
                if not first:
                    wait_ge(sp, s_mul, 4 * (b - 1))
                src = key_scale[ds(b * 2, 2), :].rearrange("r n -> (r n)")
                sp.dma_start(scale_b[par][:, :], src.partition_broadcast(P)).then_inc(s_sc_in[par], 16)

            def load_base(u, par, first=False):
                if not first:
                    wait_ge(sp, s_base, u - 1)
                sp.dma_start(base_y[par][:, :], shared_y[ds(u * P, P), :]).then_inc(s_by_in[par], 16)
                if not first:
                    wait_ge(sp, s_fin, FIN * (u - 1))
                sp.dma_start(base_x[par][:, :], x_rows[ds(u * P, P), :]).then_inc(s_bx_in[par], 16)

            def store_out(u, par):
                wait_ge(sp, s_fin, FIN * (u + 1))
                sp.dma_start(out_rows[ds(u * P, P), :], o_sb[par][:, :]).then_inc(s_out[par], 16)

            for par in range(2):
                wait_ge(sp, s_xt_out[par], 8 * SHARED)
                wait_ge(sp, s_row_out[par], 8 * SHARED)
                wait_ge(sp, s_y_out[par], 8 * SHARED)
            load_q(0, 0, first=True)
            load_scale(0, 0, first=True)
            load_base(0, 0, first=True)
            load_base(1, 1, first=True)
            load_q(1, 1, first=True)
            load_scale(1, 1, first=True)

            def body3(u0, first=False, last=False):
                for s in range(8):
                    u = u0 + s
                    if s % 2 == 1 and not (last and s > 3):
                        m = u0 // 2 if isinstance(u0, int) else None
                        pair = (m if m is not None else half(u0)) + s // 2 + 2
                        load_q(pair, (s // 2) % 2)
                    if s == 4 and not last:
                        load_scale(quarter(u0) + 2, 0)
                    if not (first and s == 0):
                        store_out(u - 1, (s + 1) % 2)
                    if not (first and s == 0) and not (last and s == 7):
                        load_base(u + 1, (s + 1) % 2)
                    if s == 0 and not first:
                        load_scale(quarter(u0) + 1, 1)

            def half(u0):
                return u0 // 2 if isinstance(u0, int) else g8 * 4

            def quarter(u0):
                return u0 // 4 if isinstance(u0, int) else g8 * 2

            body3(0, first=True)
            with sp.Fori(1, QT // 8 - 1) as g:
                g8 = sp.snap(g)
                body3(g8 * 8)
            body3(QT - 8, last=True)
            store_out(QT - 1, 1)
            wait_ge(sp, s_out[0], 8 * QT)
            wait_ge(sp, s_out[1], 8 * QT)

        @block.gpsimd
        def _(pool):
            g = nc.gpsimd
            g.memset(ident_h[:, :], 0.0).then_inc(s_iota, 1)
            g.memset(ident_f[:, :], 0.0).then_inc(s_iota, 1)
            g.memset(before[:, :], 1.0).then_inc(s_iota, 1)
            wait_ge(pool, s_iota, 3)
            for t in (ident_h, ident_f):
                g.affine_select(out=t[:, :], in_=t[:, :], compare_op=ALU.not_equal, fill=1.0, base=0,
                                pattern=[[-1, P]], channel_multiplier=1).then_inc(s_const, 1)
            g.affine_select(out=before[:, :], in_=before[:, :], compare_op=ALU.is_gt, fill=0.0, base=0,
                            pattern=[[1, P]], channel_multiplier=-1).then_inc(s_const, 1)
            g.memset(ones_h[:, :], 1.0).then_inc(s_const, 1)
            g.iota(iota_e[:, :], pattern=[[1, EXPERTS]], base=0, channel_multiplier=0,
                   allow_small_or_imprecise_dtypes=True).then_inc(s_const, 1)
            g.iota(region[:, :], pattern=[[CAP, EXPERTS]], base=0, channel_multiplier=0,
                   allow_small_or_imprecise_dtypes=True).then_inc(s_const, 1)
            g.iota(step_no[:, :], pattern=[[1, ROUTED]], base=0, channel_multiplier=0,
                   allow_small_or_imprecise_dtypes=True).then_inc(s_const, 1)
            g.memset(neg_half[:, :], -0.5).then_inc(s_const, 1)
            g.memset(zeros[:, :, :], 0.0).then_inc(s_const, 1)
            g.memset(one_row[:, :], 1.0).then_inc(s_const, 1)
            wait_ge(pool, s_const, CONSTS)

            def inv_std(i, par):
                wait_ge(pool, s_lna, (i + 1) * LNA)
                g.tensor_tensor(rstd[par][:, :], var_eps[par][:, :], neg_half[:, :], ALU.pow).then_inc(s_rstd, 1)

            def scale_w(n, par, dma):
                wait_ge(pool, s_w_in[par], dma)
                g.tensor_scalar(w_stage[par][:, :], w_stage[par][:, :], WS, None, ALU.mult).then_inc(s_wsc, 1)

            def split_w_lo(n, dst):
                wait_ge(pool, s_whi, n + 1)
                g.tensor_tensor(dst[:, 2048:4096], w_stage_of(n), dst[:, 0:2048], ALU.subtract).then_inc(s_wlo, 1)

            par_of = [0]

            def w_stage_of(n):
                return w_stage[par_of[0]][:, :]

            def prep(n, par, dst):
                par_of[0] = par
                scale_w(n, par, nth(n, par))
                split_w_lo(n, dst)

            def scatter(i, par):
                wait_ge(pool, s_rb, i * RB + 4)
                for a in range(SUB):
                    for kk in range(TOP):
                        c = a * TOP + kk
                        g.indirect_dma_start(slots_x, bass.IndirectOffsetOnAxis(ap=pos_i[par][:, c:c + 1], axis=0),
                                             x_split[par][:, a, :], None).then_inc(s_scat[par], 16)

            inv_std(0, 0)
            prep(0, 0, w_shared[0])
            prep(1, 1, w_shared[1])
            inv_std(1, 1)

            def body1(i, par, last=False):
                if not last:
                    inv_std(i + 1, 1 - par)
                prep(i + 2, par, w_split[par])
                scatter(i, par)

            prep(2, 0, w_split[0])
            scatter(0, 0)
            with pairs(pool, 1, SHARED - 1) as i:
                body1(i, 1)
                body1(i + 1, 0)
            body1(SHARED - 1, 1, last=True)

            def gather(u, par, first=False):
                if not first:
                    wait_ge(pool, s_fin, FIN * (u - 1))
                g.tensor_copy(pos_u[par][:, :], y_row_all[:, ds(u * TOP, TOP)]).then_inc(s_meta, 1)
                g.tensor_copy(gate_u[par][:, :], gates[:, ds(u, 1), :].rearrange("p o k -> p (o k)")).then_inc(s_meta, 1)
                wait_ge(pool, s_meta, 2 * u + 1)
                for kk in range(TOP):
                    g.indirect_dma_start(y_rows[par][:, kk, :], None, slots_y,
                                         bass.IndirectOffsetOnAxis(ap=pos_u[par][:, kk:kk + 1], axis=0)
                                         ).then_inc(s_gat[par], 16)

            def add_base(u, par):
                wait_ge(pool, s_by_in[par], nth(u, par))
                wait_ge(pool, s_bx_in[par], nth(u, par))
                g.tensor_tensor(base_x[par][:, :], base_x[par][:, :], base_y[par][:, :], ALU.add).then_inc(s_base, 1)

            wait_ge(pool, s_gate, 3)
            wait_ge(pool, s_y_rows, Y_ROWS)
            for par in range(2):
                wait_ge(pool, s_y_out[par], 16 * ((SHARED + ROUTED + 1 - par) // 2))
            gather(0, 0, first=True)
            add_base(0, 0)
            gather(1, 1, first=True)
            add_base(1, 1)
            with pairs(pool, 2, QT) as u:
                gather(u, 0)
                add_base(u, 0)
                gather(u + 1, 1)
                add_base(u + 1, 1)

        @block.scalar
        def _(act):
            def split_w_hi(n, par, dst, stored):
                act.wait_ge(s_wsc, n + 1)
                if stored is not None:
                    act.wait_ge(s_w_out[par], stored)
                nc.scalar.copy(dst[:, 0:2048], w_stage[par][:, :]).then_inc(s_whi, 1)

            def gelu(t, par, bias, first=False):
                for b in range(BANKS):
                    act.wait_ge(s_mm1, BANKS * t + b + 1)
                    if not first:
                        act.wait_ge(s_hlo, BANKS * (t - 1) + b + 1)
                    for half in range(2):
                        hc = 2 * b + half
                        ins = nc.scalar.activation(h32[:, hc, :], ps_h[:, hc * TILE:(hc + 1) * TILE],
                                                   ACT.Gelu_apprx_tanh, bias=bias[:, hc:hc + 1], scale=1.0 / WS)
                    ins.then_inc(s_gelu, 1)
                    if b == 0 and not (isinstance(t, int) and t < 2):
                        act.wait_ge(s_mm2, 2 * (t - 1))
                    act.wait_ge(s_gelu, BANKS * t + b + 1)
                    nc.scalar.copy(h_split[par][:, 0, 2 * b:2 * b + 2, :], h32[:, 2 * b:2 * b + 2, :]).then_inc(s_hhi, 1)

            b_s = b_t[:, EXPERTS * HC:EXPERTS * HC + HC]
            split_w_hi(0, 0, w_shared[0], None)
            split_w_hi(1, 1, w_shared[1], None)
            act.wait_ge(s_bt, 1)
            gelu(0, 0, b_s, first=True)
            split_w_hi(2, 0, w_split[0], None)
            gelu(1, 1, b_s)
            split_w_hi(3, 1, w_split[1], None)
            with pairs(act, 2, SHARED) as i:
                gelu(i, 0, b_s)
                split_w_hi(i + 2, 0, w_split[0], i * 8)
                gelu(i + 1, 1, b_s)
                split_w_hi(i + 3, 1, w_split[1], i * 8)
            act.wait_ge(s_kv_in[0], 16)
            act.wait_ge(s_w_out[0], 8 * SHARED)
            ksp = w_split[0][:, :].rearrange("p (c n) -> p c n", c=KC)
            nc.scalar.copy(ksp[:, :, 0:D], w_stage[0][:, :].rearrange("p (c n) -> p c n", c=KC)).then_inc(s_kv_hi, 1)
            act.wait_ge(s_kv_in[1], 16)
            nc.scalar.copy(v_split[:, 0, :, :], w_stage[1][:, :].rearrange("p (c n) -> p c n", c=KC)).then_inc(s_kv_hi, 1)

            def step2(j, par):
                act.wait_ge(s_bfc_in[par], nth(j, par))
                gelu(SHARED + j, par, b_fc[par])

            step2(0, 0)
            with pairs(act, 1, ROUTED) as j:
                step2(j, 1)
                step2(j + 1, 0)

            nc.scalar.activation(gap_exp[:, :], gap_all[:, :], ACT.Exp, scale=1.0 / WS).then_inc(s_gexp, 1)

            def exp(u, par):
                act.wait_ge(s_nm, u + 1)
                nc.scalar.activation(prob[par][:, :], prob[par][:, :], ACT.Exp, bias=neg_max[par][:, 0:1],
                                     accum_out=row_sum[par][:, 0:1]).then_inc(s_exp, 1)

            def p_hi(u, par, first=False):
                for kk in range(2):
                    act.wait_ge(s_pt, 2 * u + kk + 1)
                    if kk == 0 and not first:
                        act.wait_ge(s_pv, u - 1)
                    nc.scalar.copy(p_t[par][:, 0, 4 * kk:4 * kk + 4, :],
                                   ps_t[:, kk * 512:(kk + 1) * 512].rearrange("p (c n) -> p c n", n=P)).then_inc(s_phi, 1)

            exp(0, 0)
            p_hi(0, 0, first=True)
            exp(1, 1)
            p_hi(1, 1, first=True)
            exp(2, 0)
            with pairs(act, 2, QT - 2) as u:
                p_hi(u, 0)
                exp(u + 1, 1)
                p_hi(u + 1, 1)
                exp(u + 2, 0)
            p_hi(QT - 2, 0)
            exp(QT - 1, 1)
            p_hi(QT - 1, 1)

        @block.vector
        def _(dve):
            ve = nc.vector

            def ln_stats(i, par):
                dve.wait_ge(s_x_in[par], nth(i, par))
                link = chain(dve, s_lna, i * LNA)
                for a in range(SUB):
                    link(ve.bn_stats(stats[:, a, :], x_in[par][:, a, :]), wait=a == SUB - 1)
                for a in range(SUB):
                    link(ve.bn_aggr(mean_var[par][:, a, :], stats[:, a, :]), wait=a == SUB - 1)
                link(ve.tensor_scalar(var_eps[par][:, :], mean_var[par][:, :, 1], EPS, None, ALU.add))

            def ln_apply(i, par, first=False):
                dve.wait_ge(s_rstd, i + 1)
                if not first:
                    dve.wait_ge(s_row_out[par], (i - par) * 8)
                    dve.wait_ge(s_scat[par], (i - par) * 32)
                    dve.wait_ge(s_tr, i - 1)
                link = chain(dve, s_lnb, i * LNB)
                for a in range(SUB):
                    link(ve.tensor_scalar(xn[par][:, a, :], x_in[par][:, a, :], mean_var[par][:, a, 0:1],
                                          rstd[par][:, a:a + 1], ALU.subtract, ALU.mult), wait=a == SUB - 1)
                link(ve.tensor_copy(x_split[par][:, :, 0:D], xn[par][:, :, :]), wait=True)
                link(ve.tensor_tensor(x_split[par][:, :, D:ROW], xn[par][:, :, :], x_split[par][:, :, 0:D], ALU.subtract))

            def copy_xt(t, par, stored=None):
                dve.wait_ge(s_tr, t + 1)
                if not (isinstance(t, int) and t < 2):
                    dve.wait_ge(s_mm1, BANKS * (t - 1))
                if stored is not None:
                    dve.wait_ge(s_xt_out[par], stored)
                ve.tensor_copy(x_t[par][:, :, :], tr16[:, :].rearrange("p (c n) -> p c n", n=TILE)).then_inc(s_xt, 1)

            def route_a(i, par):
                dve.wait_ge(s_logit, i + 1)
                link = chain(dve, s_ra, i * RA)
                link(ve.tensor_reduce(logits[:, :, :], lg_ps.rearrange("p (a h e) -> p a e h", a=SUB, h=2), AX, ALU.add), wait=True)
                for a in range(SUB):
                    link(ve.max(top_v[:, a, :], logits[:, a, :]), wait=a == SUB - 1)
                for a in range(SUB):
                    link(ve.max_index(top_i[:, a, :], top_v[:, a, :], logits[:, a, :]), wait=a == SUB - 1)
                link(ve.tensor_copy(top_f[:, :, :], top_i[:, :, 0:TOP]), wait=True)
                link(ve.tensor_copy(exp_all[:, ds(i * SUB * TOP, SUB * TOP)], top_f[:, :, :].rearrange("p a k -> p (a k)")))
                link(ve.tensor_tensor(gap_all[:, ds(i * SUB, SUB)], top_v[:, :, 1], top_v[:, :, 0], ALU.subtract))
                link(ve.tensor_tensor(chosen[:, :, :, :].rearrange("p a k e -> p (a k) e"),
                                      top_f[:, :, :].rearrange("p a k -> p (a k)").unsqueeze(2).to_broadcast([P, SUB * TOP, EXPERTS]),
                                      iota_e[:, :].unsqueeze(1).to_broadcast([P, SUB * TOP, EXPERTS]), ALU.is_equal), wait=True)
                link(ve.tensor_tensor(mask[par][:, :, :], chosen[:, :, 0, :], chosen[:, :, 1, :], ALU.add))

            def route_b(i, par):
                dve.wait_ge(s_rank, i + 1)
                if not (isinstance(i, int) and i < 2):
                    dve.wait_ge(s_scat[par], (i - par) * 32)
                link = chain(dve, s_rb, i * RB)
                link(ve.tensor_tensor(slot_of[:, :, :], rk_ps.rearrange("p (a e) -> p a e", a=SUB),
                                      region[:, :].unsqueeze(1).to_broadcast([P, SUB, EXPERTS]), ALU.add), wait=True)
                link(ve.tensor_tensor(picked[:, :, :, :], chosen[:, :, :, :],
                                      slot_of[:, :, :].unsqueeze(2).to_broadcast([P, SUB, TOP, EXPERTS]), ALU.mult), wait=True)
                link(ve.tensor_reduce(pos_f[:, :], picked[:, :, :, :].rearrange("p a k e -> p (a k) e"), AX, ALU.add), wait=True)
                link(ve.tensor_copy(pos_i[par][:, :], pos_f[:, :]))
                link(ve.tensor_copy(pos_all[:, ds(i * SUB * TOP, SUB * TOP)], pos_f[:, :]))
                for a in range(SUB):
                    link(ve.tensor_tensor(mask_sum[:, :], mask_sum[:, :], mask[par][:, a, :], ALU.add), wait=a == 0)

            def split_h(t, par, banks):
                for b in banks:
                    dve.wait_ge(s_hhi, BANKS * t + b + 1)
                    ve.tensor_tensor(h_split[par][:, 1, 2 * b:2 * b + 2, :], h32[:, 2 * b:2 * b + 2, :],
                                     h_split[par][:, 0, 2 * b:2 * b + 2, :], ALU.subtract).then_inc(s_hlo, 1)

            def evict(t, par, bias):
                if not (isinstance(t, int) and t < 2):
                    dve.wait_ge(s_y_out[par], (t - par) * 8)
                for a in range(SUB):
                    dve.wait_ge(s_mm2, 2 * t + a + 1)
                    ve.scalar_tensor_tensor(out=y_sb[par][:, a, :], in0=ps_y[a][:, 0:D], scalar=1.0 / WS,
                                            in1=bias[:, :], op0=ALU.mult, op1=ALU.add).then_inc(s_ev, 1)

            dve.wait_ge(s_wr_in, 16)
            link = chain(dve, s_wr, 0)
            link(ve.tensor_scalar(wr32[:, :, :], wr32[:, :, :], WS, None, ALU.mult), wait=True)
            link(ve.tensor_copy(wr_s[:, :, 0:EXPERTS], wr32[:, :, :]), wait=True)
            link(ve.tensor_tensor(wr_s[:, :, EXPERTS:], wr32[:, :, :], wr_s[:, :, 0:EXPERTS], ALU.subtract))
            ve.memset(mask_sum[:, :], 0.0).then_inc(s_msum0, 1)
            dve.wait_ge(s_bt_tr, 1)
            ve.tensor_copy(b_t[:, :], bt_ps).then_inc(s_bt, 1)

            ln_stats(0, 0)
            ln_apply(0, 0, first=True)
            copy_xt(0, 0)
            ln_stats(1, 1)
            dve.wait_ge(s_const, CONSTS)
            dve.wait_ge(s_msum0, 1)
            route_a(0, 0)
            split_h(0, 0, (0, 1))
            ln_apply(1, 1, first=True)
            split_h(0, 0, (2, 3))
            route_b(0, 0)
            copy_xt(1, 1)
            dve.wait_ge(s_bpj_in, 16)

            def body1(i, par):
                ln_stats(i + 1, 1 - par)
                route_a(i, par)
                split_h(i, par, (0, 1))
                ln_apply(i + 1, 1 - par)
                split_h(i, par, (2, 3))
                route_b(i, par)
                copy_xt(i + 1, 1 - par, stored=(i + 1 - (1 - par)) * 8)
                evict(i - 1, 1 - par, b_pj_s)

            with pairs(dve, 1, SHARED - 1) as i:
                body1(i, 1)
                body1(i + 1, 0)
            route_a(SHARED - 1, 1)
            split_h(SHARED - 1, 1, range(BANKS))
            route_b(SHARED - 1, 1)

            dve.wait_ge(s_count, 1)
            link = chain(dve, s_table, 0)
            link(ve.tensor_copy(cnt[:, :], cn_ps), wait=True)
            link(ve.tensor_tensor(tab_pad[:, :], cnt[0:1, :], region[0:1, :], ALU.add))
            link(ve.tensor_scalar(cnt_i[:, :], cnt[:, :], float(TILE - 1), None, ALU.add), wait=True)
            link(ve.tensor_scalar(blk_i[:, :], cnt_i[:, :], BLK_SHIFT, None, ALU.arith_shift_right), wait=True)
            link(ve.tensor_copy(blk[:, :], blk_i[:, :]), wait=True)
            link(ve.tensor_tensor_scan(blk_end[:, :], one_row[:, :], blk[:, :], 0.0, ALU.mult, ALU.add), wait=True)
            each = [1, ROUTED, EXPERTS]
            link(ve.tensor_tensor(past[:, :, :], step_no[:, :].unsqueeze(2).to_broadcast(each),
                                  blk_end[0:1, :].unsqueeze(1).to_broadcast(each), ALU.is_ge), wait=True)
            link(ve.tensor_reduce(step_e[:, :], past[:, :, :], AX, ALU.add))
            link(ve.tensor_tensor(past_blk[:, :, :], past[:, :, :], blk[0:1, :].unsqueeze(1).to_broadcast(each), ALU.mult), wait=True)
            link(ve.tensor_reduce(step_b[:, :], past_blk[:, :, :], AX, ALU.add), wait=True)
            link(ve.tensor_tensor(step_b[:, :], step_no[:, :], step_b[:, :], ALU.subtract), wait=True)
            link(ve.tensor_scalar(step_b[:, :], step_b[:, :], float(TILE), None, ALU.mult), wait=True)
            link(ve.scalar_tensor_tensor(out=step_r[:, :], in0=step_e[:, :], scalar=float(CAP), in1=step_b[:, :],
                                         op0=ALU.mult, op1=ALU.add), wait=True)
            link(ve.tensor_scalar(step_r[:, :], step_r[:, :], float(SPARE), None, ALU.min), wait=True)
            link(ve.tensor_copy(tab_x[:, :], step_r[:, :]))
            link(ve.tensor_scalar(step_e[:, :], step_e[:, :], float(EXPERTS - 1), None, ALU.min), wait=True)
            link(ve.tensor_copy(tab_e[:, :], step_e[:, :]), wait=True)

            evict(SHARED - 2, 0, b_pj_s)
            evict(SHARED - 1, 1, b_pj_s)
            link = chain(dve, s_y_rows, 0)
            link(ve.tensor_tensor(shift_e[:, :], blk_end[:, :], blk[:, :], ALU.subtract), wait=True)
            link(ve.scalar_tensor_tensor(out=shift_e[:, :], in0=shift_e[:, :], scalar=float(TILE), in1=region[:, :],
                                         op0=ALU.mult, op1=ALU.subtract), wait=True)
            every = [P, QT * TOP, EXPERTS]
            link(ve.tensor_tensor(match_e[:, :, :], exp_all[:, :].unsqueeze(2).to_broadcast(every),
                                  iota_e[:, :].unsqueeze(1).to_broadcast(every), ALU.is_equal), wait=True)
            link(ve.tensor_tensor(match_e[:, :, :], match_e[:, :, :], shift_e[:, :].unsqueeze(1).to_broadcast(every),
                                  ALU.mult), wait=True)
            link(ve.tensor_reduce(shift_t[:, :], match_e[:, :, :], AX, ALU.add), wait=True)
            link(ve.tensor_tensor(y_row_all[:, :], pos_all[:, :], shift_t[:, :], ALU.add))
            ksp = w_split[0][:, :].rearrange("p (c n) -> p c n", c=KC)
            dve.wait_ge(s_kv_hi, 1)
            ve.tensor_tensor(ksp[:, :, D:ROW], w_stage[0][:, :].rearrange("p (c n) -> p c n", c=KC),
                             ksp[:, :, 0:D], ALU.subtract).then_inc(s_kv_lo, 1)
            dve.wait_ge(s_kv_hi, 2)
            ve.tensor_tensor(v_split[:, 1, :, :], w_stage[1][:, :].rearrange("p (c n) -> p c n", c=KC),
                             v_split[:, 0, :, :], ALU.subtract).then_inc(s_kv_lo, 1)
            for m in range(KC // 2):
                dve.wait_ge(s_k_tr, m + 1)
                ve.tensor_copy(k_t[:, :, m * TILE:(m + 1) * TILE], tr16[:, :].rearrange("p (c n) -> p c n", n=TILE)
                               ).then_inc(s_k_t, 1)

            copy_xt(SHARED, 0, stored=8 * SHARED)
            split_h(SHARED, 0, range(BANKS))
            copy_xt(SHARED + 1, 1, stored=8 * SHARED)

            def evict2(j, par):
                dve.wait_ge(s_bpjx_in[par], nth(j, par))
                evict(SHARED + j, par, b_pj[par])

            def body2(j, par):
                split_h(SHARED + j, par, range(BANKS))
                copy_xt(SHARED + j + 1, 1 - par)
                evict2(j - 1, 1 - par)

            with pairs(dve, 1, ROUTED - 2) as j:
                body2(j, 1)
                body2(j + 1, 0)
            body2(ROUTED - 2, 1)
            split_h(SHARED + ROUTED - 1, 0, range(BANKS))
            evict2(ROUTED - 2, 1)
            evict2(ROUTED - 1, 0)

            dve.wait_ge(s_gexp, 1)
            link = chain(dve, s_gate, 0)
            link(ve.tensor_scalar(gap_den[:, :], gap_exp[:, :], 1.0, None, ALU.add), wait=True)
            link(ve.reciprocal(gates[:, :, 0], gap_den[:, :]), wait=True)
            link(ve.tensor_tensor(gates[:, :, 1], gap_exp[:, :], gates[:, :, 0], ALU.mult))

            def scale_scores(u, par, bpar, loaded, first=False):
                dve.wait_ge(s_qk, u + 1)
                if loaded is not None:
                    dve.wait_ge(s_sc_in[bpar], loaded)
                if not first:
                    dve.wait_ge(s_pt, 2 * (u - 1))
                dve.nop(nofuse=True)
                ve.tensor_tensor_reduce(out=prob[par][:, :], in0=ps_h[:, par * KEYS:(par + 1) * KEYS], in1=scale_b[bpar][:, :],
                                        scale=1.0, scalar=-3.0e38, op0=ALU.mult, op1=ALU.max,
                                        accum_out=row_max[par][:, 0:1]).then_inc(s_mul, 1)
                dve.wait_ge(s_mul, u + 1)
                ve.tensor_scalar(neg_max[par][:, :], row_max[par][:, :], -1.0, None, ALU.mult).then_inc(s_nm, 1)

            def p_lo(u, par):
                for kk in range(2):
                    dve.wait_ge(s_phi, 2 * u + kk + 1)
                    ve.tensor_tensor(p_t[par][:, 1, 4 * kk:4 * kk + 4, :],
                                     ps_t[:, kk * 512:(kk + 1) * 512].rearrange("p (c n) -> p c n", n=P),
                                     p_t[par][:, 0, 4 * kk:4 * kk + 4, :], ALU.subtract).then_inc(s_plo, 1)

            def finish(u, par, first=False):
                link = chain(dve, s_fin, u * FIN)
                dve.wait_ge(s_exp, u + 1)
                link(ve.reciprocal(inv_sum[par][:, :], row_sum[par][:, :]), wait=True)
                dve.wait_ge(s_pv, u + 1)
                dve.wait_ge(s_base, u + 1)
                if not first:
                    dve.wait_ge(s_out[par], (u - par) * 8)
                link(ve.scalar_tensor_tensor(out=o_sb[par][:, :], in0=ps_y[par][:, 0:D], scalar=inv_sum[par][:, 0:1],
                                             in1=base_x[par][:, :], op0=ALU.mult, op1=ALU.add), wait=True)
                dve.wait_ge(s_meta, 2 * u + 2)
                dve.wait_ge(s_gat[par], nth(u, par, 32))
                for kk in range(TOP):
                    link(ve.scalar_tensor_tensor(out=o_sb[par][:, :], in0=y_rows[par][:, kk, :], scalar=gate_u[par][:, kk:kk + 1],
                                                 in1=o_sb[par][:, :], op0=ALU.mult, op1=ALU.add), wait=kk == 0)

            def body3(u0, g8, first=False, last=False):
                for s in range(8):
                    u, par = u0 + s, s % 2
                    p_lo(u, par)
                    if not (first and s == 0):
                        finish(u - 1, 1 - par, first=first and s < 3)
                    if not (last and s == 7):
                        n = s + 1
                        loaded = None
                        if n % 4 == 0:
                            loaded = (g8 + n // 8) * 16 + 16
                        scale_scores(u + 1, 1 - par, (n // 4) % 2, loaded, first=first and s == 0)

            scale_scores(0, 0, 0, 16, first=True)
            body3(0, 0, first=True)
            with dve.Fori(1, QT // 8 - 1) as g3:
                g = dve.snap(g3)
                body3(g * 8, g)
            body3(QT - 8, QT // 8 - 1, last=True)
            finish(QT - 1, 1)

        @block.tensor
        def _(pe):
            mm = nc.tensor.matmul
            TERMS = ((0, 0), (0, 1), (1, 0))

            def transpose_rows(t, par, src):
                for hl in range(2):
                    for c in range(DC):
                        for a in range(SUB):
                            n = (hl * DC + c) * TILE + a * P
                            o = hl * D + c * P
                            ins = nc.tensor.transpose(tr16[:, n:n + P], src[:, a, o:o + P], ident_h[:, :])
                return ins

            def tr1(i, par):
                pe.wait_ge(s_lnb, (i + 1) * LNB)
                if not (isinstance(i, int) and i == 0):
                    pe.wait_ge(s_xt, i)
                transpose_rows(i, par, x_split[par]).then_inc(s_tr, 1)

            def tr2(j, par):
                pe.wait_ge(s_xs_in[par], nth(j, par))
                pe.wait_ge(s_xt, SHARED + j)
                transpose_rows(j, par, x_split[par]).then_inc(s_tr, 1)

            def router(i, par):
                pe.wait_ge(s_xt, i + 1)
                if not (isinstance(i, int) and i == 0):
                    pe.wait_ge(s_rb, i * RB)
                for a in range(SUB):
                    for n in range(2 * DC):
                        ins = mm(lg_ps[:, a * 16:(a + 1) * 16], x_t[par][:, n, a * P:(a + 1) * P], wr_s[:, n % DC, :],
                                 start=n == 0, stop=n == 2 * DC - 1)
                ins.then_inc(s_logit, 1)

            def rank(i, par):
                pe.wait_ge(s_ra, (i + 1) * RA)
                for a in range(SUB):
                    o = rk_ps[:, a * EXPERTS:(a + 1) * EXPERTS]
                    mm(o, before[:, :], mask[par][:, a, :], start=True, stop=False)
                    if a == 1:
                        mm(o, ones_h[:, :], mask[par][:, 0, :], start=False, stop=False)
                    ins = mm(o, ones_h[:, :], mask_sum[:, :], start=False, stop=True)
                ins.then_inc(s_rank, 1)

            def up(t, par, w):
                pe.wait_ge(s_xt, t + 1)
                wv = w[:, :].rearrange("p (h c n) -> p h c n", h=2, c=DC)
                for b in range(BANKS):
                    if not (isinstance(t, int) and t == 0):
                        pe.wait_ge(s_gelu, BANKS * (t - 1) + b + 1)
                    for hc in (2 * b, 2 * b + 1):
                        n = 0
                        for wl, xl in TERMS:
                            for c in range(DC):
                                ins = mm(ps_h[:, hc * TILE:(hc + 1) * TILE], wv[:, wl, c, hc * P:(hc + 1) * P],
                                         x_t[par][:, xl * DC + c, :], start=n == 0, stop=n == 3 * DC - 1)
                                n += 1
                    ins.then_inc(s_mm1, 1)

            def down(t, par, w):
                pe.wait_ge(s_hlo, BANKS * (t + 1))
                wv = w[:, :].rearrange("p (h c n) -> p h c n", h=2, c=HC)
                for a in range(SUB):
                    if not (isinstance(t, int) and t == 0):
                        pe.wait_ge(s_ev, 2 * (t - 1) + a + 1)
                    n = 0
                    for wl, xl in TERMS:
                        for c in range(HC):
                            ins = mm(ps_y[a][:, 0:D], h_split[par][:, xl, c, a * P:(a + 1) * P], wv[:, wl, c, :],
                                     start=n == 0, stop=n == 3 * HC - 1)
                            n += 1
                    ins.then_inc(s_mm2, 1)

            pe.wait_ge(s_const, CONSTS)
            pe.wait_ge(s_bias_in, 32)
            nb = EXPERTS * HC + HC
            nc.tensor.transpose(bt_ps, b_rows[:, :], ident_f[0:nb, 0:nb]).then_inc(s_bt_tr, 1)
            tr1(0, 0)
            pe.wait_ge(s_wr, 3)
            pe.wait_ge(s_bt, 1)
            router(0, 0)
            pe.wait_ge(s_wlo, 1)
            up(0, 0, w_shared[0])
            rank(0, 0)
            tr1(1, 1)
            router(1, 1)
            pe.wait_ge(s_wlo, 2)

            def body1(i, par):
                up(i, par, w_shared[0])
                rank(i, par)
                tr1(i + 1, 1 - par)
                down(i - 1, 1 - par, w_shared[1])
                router(i + 1, 1 - par)

            body1(1, 1)
            body1(2, 0)
            with pairs(pe, 3, SHARED - 1) as i:
                body1(i, 1)
                body1(i + 1, 0)
            up(SHARED - 1, 1, w_shared[0])
            rank(SHARED - 1, 1)
            pe.wait_ge(s_rb, SHARED * RB)
            mm(cn_ps, ones_h[:, :], mask_sum[:, :], start=True, stop=True).then_inc(s_count, 1)
            down(SHARED - 2, 0, w_shared[1])
            down(SHARED - 1, 1, w_shared[1])
            ksp = w_split[0][:, :].rearrange("p (c n) -> p c n", c=KC)
            pe.wait_ge(s_kv_lo, 1)
            for m in range(KC // 2):
                if m:
                    pe.wait_ge(s_k_t, m)
                transpose_rows(m, 0, ksp[:, 2 * m:2 * m + 2, :]).then_inc(s_k_tr, 1)
            pe.wait_ge(s_k_t, KC // 2)

            def up2(j, par):
                pe.wait_ge(s_wfc_in[par], nth(j, par))
                up(SHARED + j, par, w_fc[par])

            def down2(j, par):
                pe.wait_ge(s_wpj_in[par], nth(j, par))
                down(SHARED + j, par, w_pj[par])

            def body2(j, par):
                up2(j, par)
                tr2(j + 1, 1 - par)
                down2(j - 1, 1 - par)

            tr2(0, 0)
            up2(0, 0)
            tr2(1, 1)
            with pairs(pe, 1, ROUTED - 2) as j:
                body2(j, 1)
                body2(j + 1, 0)
            body2(ROUTED - 2, 1)
            up2(ROUTED - 1, 0)
            down2(ROUTED - 2, 1)
            down2(ROUTED - 1, 0)

            def scores(u, par, mpar, loaded, first=False):
                if loaded is not None:
                    pe.wait_ge(s_q_in[mpar], loaded)
                if not first:
                    pe.wait_ge(s_mul, u - 1)
                for half in range(2):
                    n = 0
                    for kl, ql in TERMS:
                        for c in range(DC):
                            lo = par * KEYS + half * 512
                            ins = mm(ps_h[:, lo:lo + 512], q_t[mpar][:, ql * DC + c, par * P:(par + 1) * P],
                                     k_t[:, kl * DC + c, half * 512:(half + 1) * 512], start=n == 0, stop=n == 3 * DC - 1)
                            n += 1
                ins.then_inc(s_qk, 1)

            def transpose_probs(u, par, first=False):
                pe.wait_ge(s_exp, u + 1)
                for kk in range(2):
                    if not first:
                        pe.wait_ge(s_plo, 2 * (u - 1) + kk + 1)
                    for c in range(4 * kk, 4 * kk + 4):
                        ins = nc.tensor.transpose(ps_t[:, c * P:(c + 1) * P], prob[par][:, c * P:(c + 1) * P], ident_f[:, :])
                    ins.then_inc(s_pt, 1)

            def values(u, par, first=False):
                pe.wait_ge(s_plo, 2 * (u + 1))
                if not first:
                    pe.wait_ge(s_fin, FIN * (u - 2) + 2)
                n = 0
                for vl, pl in TERMS:
                    for c in range(KC):
                        ins = mm(ps_y[par][:, 0:D], p_t[par][:, pl, c, :], v_split[:, vl, c, :],
                                 start=n == 0, stop=n == 3 * KC - 1)
                        n += 1
                ins.then_inc(s_pv, 1)

            def body3(u0, g8, first=False, last=False):
                for s in range(8):
                    u, par = u0 + s, s % 2
                    transpose_probs(u, par, first=first and s == 0)
                    if not (last and s == 7):
                        n = s + 1
                        loaded = None
                        if n % 2 == 0:
                            loaded = g8 * 32 + (n // 4) * 16 + 16
                        scores(u + 1, 1 - par, (n // 2) % 2, loaded, first=first and s == 0)
                    values(u, par, first=first and s < 2)

            pe.wait_ge(s_kv_lo, 2)
            pe.wait_ge(s_ev, 2 * (SHARED + ROUTED))
            scores(0, 0, 0, 16, first=True)
            body3(0, 0, first=True)
            with pe.Fori(1, QT // 8 - 1) as g3:
                g = pe.snap(g3)
                body3(g * 8, g)
            body3(QT - 8, QT // 8 - 1, last=True)


_INS = ["L0_attn_q", "L0_attn_k", "L0_attn_v", "L0_ffn_Wfc_s", "L0_ffn_bfc_s", "L0_ffn_Wproj_s", "L0_ffn_bproj_s",
        "L0_ffn_Wr", "L0_ffn_Wfc", "L0_ffn_bfc", "L0_ffn_Wproj", "L0_ffn_bproj"]
_OUTS = [((8, 512, 256), "float32")]


def kernel(**inputs):
    import numpy as _np
    import concourse.bacc as _bacc
    from concourse import mybir as _mybir
    from concourse.bass_utils import run_bass_kernel_spmd as _run

    nc = _bacc.Bacc("TRN2", target_bir_lowering=False, num_devices=1)
    arrays, args = {}, []
    for name in _INS:
        a = _np.ascontiguousarray(inputs[name])
        arrays[f"in_{name}_dram"] = a
        args.append(nc.dram_tensor(f"in_{name}_dram", a.shape, _mybir.dt.from_np(a.dtype), kind="ExternalInput").ap())
    for n, (shape, dtype) in enumerate(_OUTS):
        dt = _mybir.dt.from_np(_np.dtype(dtype))
        args.append(nc.dram_tensor(f"out_{n}_dram", shape, dt, kind="ExternalOutput").ap())
    moe_attention_block(nc, *args)
    r = _run(nc, [arrays], core_ids=[0])
    return r.results[0]["out_0_dram"]
```

```python
from contextlib import ExitStack, contextmanager

import concourse.bass as bass
from concourse import mybir

TOKENS, D = 4096, 256
BATCH, QLEN, KEYS = 8, 512, 1024
HID, EXPERTS, TOP = 1024, 8, 2
P = 128
TILE = 256
SUB = TILE // P
DC = D // P
HC = HID // P
BANKS = 4
SHARED = TOKENS // TILE
BLK_SHIFT = 8
ROUTED = (TOKENS * TOP + EXPERTS * (TILE - 1)) // TILE
CAP = TOKENS + TILE
SPARE = EXPERTS * CAP
QT = TOKENS // P
KC = KEYS // P
KH = KC // 2
WS = 256.0
EPS = 1e-5
ROW = 2 * D


def moe_attention_block(nc, q, k, v, wfc_s, bfc_s, wproj_s, bproj_s, wr, wfc, bfc, wproj, bproj, out):
    f32, f16 = mybir.dt.float32, mybir.dt.float16
    i32, u32 = mybir.dt.int32, mybir.dt.uint32
    ALU = mybir.AluOpType
    ACT = mybir.ActivationFunctionType
    AX = mybir.AxisListType.X
    ds = bass.ds

    x_rows = q.rearrange("b s d -> (b s) d")
    out_rows = out.rearrange("b s d -> (b s) d")
    k_rows = k.rearrange("b s d -> (b s) d")
    v_rows = v.rearrange("b s d -> (b s) d")
    wfc_rows = wfc.rearrange("e c n -> (e c) n")
    wproj_rows = wproj.rearrange("e h n -> (e h) n")
    bfc_rows = bfc.rearrange("e (h p) -> (e h) p", p=P)
    bfc_s_rows = bfc_s.rearrange("(h p) -> h p", p=P)

    def dram(name, shape, dt):
        return nc.dram_tensor(name, shape, dt, kind="Internal").ap()

    slots_x = dram("slots_x", (SPARE + TILE, ROW), f16)
    slots_y = dram("slots_y", (ROUTED * TILE, D), f32)
    shared_y = dram("shared_y", (TOKENS, D), f32)
    xt_d = dram("xt_d", (SHARED * P, 2 * DC * TILE), f16)
    key_scale = dram("key_scale", (SHARED, SUB * D), f32)
    wpack = dram("wpack", (EXPERTS * P, 4 * 2048), f16)
    bfct_d = dram("bfct_d", (P, EXPERTS * HC), f32)

    ctx = ExitStack()
    with ctx:
        def sb(name, shape, dt):
            return ctx.enter_context(nc.sbuf_tensor(name, shape, dt))

        def sem(name):
            return ctx.enter_context(nc.semaphore(name))

        def sem2(name):
            return [sem(name + "_even"), sem(name + "_odd")]

        def sb2(name, shape, dt):
            return [sb(name + str(n), shape, dt) for n in range(2)]

        ident_h = sb("ident_h", [P, P], f16)
        ident_f = sb("ident_f", [P, P], f32)
        before = sb("before", [P, P], f16)
        ones_h = sb("ones_h", [P, P], f16)
        iota_e = sb("iota_e", [P, EXPERTS], f32)
        region = sb("region", [P, EXPERTS], f32)
        step_no = sb("step_no", [1, ROUTED], f32)
        neg_half = sb("neg_half", [P, SUB], f32)
        zeros = sb("zeros", [P, SUB, ROW], f16)
        one_row = sb("one_row", [P, EXPERTS], f32)
        x_in = sb2("x_in", [P, SUB, D], f32)
        stats = sb("stats", [P, SUB, 6], f32)
        mean_var = sb2("mean_var", [P, SUB, 2], f32)
        var_eps = sb2("var_eps", [P, SUB], f32)
        rstd = sb2("rstd", [P, SUB], f32)
        xn = sb2("xn", [P, SUB, D], f32)
        x_split = sb2("x_split", [P, SUB, ROW], f16)
        x_t = sb2("x_t", [P, 2 * DC, TILE], f16)
        wr32 = sb("wr32", [P, DC, EXPERTS], f32)
        wr_s = sb("wr_s", [P, DC, 2 * EXPERTS], f16)
        logits = sb("logits", [P, SUB, EXPERTS], f32)
        top_v = sb("top_v", [P, SUB, 8], f32)
        top_i = sb("top_i", [P, SUB, 8], u32)
        top_f = sb("top_f", [P, SUB, TOP], f32)
        chosen = sb("chosen", [P, SUB, TOP, EXPERTS], f32)
        mask = sb2("mask", [P, SUB, EXPERTS], f16)
        mask_sum = sb("mask_sum", [P, EXPERTS], f16)
        slot_of = sb("slot_of", [P, SUB, EXPERTS], f32)
        picked = sb("picked", [P, SUB, TOP, EXPERTS], f32)
        pos_f = sb("pos_f", [P, SUB * TOP], f32)
        pos_i = sb2("pos_i", [P, SUB * TOP], i32)
        pos_all = sb("pos_all", [P, QT * TOP], f32)
        exp_all = sb("exp_all", [P, QT * TOP], f32)
        match_e = sb("match_e", [P, QT * TOP, EXPERTS], f32)
        shift_e = sb("shift_e", [P, EXPERTS], f32)
        shift_t = sb("shift_t", [P, QT * TOP], f32)
        y_row_all = sb("y_row_all", [P, QT * TOP], i32)
        gap_all = sb("gap_all", [P, QT], f32)
        w_stage = sb2("w_stage", [P, 2048], f32)
        w_split = sb2("w_split", [P, 4096], f16)
        w_shared = sb2("w_shared", [P, 4096], f16)
        w_fc = sb2("w_fc", [P, 4096], f16)
        w_pj = sb2("w_pj", [P, 4096], f16)
        b_rows = sb("b_rows", [EXPERTS * HC + HC, P], f32)
        b_t = sb("b_t", [P, EXPERTS * HC + HC], f32)
        b_fc = sb2("b_fc", [P, HC], f32)
        b_pj = sb2("b_pj", [P, D], f32)
        b_pj_s = sb("b_pj_s", [P, D], f32)
        h32 = sb("h32", [P, HC, TILE], f32)
        h_split = sb2("h_split", [P, 2, HC, TILE], f16)
        y_sb = sb2("y_sb", [P, SUB, D], f32)
        cnt = sb("cnt", [P, EXPERTS], f32)
        cnt_i = sb("cnt_i", [P, EXPERTS], i32)
        blk_i = sb("blk_i", [P, EXPERTS], i32)
        blk = sb("blk", [P, EXPERTS], f32)
        blk_end = sb("blk_end", [P, EXPERTS], f32)
        past = sb("past", [1, ROUTED, EXPERTS], f32)
        past_blk = sb("past_blk", [1, ROUTED, EXPERTS], f32)
        step_e = sb("step_e", [1, ROUTED], f32)
        step_b = sb("step_b", [1, ROUTED], f32)
        step_r = sb("step_r", [1, ROUTED], f32)
        tab_e = sb("tab_e", [1, ROUTED], i32)
        tab_x = sb("tab_x", [1, ROUTED], i32)
        tab_pad = sb("tab_pad", [1, EXPERTS], i32)
        k_t = sb("k_t", [P, 2 * DC, KEYS], f16)
        v_split = sb("v_split", [P, 2, KC, D], f16)
        q_t = sb2("q_t", [P, 2 * DC, TILE], f16)
        scale_b = sb2("scale_b", [P, KEYS], f32)
        prob = sb2("prob", [P, KEYS], f32)
        row_max = sb2("row_max", [P, 1], f32)
        neg_max = sb2("neg_max", [P, 1], f32)
        row_sum = sb2("row_sum", [P, 1], f32)
        inv_sum = sb2("inv_sum", [P, 1], f32)
        p_t = sb2("p_t", [P, 2, KC, P], f16)
        gap_exp = sb("gap_exp", [P, QT], f32)
        gap_den = sb("gap_den", [P, QT], f32)
        gates = sb("gates", [P, QT, TOP], f32)
        gate_u = sb2("gate_u", [P, TOP], f32)
        pos_u = sb2("pos_u", [P, TOP], i32)
        y_rows = sb2("y_rows", [P, TOP, D], f32)
        base_y = sb2("base_y", [P, D], f32)
        base_x = sb2("base_x", [P, D], f32)
        o_sb = sb2("o_sb", [P, D], f32)

        k_split = [t[:, :, :, :].rearrange("p h c n -> p (h c n)").rearrange("p (c n) -> p c n", c=KH) for t in p_t]

        ps_h = ctx.enter_context(nc.psum_tensor("ps_h", [P, BANKS * 512], f32))
        ps_y = [ctx.enter_context(nc.psum_tensor(f"ps_y{a}", [P, 512], f32)) for a in range(2)]
        ps_t = ctx.enter_context(nc.psum_tensor("ps_t", [P, 1024], f32))
        tr16 = ps_t[:, 0:512].bitcast(f16)
        misc = ps_t[:, 512:1024]
        lg_ps = misc[:, 0:SUB * 2 * EXPERTS]
        rk_ps = misc[:, 32:32 + SUB * EXPERTS]
        cn_ps = misc[:, 48:48 + EXPERTS]
        bt_ps = misc[:, 128:128 + EXPERTS * HC + HC]

        s_const = sem("s_const")
        s_bias_in = sem("s_bias_in")
        s_wr_in = sem("s_wr_in")
        s_bpj_in = sem("s_bpj_in")
        s_x_in = sem2("s_x_in")
        s_row_out = sem2("s_row_out")
        s_xt_out = sem2("s_xt_out")
        s_w_in = sem2("s_w_in")
        s_w_out = sem2("s_w_out")
        s_bt_out = sem("s_bt_out")
        s_scat = sem2("s_scat")
        s_y_out = sem2("s_y_out")
        s_pad = sem("s_pad")
        s_xs_in = sem2("s_xs_in")
        s_wfc_in = sem2("s_wfc_in")
        s_bfc_in = sem2("s_bfc_in")
        s_wpj_in = sem2("s_wpj_in")
        s_bpjx_in = sem2("s_bpjx_in")
        s_kv_in = sem2("s_kv_in")
        s_q_in = sem2("s_q_in")
        s_sc_in = sem2("s_sc_in")
        s_by_in = sem2("s_by_in")
        s_bx_in = sem2("s_bx_in")
        s_gat = sem2("s_gat")
        s_out = sem2("s_out")
        s_iota = sem("s_iota")
        s_bt_tr = sem("s_bt_tr")
        s_bt = sem("s_bt")
        s_wr = sem("s_wr")
        s_w0_in = sem2("s_w0_in")
        s_w0_hi = sem("s_w0_hi")
        s_w0_lo = sem("s_w0_lo")
        s_warm = sem("s_warm")
        s_lna = sem("s_lna")
        s_rstd = sem("s_rstd")
        s_lnb = sem("s_lnb")
        s_tr = sem("s_tr")
        s_xt = sem("s_xt")
        s_logit = sem("s_logit")
        s_ra = sem("s_ra")
        s_rank = sem("s_rank")
        s_rb = sem("s_rb")
        s_msum0 = sem("s_msum0")
        s_count = sem("s_count")
        s_table = sem("s_table")
        s_y_rows = sem("s_y_rows")
        s_wsc = sem("s_wsc")
        s_whi = sem("s_whi")
        s_wlo = sem("s_wlo")
        s_mm1 = sem("s_mm1")
        s_gelu = sem("s_gelu")
        s_hhi = sem("s_hhi")
        s_hlo = sem("s_hlo")
        s_mm2 = sem("s_mm2")
        s_ev = sem("s_ev")
        s_kv_hi = sem("s_kv_hi")
        s_kv_lo = sem("s_kv_lo")
        s_k_tr = sem("s_k_tr")
        s_k_t = sem("s_k_t")
        s_gexp = sem("s_gexp")
        s_gate = sem("s_gate")
        s_qk = sem("s_qk")
        s_mul = sem("s_mul")
        s_nm = sem("s_nm")
        s_exp = sem("s_exp")
        s_inv = sem("s_inv")
        s_pt = sem("s_pt")
        s_phi = sem("s_phi")
        s_plo = sem("s_plo")
        s_pv = sem("s_pv")
        s_meta = sem("s_meta")
        s_base = sem("s_base")
        s_fin = sem("s_fin")

        LNA, LNB, RA, RB, TABLE, Y_ROWS, FIN = 5, 4, 10, 7, 17, 6, 3
        CONSTS = 10
        PREPS = 2 + SHARED

        def chain(eng, s, start):
            at = [start]

            def settle():
                wait_ge(eng, s, at[0])

            def link(ins, wait=False):
                ins.then_inc(s, 1)
                at[0] = at[0] + 1
                if wait:
                    settle()
            return link, settle

        def wait_ge(eng, s, value):
            eng.wait_ge(s, value)
            eng.nop(nofuse=True)

        @contextmanager
        def pairs(eng, first, end):
            with eng.Fori(0, (end - first) // 2) as m:
                yield eng.snap(m * 2 + first)

        def nth(n, par, each=16):
            return (n - par) * (each // 2) + each

        def rows(ap, first, n):
            return ap[ds(first, n), :].rearrange("(a p) d -> p a d", p=P)

        block = ctx.enter_context(nc.Block())

        @block.sync
        def _(sp):
            def load_x(i, par, first=False):
                if not first:
                    wait_ge(sp, s_lnb, (i - 1) * LNB)
                sp.dma_start(x_in[par][:, :, :], rows(x_rows, i * TILE, TILE)).then_inc(s_x_in[par], 16)

            def load_w(n, par, fc_src, pj_src, first=False):
                if not first and isinstance(n, int) and n == 2:
                    wait_ge(sp, s_w0_lo, DC)
                elif not first:
                    wait_ge(sp, s_wlo, n - 2)
                dst = w_stage[par]
                if par == 0:
                    sp.dma_start(dst[:, :].rearrange("p (c n) -> p c n", c=DC),
                                 fc_src.rearrange("(c p) n -> p c n", p=P)).then_inc(s_w_in[0], 16)
                else:
                    sp.dma_start(dst[:, :].rearrange("p (c n) -> p c n", c=HC),
                                 pj_src.rearrange("(c p) n -> p c n", p=P)).then_inc(s_w_in[1], 16)

            def load_expert(i, par):
                load_w(i + 2, par, wfc_rows[ds((i - par) * (D // 2), D), :],
                       wproj_rows[ds((i - par) * (HID // 2), HID), :])

            def store_w(i, par):
                wait_ge(sp, s_wlo, i + 2)
                sp.dma_start(wpack[ds((i - par) * (P // 2), P), par * 4096:(par + 1) * 4096],
                             w_split[par][:, :]).then_inc(s_w_out[par], 16)

            def store_row(i, par):
                wait_ge(sp, s_lnb, i * LNB + 2)
                sp.dma_start(key_scale[ds(i, 1), :], xn[par][0:1, :, :].rearrange("p a d -> p (a d)")
                             ).then_inc(s_row_out[par], 16)

            def store_xt(i, par):
                wait_ge(sp, s_xt, i + 1)
                sp.dma_start(xt_d[ds(i * P, P), :], x_t[par][:, :, :].rearrange("p c n -> p (c n)")
                             ).then_inc(s_xt_out[par], 16)

            def store_shared(i, par):
                wait_ge(sp, s_ev, 2 * i + 2)
                sp.dma_start(rows(shared_y, i * TILE, TILE), y_sb[par][:, :, :]).then_inc(s_y_out[par], 16)

            load_x(0, 0, first=True)
            for c in range(DC):
                sp.dma_start(w_stage[0][:, c * HID:(c + 1) * HID], wfc_s[c * P:(c + 1) * P, :]).then_inc(s_w0_in[c], 16)
            sp.dma_start(wr32[:, :, :], wr.rearrange("(c p) e -> p c e", p=P)).then_inc(s_wr_in, 16)
            sp.dma_start(b_rows[0:EXPERTS * HC, :], bfc_rows).then_inc(s_bias_in, 16)
            sp.dma_start(b_rows[EXPERTS * HC:, :], bfc_s_rows).then_inc(s_bias_in, 16)
            load_x(1, 1, first=True)
            load_w(1, 1, wfc_s, wproj_s, first=True)
            sp.dma_start(b_pj_s[:, :], bproj_s.partition_broadcast(P)).then_inc(s_bpj_in, 16)
            store_row(0, 0)
            store_xt(0, 0)
            load_x(2, 0)
            load_expert(0, 0)
            load_expert(1, 1)
            store_row(1, 1)
            wait_ge(sp, s_bt, 1)
            sp.dma_start(bfct_d, b_t[:, 0:EXPERTS * HC]).then_inc(s_bt_out, 16)
            store_w(0, 0)
            store_xt(1, 1)

            def body1(i, par, last=False):
                if not last:
                    load_x(i + 2, par)
                load_expert(i + 1, 1 - par)
                store_row(i + 1, 1 - par)
                store_w(i, par)
                store_xt(i + 1, 1 - par)
                store_shared(i - 1, 1 - par)

            with pairs(sp, 1, SHARED - 3) as i:
                body1(i, 1)
                body1(i + 1, 0)
            body1(SHARED - 3, 1)
            for n, (dst, src) in enumerate(((prob, k_rows), (scale_b, v_rows))):
                for h in range(2):
                    sp.dma_start(dst[h][:, :].rearrange("p (c n) -> p c n", c=KH), rows(src, h * KH * P, KH * P)
                                 ).then_inc(s_kv_in[n], 16)
                if n == 0:
                    body1(SHARED - 2, 0, last=True)
            wait_ge(sp, s_table, TABLE)
            for e in range(EXPERTS):
                pad = sp.value_load(tab_pad[0:1, e:e + 1], min_val=0, max_val=SPARE - TILE)
                sp.dma_start(rows(slots_x, pad, TILE), zeros[:, :, :]).then_inc(s_pad, 16)
            sp.dma_start(rows(slots_x, SPARE, TILE), zeros[:, :, :]).then_inc(s_pad, 16)
            store_w(SHARED - 1, 1)
            wait_ge(sp, s_w_out[0], 8 * SHARED)
            wait_ge(sp, s_w_out[1], 8 * SHARED)
            wait_ge(sp, s_bt_out, 16)

            def load_fc(j, par, first=False):
                if not first:
                    wait_ge(sp, s_mm1, BANKS * (SHARED + j - 1))
                e = sp.value_load(tab_e[0:1, ds(j, 1)], min_val=0, max_val=EXPERTS - 1)
                sp.dma_start(w_fc[par][:, :], wpack[ds(e * P, P), 0:4096]).then_inc(s_wfc_in[par], 16)
                if not first:
                    wait_ge(sp, s_gelu, BANKS * (SHARED + j - 1))
                sp.dma_start(b_fc[par][:, :], bfct_d[:, ds(e * HC, HC)]).then_inc(s_bfc_in[par], 16)

            def load_pj(j, par, first=False):
                if not first:
                    wait_ge(sp, s_mm2, 2 * (SHARED + j - 1))
                e = sp.value_load(tab_e[0:1, ds(j, 1)], min_val=0, max_val=EXPERTS - 1)
                sp.dma_start(w_pj[par][:, :], wpack[ds(e * P, P), 4096:8192]).then_inc(s_wpj_in[par], 16)
                if not first:
                    wait_ge(sp, s_ev, 2 * (SHARED + j - 1))
                sp.dma_start(b_pj[par][:, :], bproj[ds(e, 1), :].rearrange("e n -> (e n)").partition_broadcast(P)
                             ).then_inc(s_bpjx_in[par], 16)

            def load_slots(j, par):
                wait_ge(sp, s_tr, SHARED + j - 1)
                r = sp.value_load(tab_x[0:1, ds(j, 1)], min_val=0, max_val=SPARE)
                sp.dma_start(x_split[par][:, :, :], rows(slots_x, r, TILE)).then_inc(s_xs_in[par], 16)

            def store_slots(j, par):
                wait_ge(sp, s_ev, 2 * (SHARED + j) + 2)
                sp.dma_start(rows(slots_y, j * TILE, TILE), y_sb[par][:, :, :]).then_inc(s_y_out[par], 16)

            load_fc(0, 0, first=True)
            wait_ge(sp, s_scat[0], 32 * SHARED)
            wait_ge(sp, s_scat[1], 32 * SHARED)
            wait_ge(sp, s_pad, 16 * (EXPERTS + 1))
            load_slots(0, 0)
            load_slots(1, 1)
            load_fc(1, 1, first=True)
            load_pj(0, 0, first=True)
            store_shared(SHARED - 2, 0)
            store_shared(SHARED - 1, 1)

            load_fc(2, 0)
            load_slots(3, 1)
            load_slots(2, 0)
            load_pj(1, 1, first=True)

            def body2(j, par, tail=0):
                if tail < 2:
                    load_fc(j + 1, 1 - par)
                if tail < 1:
                    load_slots(j + 2, par)
                load_pj(j, par)
                store_slots(j - 2, par)

            body2(2, 0, tail=1)
            load_slots(4, 0)
            with pairs(sp, 3, ROUTED - 4) as j:
                body2(j, 1)
                body2(j + 1, 0)
            body2(ROUTED - 4, 1)
            body2(ROUTED - 3, 0)
            body2(ROUTED - 2, 1, tail=1)
            body2(ROUTED - 1, 0, tail=2)

            def load_q(m, par, first=False):
                if not first:
                    wait_ge(sp, s_qk, 2 * m - 2)
                sp.dma_start(q_t[par][:, :, :].rearrange("p c n -> p (c n)"), xt_d[ds(m * P, P), :]
                             ).then_inc(s_q_in[par], 16)

            def load_scale(b, par, first=False):
                if not first:
                    wait_ge(sp, s_mul, 4 * (b - 1))
                src = key_scale[ds(b * 2, 2), :].rearrange("r n -> (r n)")
                sp.dma_start(scale_b[par][:, :], src.partition_broadcast(P)).then_inc(s_sc_in[par], 16)

            def load_base(u, par, first=False):
                if not first:
                    wait_ge(sp, s_base, u - 1)
                sp.dma_start(base_y[par][:, :], shared_y[ds(u * P, P), :]).then_inc(s_by_in[par], 16)
                if not first:
                    wait_ge(sp, s_fin, FIN * (u - 1))
                sp.dma_start(base_x[par][:, :], x_rows[ds(u * P, P), :]).then_inc(s_bx_in[par], 16)

            def store_out(u, par):
                wait_ge(sp, s_fin, FIN * (u + 1))
                sp.dma_start(out_rows[ds(u * P, P), :], o_sb[par][:, :]).then_inc(s_out[par], 16)

            for par in range(2):
                wait_ge(sp, s_xt_out[par], 8 * SHARED)
                wait_ge(sp, s_row_out[par], 8 * SHARED)
                wait_ge(sp, s_y_out[par], 8 * SHARED)
            wait_ge(sp, s_kv_lo, 4)
            load_q(0, 0, first=True)
            load_scale(0, 0, first=True)
            store_slots(ROUTED - 2, 1)
            load_q(1, 1, first=True)
            load_base(0, 0, first=True)
            store_slots(ROUTED - 1, 0)
            load_base(1, 1, first=True)
            load_scale(1, 1, first=True)

            def body3(u0, first=False, last=False):
                for s in range(8):
                    u = u0 + s
                    if s % 2 == 1 and not (last and s > 3):
                        m = u0 // 2 if isinstance(u0, int) else None
                        pair = (m if m is not None else half(u0)) + s // 2 + 2
                        load_q(pair, (s // 2) % 2)
                    if s == 2 and not last:
                        load_scale(quarter(u0) + 2, 0)
                    if s == 6 and not last:
                        load_scale(quarter(u0) + 3, 1)
                    if not (first and s == 0):
                        store_out(u - 1, (s + 1) % 2)
                    if not (first and s == 0) and not (last and s == 7):
                        load_base(u + 1, (s + 1) % 2)

            def half(u0):
                return u0 // 2 if isinstance(u0, int) else g8 * 4

            def quarter(u0):
                return u0 // 4 if isinstance(u0, int) else g8 * 2

            body3(0, first=True)
            with sp.Fori(1, QT // 8 - 1) as g:
                g8 = sp.snap(g)
                body3(g8 * 8)
            body3(QT - 8, last=True)
            store_out(QT - 1, 1)
            wait_ge(sp, s_out[0], 8 * QT)
            wait_ge(sp, s_out[1], 8 * QT)

        @block.gpsimd
        def _(pool):
            g = nc.gpsimd
            g.memset(ident_h[:, :], 0.0).then_inc(s_iota, 1)
            g.memset(ident_f[:, :], 0.0).then_inc(s_iota, 1)
            g.memset(before[:, :], 1.0).then_inc(s_iota, 1)
            wait_ge(pool, s_iota, 3)
            for t in (ident_h, ident_f):
                g.affine_select(out=t[:, :], in_=t[:, :], compare_op=ALU.not_equal, fill=1.0, base=0,
                                pattern=[[-1, P]], channel_multiplier=1).then_inc(s_const, 1)
            g.affine_select(out=before[:, :], in_=before[:, :], compare_op=ALU.is_gt, fill=0.0, base=0,
                            pattern=[[1, P]], channel_multiplier=-1).then_inc(s_const, 1)
            g.memset(ones_h[:, :], 1.0).then_inc(s_const, 1)
            g.iota(iota_e[:, :], pattern=[[1, EXPERTS]], base=0, channel_multiplier=0,
                   allow_small_or_imprecise_dtypes=True).then_inc(s_const, 1)
            g.iota(region[:, :], pattern=[[CAP, EXPERTS]], base=0, channel_multiplier=0,
                   allow_small_or_imprecise_dtypes=True).then_inc(s_const, 1)
            g.iota(step_no[:, :], pattern=[[1, ROUTED]], base=0, channel_multiplier=0,
                   allow_small_or_imprecise_dtypes=True).then_inc(s_const, 1)
            g.memset(neg_half[:, :], -0.5).then_inc(s_const, 1)
            g.memset(zeros[:, :, :], 0.0).then_inc(s_const, 1)
            g.memset(one_row[:, :], 1.0).then_inc(s_const, 1)
            wait_ge(pool, s_const, CONSTS)

            def inv_std(i, par):
                wait_ge(pool, s_lna, (i + 1) * LNA)
                g.tensor_tensor(rstd[par][:, :], var_eps[par][:, :], neg_half[:, :], ALU.pow).then_inc(s_rstd, 1)

            def split_w_lo(n, par, dst):
                wait_ge(pool, s_whi, n)
                g.tensor_tensor(dst[:, 2048:4096], w_stage[par][:, :], dst[:, 0:2048], ALU.subtract).then_inc(s_wlo, 1)

            def scatter(i, par):
                wait_ge(pool, s_rb, i * RB + 6)
                for a in range(SUB):
                    for kk in range(TOP):
                        c = a * TOP + kk
                        g.indirect_dma_start(slots_x, bass.IndirectOffsetOnAxis(ap=pos_i[par][:, c:c + 1], axis=0),
                                             x_split[par][:, a, :], None).then_inc(s_scat[par], 16)

            inv_std(0, 0)
            inv_std(1, 1)
            split_w_lo(1, 1, w_shared[1])

            def body1(i, par, last=False):
                if not last:
                    inv_std(i + 1, 1 - par)
                scatter(i, par)
                split_w_lo(i + 2, par, w_split[par])

            split_w_lo(2, 0, w_split[0])
            scatter(0, 0)
            with pairs(pool, 1, SHARED - 1) as i:
                body1(i, 1)
                body1(i + 1, 0)
            body1(SHARED - 1, 1, last=True)

            def gather(u, par, first=False):
                if not first:
                    wait_ge(pool, s_fin, FIN * (u - 1))
                g.tensor_copy(pos_u[par][:, :], y_row_all[:, ds(u * TOP, TOP)]).then_inc(s_meta, 1)
                g.tensor_copy(gate_u[par][:, :], gates[:, ds(u, 1), :].rearrange("p o k -> p (o k)")).then_inc(s_meta, 1)
                wait_ge(pool, s_meta, 2 * u + 1)
                for kk in range(TOP):
                    g.indirect_dma_start(y_rows[par][:, kk, :], None, slots_y,
                                         bass.IndirectOffsetOnAxis(ap=pos_u[par][:, kk:kk + 1], axis=0)
                                         ).then_inc(s_gat[par], 16)

            def add_base(u, par):
                wait_ge(pool, s_by_in[par], nth(u, par))
                wait_ge(pool, s_bx_in[par], nth(u, par))
                g.tensor_tensor(base_x[par][:, :], base_x[par][:, :], base_y[par][:, :], ALU.add).then_inc(s_base, 1)

            wait_ge(pool, s_gate, 3)
            wait_ge(pool, s_y_rows, Y_ROWS)
            for par in range(2):
                wait_ge(pool, s_y_out[par], 16 * ((SHARED + ROUTED + 1 - par) // 2))
            gather(0, 0, first=True)
            add_base(0, 0)
            gather(1, 1, first=True)
            add_base(1, 1)
            with pairs(pool, 2, QT) as u:
                gather(u, 0)
                add_base(u, 0)
                gather(u + 1, 1)
                add_base(u + 1, 1)

        @block.scalar
        def _(act):
            def split_w_hi(n, par, dst, stored):
                act.wait_ge(s_w_in[par], nth(n, par) - (16 if par == 0 else 0))
                nc.scalar.mul(w_stage[par][:, :], w_stage[par][:, :], WS).then_inc(s_wsc, 1)
                act.wait_ge(s_wsc, n)
                if stored is not None:
                    act.wait_ge(s_w_out[par], stored)
                nc.scalar.copy(dst[:, 0:2048], w_stage[par][:, :]).then_inc(s_whi, 1)

            def gelu(t, par, bias, first=False):
                for b in range(BANKS):
                    act.wait_ge(s_mm1, BANKS * t + b + 1)
                    if not first:
                        act.wait_ge(s_hlo, BANKS * (t - 1) + b + 1)
                    for half in range(2):
                        hc = 2 * b + half
                        ins = nc.scalar.activation(h32[:, hc, :], ps_h[:, hc * TILE:(hc + 1) * TILE],
                                                   ACT.Gelu_apprx_tanh, bias=bias[:, hc:hc + 1], scale=1.0 / WS)
                    ins.then_inc(s_gelu, 1)
                    if b == 0 and not (isinstance(t, int) and t < 2):
                        act.wait_ge(s_mm2, 2 * (t - 1))
                    act.wait_ge(s_gelu, BANKS * t + b + 1)
                    nc.scalar.copy(h_split[par][:, 0, 2 * b:2 * b + 2, :], h32[:, 2 * b:2 * b + 2, :]).then_inc(s_hhi, 1)

            b_s = b_t[:, EXPERTS * HC:EXPERTS * HC + HC]
            act.wait_ge(s_const, CONSTS)
            nc.scalar.activation(gap_exp[:, 0:SUB], neg_half[:, :], ACT.Gelu_apprx_tanh).then_inc(s_warm, 1)
            for c in range(DC):
                act.wait_ge(s_w0_in[c], 16)
                nc.scalar.mul(w_shared[0][:, c * HID:(c + 1) * HID], w_stage[0][:, c * HID:(c + 1) * HID], WS
                              ).then_inc(s_w0_hi, 1)
            split_w_hi(1, 1, w_shared[1], None)
            act.wait_ge(s_bt, 1)
            gelu(0, 0, b_s, first=True)
            split_w_hi(2, 0, w_split[0], None)
            gelu(1, 1, b_s)
            split_w_hi(3, 1, w_split[1], None)
            with pairs(act, 2, SHARED - 2) as i:
                gelu(i, 0, b_s)
                split_w_hi(i + 2, 0, w_split[0], i * 8)
                gelu(i + 1, 1, b_s)
                split_w_hi(i + 3, 1, w_split[1], i * 8)
            gelu(SHARED - 2, 0, b_s)
            split_w_hi(SHARED, 0, w_split[0], (SHARED - 2) * 8)
            split_w_hi(SHARED + 1, 1, w_split[1], (SHARED - 2) * 8)
            gelu(SHARED - 1, 1, b_s)
            act.wait_ge(s_kv_in[0], 32)
            for h in range(2):
                nc.scalar.copy(k_split[h][:, :, 0:D], prob[h][:, :].rearrange("p (c n) -> p c n", c=KH)).then_inc(s_kv_hi, 1)
            act.wait_ge(s_kv_in[1], 32)
            for h in range(2):
                nc.scalar.copy(v_split[:, 0, h * KH:(h + 1) * KH, :], scale_b[h][:, :].rearrange("p (c n) -> p c n", c=KH)
                               ).then_inc(s_kv_hi, 1)

            def step2(j, par):
                act.wait_ge(s_bfc_in[par], nth(j, par))
                gelu(SHARED + j, par, b_fc[par])

            step2(0, 0)
            with pairs(act, 1, ROUTED) as j:
                step2(j, 1)
                step2(j + 1, 0)

            act.wait_ge(s_warm, 1)
            nc.scalar.activation(gap_exp[:, :], gap_all[:, :], ACT.Exp, scale=1.0 / WS).then_inc(s_gexp, 1)

            def exp(u, par, first=False):
                act.wait_ge(s_nm, u + 1)
                if not first:
                    act.wait_ge(s_inv, u - 1)
                nc.scalar.activation(prob[par][:, :], prob[par][:, :], ACT.Exp, bias=neg_max[par][:, 0:1],
                                     accum_out=row_sum[par][:, 0:1]).then_inc(s_exp, 1)

            def p_hi(u, par, first=False):
                for kk in range(2):
                    act.wait_ge(s_pt, 2 * u + kk + 1)
                    if kk == 0 and not first:
                        act.wait_ge(s_pv, u - 1)
                    nc.scalar.copy(p_t[par][:, 0, 4 * kk:4 * kk + 4, :],
                                   ps_t[:, kk * 512:(kk + 1) * 512].rearrange("p (c n) -> p c n", n=P)).then_inc(s_phi, 1)

            exp(0, 0, first=True)
            exp(1, 1, first=True)
            for u in range(2):
                p_hi(u, u, first=True)
                exp(u + 2, u)
            with pairs(act, 2, QT - 2) as u:
                p_hi(u, 0)
                exp(u + 2, 0)
                p_hi(u + 1, 1)
                exp(u + 3, 1)
            p_hi(QT - 2, 0)
            p_hi(QT - 1, 1)

        @block.vector
        def _(dve):
            ve = nc.vector

            def copy_xt(t, par, stored=None):
                dve.wait_ge(s_tr, t + 1)
                if not (isinstance(t, int) and t < 2):
                    dve.wait_ge(s_mm1, BANKS * (t - 1))
                if stored is not None:
                    dve.wait_ge(s_xt_out[par], stored)
                ve.tensor_copy(x_t[par][:, :, :], tr16[:, :].rearrange("p (c n) -> p c n", n=TILE)).then_inc(s_xt, 1)

            def front_a(stat=None, route=None):
                if stat is not None:
                    i, par = stat
                    lna, lna_settle = chain(dve, s_lna, i * LNA)
                    dve.wait_ge(s_x_in[par], nth(i, par))
                    dve.nop(nofuse=True)
                    lna(ve.bn_stats(stats[:, 0, :], x_in[par][:, 0, :]))
                if route is not None:
                    r, rpar = route
                    ra, ra_settle = chain(dve, s_ra, r * RA)
                    dve.wait_ge(s_logit, r + 1)
                    ra(ve.tensor_reduce(logits[:, :, :], lg_ps.rearrange("p (a h e) -> p a e h", a=SUB, h=2), AX, ALU.add))
                if stat is not None:
                    lna(ve.bn_stats(stats[:, 1, :], x_in[par][:, 1, :]))
                if route is not None:
                    ra_settle()
                    for a in range(SUB):
                        ra(ve.max(top_v[:, a, :], logits[:, a, :]))
                    ra_settle()
                    for a in range(SUB):
                        ra(ve.max_index(top_i[:, a, :], top_v[:, a, :], logits[:, a, :]))
                if stat is not None:
                    lna_settle()
                    for a in range(SUB):
                        lna(ve.bn_aggr(mean_var[par][:, a, :], stats[:, a, :]))
                if route is not None:
                    ra_settle()
                    ra(ve.tensor_copy(top_f[:, :, :], top_i[:, :, 0:TOP]))
                if stat is not None:
                    lna_settle()
                    lna(ve.tensor_scalar(var_eps[par][:, :], mean_var[par][:, :, 1], EPS, None, ALU.add))
                if route is not None:
                    ra_settle()
                    top_flat = top_f[:, :, :].rearrange("p a k -> p (a k)")
                    ra(ve.tensor_tensor(chosen[:, :, :, :].rearrange("p a k e -> p (a k) e"),
                                        top_flat.unsqueeze(2).to_broadcast([P, SUB * TOP, EXPERTS]),
                                        iota_e[:, :].unsqueeze(1).to_broadcast([P, SUB * TOP, EXPERTS]), ALU.is_equal))
                    ra(ve.tensor_copy(exp_all[:, ds(r * SUB * TOP, SUB * TOP)], top_flat))
                    ra(ve.tensor_tensor(gap_all[:, ds(r * SUB, SUB)], top_v[:, :, 1], top_v[:, :, 0], ALU.subtract))
                    ra_settle()
                    ra(ve.tensor_tensor(mask[rpar][:, :, :], chosen[:, :, 0, :], chosen[:, :, 1, :], ALU.add))

            def front_b(norm=None, route=None):
                if norm is not None:
                    i, par = norm
                    lnb, lnb_settle = chain(dve, s_lnb, i * LNB)
                    dve.wait_ge(s_rstd, i + 1)
                    if not (isinstance(i, int) and i < 2):
                        dve.wait_ge(s_row_out[par], (i - par) * 8)
                        dve.wait_ge(s_scat[par], (i - par) * 32)
                        dve.wait_ge(s_tr, i - 1)
                    for a in range(SUB):
                        lnb(ve.tensor_scalar(xn[par][:, a, :], x_in[par][:, a, :], mean_var[par][:, a, 0:1],
                                             rstd[par][:, a:a + 1], ALU.subtract, ALU.mult))
                    lnb_settle()
                    lnb(ve.tensor_copy(x_split[par][:, :, 0:D], xn[par][:, :, :]))
                if route is not None:
                    r, rpar = route
                    rb, rb_settle = chain(dve, s_rb, r * RB)
                    dve.wait_ge(s_rank, r + 1)
                    if not (isinstance(r, int) and r < 2):
                        dve.wait_ge(s_scat[rpar], (r - rpar) * 32)
                    rb(ve.tensor_tensor(mask_sum[:, :], mask_sum[:, :], mask[rpar][:, 0, :], ALU.add))
                    rb(ve.tensor_tensor(slot_of[:, :, :], rk_ps.rearrange("p (a e) -> p a e", a=SUB),
                                        region[:, :].unsqueeze(1).to_broadcast([P, SUB, EXPERTS]), ALU.add))
                if norm is not None:
                    lnb_settle()
                    lnb(ve.tensor_tensor(x_split[par][:, :, D:ROW], xn[par][:, :, :], x_split[par][:, :, 0:D],
                                         ALU.subtract))
                if route is not None:
                    rb_settle()
                    rb(ve.tensor_tensor(mask_sum[:, :], mask_sum[:, :], mask[rpar][:, 1, :], ALU.add))
                    rb(ve.tensor_tensor(picked[:, :, :, :], chosen[:, :, :, :],
                                        slot_of[:, :, :].unsqueeze(2).to_broadcast([P, SUB, TOP, EXPERTS]), ALU.mult))
                    rb_settle()
                    rb(ve.tensor_reduce(pos_f[:, :], picked[:, :, :, :].rearrange("p a k e -> p (a k) e"), AX, ALU.add))
                    rb_settle()
                    rb(ve.tensor_copy(pos_i[rpar][:, :], pos_f[:, :]))
                    rb(ve.tensor_copy(pos_all[:, ds(r * SUB * TOP, SUB * TOP)], pos_f[:, :]))

            def split_h(t, par, banks):
                for b in banks:
                    dve.wait_ge(s_hhi, BANKS * t + b + 1)
                    ve.tensor_tensor(h_split[par][:, 1, 2 * b:2 * b + 2, :], h32[:, 2 * b:2 * b + 2, :],
                                     h_split[par][:, 0, 2 * b:2 * b + 2, :], ALU.subtract).then_inc(s_hlo, 1)

            def evict(t, par, bias):
                if not (isinstance(t, int) and t < 2):
                    dve.wait_ge(s_y_out[par], (t - par) * 8)
                for a in range(SUB):
                    dve.wait_ge(s_mm2, 2 * t + a + 1)
                    ve.scalar_tensor_tensor(out=y_sb[par][:, a, :], in0=ps_y[a][:, 0:D], scalar=1.0 / WS,
                                            in1=bias[:, :], op0=ALU.mult, op1=ALU.add).then_inc(s_ev, 1)

            dve.wait_ge(s_wr_in, 16)
            link, _ = chain(dve, s_wr, 0)
            link(ve.tensor_scalar(wr32[:, :, :], wr32[:, :, :], WS, None, ALU.mult), wait=True)
            link(ve.tensor_copy(wr_s[:, :, 0:EXPERTS], wr32[:, :, :]), wait=True)
            link(ve.tensor_tensor(wr_s[:, :, EXPERTS:], wr32[:, :, :], wr_s[:, :, 0:EXPERTS], ALU.subtract))
            ve.memset(mask_sum[:, :], 0.0).then_inc(s_msum0, 1)
            dve.wait_ge(s_bt_tr, 1)
            ve.tensor_copy(b_t[:, :], bt_ps).then_inc(s_bt, 1)

            def split_w0_lo(c):
                dve.wait_ge(s_w0_hi, c + 1)
                ve.scalar_tensor_tensor(out=w_shared[0][:, 2048 + c * HID:2048 + (c + 1) * HID],
                                        in0=w_stage[0][:, c * HID:(c + 1) * HID], scalar=WS,
                                        in1=w_shared[0][:, c * HID:(c + 1) * HID],
                                        op0=ALU.mult, op1=ALU.subtract).then_inc(s_w0_lo, 1)

            front_a(stat=(0, 0))
            split_w0_lo(0)
            front_b(norm=(0, 0))
            split_w0_lo(1)
            copy_xt(0, 0)
            dve.wait_ge(s_const, CONSTS)
            dve.wait_ge(s_msum0, 1)
            front_a(stat=(1, 1), route=(0, 0))
            front_b(norm=(1, 1), route=(0, 0))
            split_h(0, 0, range(BANKS))
            copy_xt(1, 1)
            dve.wait_ge(s_bpj_in, 16)

            def body1(i, par):
                front_a(stat=(i + 1, 1 - par), route=(i, par))
                front_b(norm=(i + 1, 1 - par), route=(i, par))
                split_h(i, par, range(BANKS))
                copy_xt(i + 1, 1 - par, stored=(i + 1 - (1 - par)) * 8)
                evict(i - 1, 1 - par, b_pj_s)

            with pairs(dve, 1, SHARED - 1) as i:
                body1(i, 1)
                body1(i + 1, 0)
            front_a(route=(SHARED - 1, 1))
            front_b(route=(SHARED - 1, 1))

            dve.wait_ge(s_count, 1)
            link, _ = chain(dve, s_table, 0)
            link(ve.tensor_copy(cnt[:, :], cn_ps), wait=True)
            link(ve.tensor_tensor(tab_pad[:, :], cnt[0:1, :], region[0:1, :], ALU.add))
            link(ve.tensor_scalar(cnt_i[:, :], cnt[:, :], float(TILE - 1), None, ALU.add), wait=True)
            link(ve.tensor_scalar(blk_i[:, :], cnt_i[:, :], BLK_SHIFT, None, ALU.arith_shift_right), wait=True)
            link(ve.tensor_copy(blk[:, :], blk_i[:, :]), wait=True)
            link(ve.tensor_tensor_scan(blk_end[:, :], one_row[:, :], blk[:, :], 0.0, ALU.mult, ALU.add), wait=True)
            each = [1, ROUTED, EXPERTS]
            link(ve.tensor_tensor(past[:, :, :], step_no[:, :].unsqueeze(2).to_broadcast(each),
                                  blk_end[0:1, :].unsqueeze(1).to_broadcast(each), ALU.is_ge), wait=True)
            link(ve.tensor_reduce(step_e[:, :], past[:, :, :], AX, ALU.add))
            link(ve.tensor_tensor(past_blk[:, :, :], past[:, :, :], blk[0:1, :].unsqueeze(1).to_broadcast(each), ALU.mult), wait=True)
            link(ve.tensor_reduce(step_b[:, :], past_blk[:, :, :], AX, ALU.add), wait=True)
            link(ve.tensor_tensor(step_b[:, :], step_no[:, :], step_b[:, :], ALU.subtract), wait=True)
            link(ve.tensor_scalar(step_b[:, :], step_b[:, :], float(TILE), None, ALU.mult), wait=True)
            link(ve.scalar_tensor_tensor(out=step_r[:, :], in0=step_e[:, :], scalar=float(CAP), in1=step_b[:, :],
                                         op0=ALU.mult, op1=ALU.add), wait=True)
            link(ve.tensor_scalar(step_r[:, :], step_r[:, :], float(SPARE), None, ALU.min), wait=True)
            link(ve.tensor_copy(tab_x[:, :], step_r[:, :]))
            link(ve.tensor_scalar(step_e[:, :], step_e[:, :], float(EXPERTS - 1), None, ALU.min), wait=True)
            link(ve.tensor_copy(tab_e[:, :], step_e[:, :]), wait=True)

            split_h(SHARED - 1, 1, range(BANKS))
            evict(SHARED - 2, 0, b_pj_s)
            for h in range(2):
                dve.wait_ge(s_kv_hi, 1 + h)
                ve.tensor_tensor(k_split[h][:, :, D:ROW], prob[h][:, :].rearrange("p (c n) -> p c n", c=KH),
                                 k_split[h][:, :, 0:D], ALU.subtract).then_inc(s_kv_lo, 1)
            evict(SHARED - 1, 1, b_pj_s)
            for m in range(KC // 2):
                dve.wait_ge(s_k_tr, m + 1)
                ve.tensor_copy(k_t[:, :, m * TILE:(m + 1) * TILE], tr16[:, :].rearrange("p (c n) -> p c n", n=TILE)
                               ).then_inc(s_k_t, 1)
            for h in range(2):
                dve.wait_ge(s_kv_hi, 3 + h)
                half = slice(h * KH, (h + 1) * KH)
                ve.tensor_tensor(v_split[:, 1, half, :], scale_b[h][:, :].rearrange("p (c n) -> p c n", c=KH),
                                 v_split[:, 0, half, :], ALU.subtract).then_inc(s_kv_lo, 1)

            copy_xt(SHARED, 0, stored=8 * SHARED)
            link, _ = chain(dve, s_y_rows, 0)
            link(ve.tensor_tensor(shift_e[:, :], blk_end[:, :], blk[:, :], ALU.subtract), wait=True)
            link(ve.scalar_tensor_tensor(out=shift_e[:, :], in0=shift_e[:, :], scalar=float(TILE), in1=region[:, :],
                                         op0=ALU.mult, op1=ALU.subtract), wait=True)
            every = [P, QT * TOP, EXPERTS]
            link(ve.tensor_tensor(match_e[:, :, :], exp_all[:, :].unsqueeze(2).to_broadcast(every),
                                  iota_e[:, :].unsqueeze(1).to_broadcast(every), ALU.is_equal), wait=True)
            link(ve.tensor_tensor(match_e[:, :, :], match_e[:, :, :], shift_e[:, :].unsqueeze(1).to_broadcast(every),
                                  ALU.mult), wait=True)
            link(ve.tensor_reduce(shift_t[:, :], match_e[:, :, :], AX, ALU.add), wait=True)
            link(ve.tensor_tensor(y_row_all[:, :], pos_all[:, :], shift_t[:, :], ALU.add))
            split_h(SHARED, 0, range(BANKS))
            copy_xt(SHARED + 1, 1, stored=8 * SHARED)

            def evict2(j, par):
                dve.wait_ge(s_bpjx_in[par], nth(j, par))
                evict(SHARED + j, par, b_pj[par])

            def body2(j, par):
                split_h(SHARED + j, par, range(BANKS))
                copy_xt(SHARED + j + 1, 1 - par)
                evict2(j - 1, 1 - par)

            with pairs(dve, 1, ROUTED - 2) as j:
                body2(j, 1)
                body2(j + 1, 0)
            body2(ROUTED - 2, 1)
            split_h(SHARED + ROUTED - 1, 0, range(BANKS))
            evict2(ROUTED - 2, 1)

            def scale_scores(u, par, bpar, loaded, first=False):
                dve.wait_ge(s_qk, u + 1)
                if loaded is not None:
                    dve.wait_ge(s_sc_in[bpar], loaded)
                if not first:
                    dve.wait_ge(s_pt, 2 * (u - 1))
                dve.nop(nofuse=True)
                ve.tensor_tensor_reduce(out=prob[par][:, :], in0=ps_h[:, par * KEYS:(par + 1) * KEYS], in1=scale_b[bpar][:, :],
                                        scale=1.0, scalar=-3.0e38, op0=ALU.mult, op1=ALU.max,
                                        accum_out=row_max[par][:, 0:1]).then_inc(s_mul, 1)
                dve.wait_ge(s_mul, u + 1)
                ve.tensor_scalar(neg_max[par][:, :], row_max[par][:, :], -1.0, None, ALU.mult).then_inc(s_nm, 1)

            def p_lo(u, par, first=False):
                dve.wait_ge(s_exp, u + 1)
                if not first:
                    dve.wait_ge(s_fin, FIN * (u - 2) + 1)
                ve.reciprocal(inv_sum[par][:, :], row_sum[par][:, :]).then_inc(s_inv, 1)
                for kk in range(2):
                    dve.wait_ge(s_phi, 2 * u + kk + 1)
                    ve.tensor_tensor(p_t[par][:, 1, 4 * kk:4 * kk + 4, :],
                                     ps_t[:, kk * 512:(kk + 1) * 512].rearrange("p (c n) -> p c n", n=P),
                                     p_t[par][:, 0, 4 * kk:4 * kk + 4, :], ALU.subtract).then_inc(s_plo, 1)

            def finish(u, par, first=False):
                link, _ = chain(dve, s_fin, u * FIN)
                dve.wait_ge(s_inv, u + 1)
                dve.wait_ge(s_pv, u + 1)
                dve.wait_ge(s_base, u + 1)
                if not first:
                    dve.wait_ge(s_out[par], (u - par) * 8)
                link(ve.scalar_tensor_tensor(out=o_sb[par][:, :], in0=ps_y[par][:, 0:D], scalar=inv_sum[par][:, 0:1],
                                             in1=base_x[par][:, :], op0=ALU.mult, op1=ALU.add), wait=True)
                dve.wait_ge(s_meta, 2 * u + 2)
                dve.wait_ge(s_gat[par], nth(u, par, 32))
                for kk in range(TOP):
                    link(ve.scalar_tensor_tensor(out=o_sb[par][:, :], in0=y_rows[par][:, kk, :], scalar=gate_u[par][:, kk:kk + 1],
                                                 in1=o_sb[par][:, :], op0=ALU.mult, op1=ALU.add), wait=kk == 0)

            def body3(u0, g8, first=False, last=False):
                for s in range(8):
                    u, par = u0 + s, s % 2
                    p_lo(u, par, first=first and s < 2)
                    if not (last and s >= 6):
                        n = s + 2
                        loaded = None
                        if n % 4 == 0:
                            loaded = (g8 + n // 8) * 16 + 16
                        scale_scores(u + 2, par, (n // 4) % 2, loaded)
                    if not (first and s == 0):
                        finish(u - 1, 1 - par, first=first and s < 3)

            dve.wait_ge(s_gexp, 1)
            link, _ = chain(dve, s_gate, 0)
            link(ve.tensor_scalar(gap_den[:, :], gap_exp[:, :], 1.0, None, ALU.add), wait=True)
            link(ve.reciprocal(gates[:, :, 0], gap_den[:, :]), wait=True)
            link(ve.tensor_tensor(gates[:, :, 1], gap_exp[:, :], gates[:, :, 0], ALU.mult))
            scale_scores(0, 0, 0, 16, first=True)
            evict2(ROUTED - 1, 0)
            scale_scores(1, 1, 0, None, first=True)

            body3(0, 0, first=True)
            with dve.Fori(1, QT // 8 - 1) as g3:
                g = dve.snap(g3)
                body3(g * 8, g)
            body3(QT - 8, QT // 8 - 1, last=True)
            finish(QT - 1, 1)

        @block.tensor
        def _(pe):
            mm = nc.tensor.matmul
            TERMS = ((0, 0), (0, 1), (1, 0))

            def transpose_rows(t, par, src):
                for hl in range(2):
                    for c in range(DC):
                        for a in range(SUB):
                            n = (hl * DC + c) * TILE + a * P
                            o = hl * D + c * P
                            ins = nc.tensor.transpose(tr16[:, n:n + P], src[:, a, o:o + P], ident_h[:, :])
                return ins

            def tr1(i, par):
                pe.wait_ge(s_lnb, (i + 1) * LNB)
                if not (isinstance(i, int) and i == 0):
                    pe.wait_ge(s_xt, i)
                transpose_rows(i, par, x_split[par]).then_inc(s_tr, 1)

            def tr2(j, par):
                pe.wait_ge(s_xs_in[par], nth(j, par))
                pe.wait_ge(s_xt, SHARED + j)
                transpose_rows(j, par, x_split[par]).then_inc(s_tr, 1)

            def router(i, par):
                pe.wait_ge(s_xt, i + 1)
                if not (isinstance(i, int) and i == 0):
                    pe.wait_ge(s_rb, i * RB)
                for a in range(SUB):
                    for n in range(2 * DC):
                        ins = mm(lg_ps[:, a * 16:(a + 1) * 16], x_t[par][:, n, a * P:(a + 1) * P], wr_s[:, n % DC, :],
                                 start=n == 0, stop=n == 2 * DC - 1)
                ins.then_inc(s_logit, 1)

            def rank(i, par):
                pe.wait_ge(s_ra, (i + 1) * RA)
                for a in range(SUB):
                    o = rk_ps[:, a * EXPERTS:(a + 1) * EXPERTS]
                    mm(o, before[:, :], mask[par][:, a, :], start=True, stop=False)
                    if a == 1:
                        mm(o, ones_h[:, :], mask[par][:, 0, :], start=False, stop=False)
                    ins = mm(o, ones_h[:, :], mask_sum[:, :], start=False, stop=True)
                ins.then_inc(s_rank, 1)

            def up(t, par, w, banks=range(BANKS)):
                pe.wait_ge(s_xt, t + 1)
                wv = w[:, :].rearrange("p (h c n) -> p h c n", h=2, c=DC)
                for b in banks:
                    if not (isinstance(t, int) and t == 0):
                        pe.wait_ge(s_gelu, BANKS * (t - 1) + b + 1)
                    for hc in (2 * b, 2 * b + 1):
                        n = 0
                        for wl, xl in TERMS:
                            for c in range(DC):
                                ins = mm(ps_h[:, hc * TILE:(hc + 1) * TILE], wv[:, wl, c, hc * P:(hc + 1) * P],
                                         x_t[par][:, xl * DC + c, :], start=n == 0, stop=n == 3 * DC - 1)
                                n += 1
                    ins.then_inc(s_mm1, 1)

            def down(t, par, w, halves=range(SUB)):
                pe.wait_ge(s_hlo, BANKS * (t + 1))
                wv = w[:, :].rearrange("p (h c n) -> p h c n", h=2, c=HC)
                for a in halves:
                    if not (isinstance(t, int) and t == 0):
                        pe.wait_ge(s_ev, 2 * (t - 1) + a + 1)
                    n = 0
                    for wl, xl in TERMS:
                        for c in range(HC):
                            ins = mm(ps_y[a][:, 0:D], h_split[par][:, xl, c, a * P:(a + 1) * P], wv[:, wl, c, :],
                                     start=n == 0, stop=n == 3 * HC - 1)
                            n += 1
                    ins.then_inc(s_mm2, 1)

            pe.wait_ge(s_const, CONSTS)
            pe.wait_ge(s_bias_in, 32)
            nb = EXPERTS * HC + HC
            nc.tensor.transpose(bt_ps, b_rows[:, :], ident_f[0:nb, 0:nb]).then_inc(s_bt_tr, 1)
            tr1(0, 0)
            pe.wait_ge(s_wr, 3)
            pe.wait_ge(s_bt, 1)
            router(0, 0)
            pe.wait_ge(s_w0_lo, DC)
            up(0, 0, w_shared[0], (0, 1, 2))
            rank(0, 0)
            up(0, 0, w_shared[0], (3,))
            tr1(1, 1)
            router(1, 1)
            pe.wait_ge(s_wlo, 1)

            def body1(i, par):
                up(i, par, w_shared[0], (0, 1, 2))
                rank(i, par)
                up(i, par, w_shared[0], (3,))
                down(i - 1, 1 - par, w_shared[1], (0,))
                tr1(i + 1, 1 - par)
                down(i - 1, 1 - par, w_shared[1], (1,))
                router(i + 1, 1 - par)

            body1(1, 1)
            body1(2, 0)
            with pairs(pe, 3, SHARED - 1) as i:
                body1(i, 1)
                body1(i + 1, 0)
            up(SHARED - 1, 1, w_shared[0], (0, 1))
            rank(SHARED - 1, 1)
            up(SHARED - 1, 1, w_shared[0], (2, 3))
            pe.wait_ge(s_rb, SHARED * RB)
            mm(cn_ps, ones_h[:, :], mask_sum[:, :], start=True, stop=True).then_inc(s_count, 1)
            down(SHARED - 2, 0, w_shared[1])
            down(SHARED - 1, 1, w_shared[1])
            for m in range(KC // 2):
                pe.wait_ge(s_kv_lo, m // 2 + 1)
                if m:
                    pe.wait_ge(s_k_t, m)
                lo = 2 * (m % 2)
                transpose_rows(m, 0, k_split[m // 2][:, lo:lo + 2, :]).then_inc(s_k_tr, 1)
            pe.wait_ge(s_k_t, KC // 2)

            def up2(j, par):
                pe.wait_ge(s_wfc_in[par], nth(j, par))
                up(SHARED + j, par, w_fc[par])

            def down2(j, par):
                pe.wait_ge(s_wpj_in[par], nth(j, par))
                down(SHARED + j, par, w_pj[par])

            def body2(j, par):
                up2(j, par)
                tr2(j + 1, 1 - par)
                down2(j - 1, 1 - par)

            tr2(0, 0)
            up2(0, 0)
            tr2(1, 1)
            with pairs(pe, 1, ROUTED - 2) as j:
                body2(j, 1)
                body2(j + 1, 0)
            body2(ROUTED - 2, 1)
            up2(ROUTED - 1, 0)
            down2(ROUTED - 2, 1)

            def scores(u, par, mpar, loaded, first=False):
                if loaded is not None:
                    pe.wait_ge(s_q_in[mpar], loaded)
                if not first:
                    pe.wait_ge(s_mul, u - 1)
                for half in range(2):
                    n = 0
                    for kl, ql in TERMS:
                        for c in range(DC):
                            lo = par * KEYS + half * 512
                            ins = mm(ps_h[:, lo:lo + 512], q_t[mpar][:, ql * DC + c, par * P:(par + 1) * P],
                                     k_t[:, kl * DC + c, half * 512:(half + 1) * 512], start=n == 0, stop=n == 3 * DC - 1)
                            n += 1
                ins.then_inc(s_qk, 1)

            def transpose_probs(u, par, first=False):
                pe.wait_ge(s_exp, u + 1)
                for kk in range(2):
                    if not first:
                        pe.wait_ge(s_plo, 2 * (u - 1) + kk + 1)
                    for c in range(4 * kk, 4 * kk + 4):
                        ins = nc.tensor.transpose(ps_t[:, c * P:(c + 1) * P], prob[par][:, c * P:(c + 1) * P], ident_f[:, :])
                    ins.then_inc(s_pt, 1)

            def values(u, par, first=False):
                pe.wait_ge(s_plo, 2 * (u + 1))
                if first:
                    pe.wait_ge(s_ev, 2 * (SHARED + ROUTED - 1) + par + 1)
                else:
                    pe.wait_ge(s_fin, FIN * (u - 2) + 1)
                n = 0
                for vl, pl in TERMS:
                    for c in range(KC):
                        ins = mm(ps_y[par][:, 0:D], p_t[par][:, pl, c, :], v_split[:, vl, c, :],
                                 start=n == 0, stop=n == 3 * KC - 1)
                        n += 1
                ins.then_inc(s_pv, 1)

            def body3(u0, g8, first=False, last=False):
                for s in range(8):
                    u, par = u0 + s, s % 2
                    transpose_probs(u, par, first=first and s == 0)
                    if not (last and s >= 6):
                        n = s + 2
                        loaded = None
                        if n % 2 == 0:
                            loaded = g8 * 32 + (n // 4) * 16 + 16
                        scores(u + 2, par, (n // 2) % 2, loaded)
                    values(u, par, first=first and s < 2)

            for b in range(BANKS):
                pe.wait_ge(s_gelu, BANKS * (SHARED + ROUTED - 1) + b + 1)
            pe.wait_ge(s_kv_lo, 4)
            scores(0, 0, 0, 16, first=True)
            down2(ROUTED - 1, 0)
            scores(1, 1, 0, None, first=True)
            body3(0, 0, first=True)
            with pe.Fori(1, QT // 8 - 1) as g3:
                g = pe.snap(g3)
                body3(g * 8, g)
            body3(QT - 8, QT // 8 - 1, last=True)


_INS = ["L0_attn_q", "L0_attn_k", "L0_attn_v", "L0_ffn_Wfc_s", "L0_ffn_bfc_s", "L0_ffn_Wproj_s", "L0_ffn_bproj_s",
        "L0_ffn_Wr", "L0_ffn_Wfc", "L0_ffn_bfc", "L0_ffn_Wproj", "L0_ffn_bproj"]
_OUTS = [((8, 512, 256), "float32")]


def kernel(**inputs):
    import numpy as _np
    import concourse.bacc as _bacc
    from concourse import mybir as _mybir
    from concourse.bass_utils import run_bass_kernel_spmd as _run

    nc = _bacc.Bacc("TRN2", target_bir_lowering=False, num_devices=1)
    arrays, args = {}, []
    for name in _INS:
        a = _np.ascontiguousarray(inputs[name])
        arrays[f"in_{name}_dram"] = a
        args.append(nc.dram_tensor(f"in_{name}_dram", a.shape, _mybir.dt.from_np(a.dtype), kind="ExternalInput").ap())
    for n, (shape, dtype) in enumerate(_OUTS):
        dt = _mybir.dt.from_np(_np.dtype(dtype))
        args.append(nc.dram_tensor(f"out_{n}_dram", shape, dt, kind="ExternalOutput").ap())
    moe_attention_block(nc, *args)
    r = _run(nc, [arrays], core_ids=[0])
    return r.results[0]["out_0_dram"]
```

```python
from contextlib import ExitStack, contextmanager

import concourse.bass as bass
from concourse import mybir

TOKENS, D = 4096, 256
BATCH, QLEN, KEYS = 8, 512, 1024
HID, EXPERTS, TOP = 1024, 8, 2
P = 128
TILE = 256
SUB = TILE // P
DC = D // P
HC = HID // P
BANKS = 4
SHARED = TOKENS // TILE
BLK_SHIFT = 7
BLOCKS = (TOKENS * TOP + EXPERTS * (P - 1)) // P
FULLS = (BLOCKS - EXPERTS) // 2
HALVES = BLOCKS - 2 * FULLS
ROUTED = FULLS + HALVES
MIXED = 2 * HALVES
CAP = TOKENS + P
SPARE = EXPERTS * CAP
QT = TOKENS // P
KC = KEYS // P
KH = KC // 2
WS = 256.0
EPS = 1e-5
ROW = 2 * D


def is_half(j):
    return j < MIXED and j % 2 == 1


def moe_attention_block(nc, q, k, v, wfc_s, bfc_s, wproj_s, bproj_s, wr, wfc, bfc, wproj, bproj, out):
    f32, f16 = mybir.dt.float32, mybir.dt.float16
    i32, u32 = mybir.dt.int32, mybir.dt.uint32
    ALU = mybir.AluOpType
    ACT = mybir.ActivationFunctionType
    AX = mybir.AxisListType.X
    ds = bass.ds

    x_rows = q.rearrange("b s d -> (b s) d")
    out_rows = out.rearrange("b s d -> (b s) d")
    k_rows = k.rearrange("b s d -> (b s) d")
    v_rows = v.rearrange("b s d -> (b s) d")
    wfc_rows = wfc.rearrange("e c n -> (e c) n")
    wproj_rows = wproj.rearrange("e h n -> (e h) n")
    bfc_rows = bfc.rearrange("e (h p) -> (e h) p", p=P)
    bfc_s_rows = bfc_s.rearrange("(h p) -> h p", p=P)

    def dram(name, shape, dt):
        return nc.dram_tensor(name, shape, dt, kind="Internal").ap()

    slots_x = dram("slots_x", (SPARE + TILE, ROW), f16)
    slots_y = dram("slots_y", (BLOCKS * P, D), f32)
    shared_y = dram("shared_y", (TOKENS, D), f32)
    xt_d = dram("xt_d", (SHARED * P, 2 * DC * TILE), f16)
    key_scale = dram("key_scale", (SHARED, SUB * D), f32)
    wpack = dram("wpack", (EXPERTS * P, 4 * 2048), f16)
    bfct_d = dram("bfct_d", (P, EXPERTS * HC), f32)

    ctx = ExitStack()
    with ctx:
        def sb(name, shape, dt):
            return ctx.enter_context(nc.sbuf_tensor(name, shape, dt))

        def sem(name):
            return ctx.enter_context(nc.semaphore(name))

        def sem2(name):
            return [sem(name + "_even"), sem(name + "_odd")]

        def sb2(name, shape, dt):
            return [sb(name + str(n), shape, dt) for n in range(2)]

        ident_h = sb("ident_h", [P, P], f16)
        ident_f = sb("ident_f", [P, P], f32)
        before = sb("before", [P, P], f16)
        ones_h = sb("ones_h", [P, P], f16)
        iota_e = sb("iota_e", [P, EXPERTS], f32)
        region = sb("region", [P, EXPERTS], f32)
        step_no = sb("step_no", [1, ROUTED], f32)
        step_at = sb("step_at", [1, ROUTED], f32)
        neg_half = sb("neg_half", [P, SUB], f32)
        zeros = sb("zeros", [P, SUB, ROW], f16)
        one_row = sb("one_row", [P, EXPERTS], f32)
        x_in = sb2("x_in", [P, SUB, D], f32)
        stats = sb("stats", [P, SUB, 6], f32)
        mean_var = sb2("mean_var", [P, SUB, 2], f32)
        var_eps = sb2("var_eps", [P, SUB], f32)
        rstd = sb2("rstd", [P, SUB], f32)
        xn = sb2("xn", [P, SUB, D], f32)
        x_split = sb2("x_split", [P, SUB, ROW], f16)
        x_t = sb2("x_t", [P, 2 * DC, TILE], f16)
        wr32 = sb("wr32", [P, DC, EXPERTS], f32)
        wr_s = sb("wr_s", [P, DC, 2 * EXPERTS], f16)
        logits = sb("logits", [P, SUB, EXPERTS], f32)
        top_v = sb("top_v", [P, SUB, 8], f32)
        top_i = sb("top_i", [P, SUB, 8], u32)
        top_f = sb("top_f", [P, SUB, TOP], f32)
        chosen = sb("chosen", [P, SUB, TOP, EXPERTS], f32)
        mask = sb2("mask", [P, SUB, EXPERTS], f16)
        mask_sum = sb("mask_sum", [P, EXPERTS], f16)
        slot_of = sb("slot_of", [P, SUB, EXPERTS], f32)
        picked = sb("picked", [P, SUB, TOP, EXPERTS], f32)
        pos_f = sb("pos_f", [P, SUB * TOP], f32)
        pos_i = sb2("pos_i", [P, SUB * TOP], i32)
        pos_all = sb("pos_all", [P, QT * TOP], f32)
        exp_all = sb("exp_all", [P, QT * TOP], f32)
        match_e = sb("match_e", [P, QT * TOP, EXPERTS], f32)
        half_from = sb("half_from", [P, EXPERTS], f32)
        half_shift = sb("half_shift", [P, EXPERTS], f32)
        past_e = sb("past_e", [P, QT * TOP, EXPERTS], f32)
        shift_t = sb("shift_t", [P, QT * TOP], f32)
        y_row_all = sb("y_row_all", [P, QT * TOP], i32)
        gap_all = sb("gap_all", [P, QT], f32)
        w_stage = sb2("w_stage", [P, 2048], f32)
        w_split = sb2("w_split", [P, 4096], f16)
        w_shared = sb2("w_shared", [P, 4096], f16)
        w_fc = sb2("w_fc", [P, 4096], f16)
        w_pj = sb2("w_pj", [P, 4096], f16)
        b_rows = sb("b_rows", [EXPERTS * HC + HC, P], f32)
        b_t = sb("b_t", [P, EXPERTS * HC + HC], f32)
        b_fc = sb2("b_fc", [P, HC], f32)
        b_pj = sb2("b_pj", [P, D], f32)
        b_pj_s = sb("b_pj_s", [P, D], f32)
        h32 = sb("h32", [P, HC, TILE], f32)
        h_split = sb2("h_split", [P, 2, HC, TILE], f16)
        y_sb = sb2("y_sb", [P, SUB, D], f32)
        cnt = sb("cnt", [P, EXPERTS], f32)
        cnt_i = sb("cnt_i", [P, EXPERTS], i32)
        blk_i = sb("blk_i", [P, EXPERTS], i32)
        pair_i = sb("pair_i", [P, EXPERTS], i32)
        blk = sb("blk", [P, EXPERTS], f32)
        pair = sb("pair", [P, EXPERTS], f32)
        full = sb("full", [P, EXPERTS], f32)
        odd = sb("odd", [P, EXPERTS], f32)
        ends = sb("ends", [P, 2, EXPERTS + 1], f32)
        base = sb("base", [P, 2, EXPERTS], f32)
        base_up = sb("base_up", [P, 2, EXPERTS], f32)
        past = sb("past", [1, ROUTED, EXPERTS], f32)
        past_up = sb("past_up", [1, ROUTED, EXPERTS], f32)
        step_e = sb("step_e", [1, ROUTED], f32)
        step_b = sb("step_b", [1, ROUTED], f32)
        step_r = sb("step_r", [1, ROUTED], f32)
        tab_e = sb("tab_e", [1, ROUTED], i32)
        tab_x = sb("tab_x", [1, ROUTED], i32)
        tab_pad = sb("tab_pad", [1, EXPERTS], i32)
        k_t = sb("k_t", [P, 2 * DC, KEYS], f16)
        v_split = sb("v_split", [P, 2, KC, D], f16)
        q_t = sb2("q_t", [P, 2 * DC, TILE], f16)
        scale_b = sb2("scale_b", [P, KEYS], f32)
        prob = sb2("prob", [P, KEYS], f32)
        row_max = sb2("row_max", [P, 1], f32)
        neg_max = sb2("neg_max", [P, 1], f32)
        row_sum = sb2("row_sum", [P, 1], f32)
        inv_sum = sb2("inv_sum", [P, 1], f32)
        p_t = sb2("p_t", [P, 2, KC, P], f16)
        gap_exp = sb("gap_exp", [P, QT], f32)
        gap_den = sb("gap_den", [P, QT], f32)
        gates = sb("gates", [P, QT, TOP], f32)
        gate_u = sb2("gate_u", [P, TOP], f32)
        pos_u = sb2("pos_u", [P, TOP], i32)
        y_rows = sb2("y_rows", [P, TOP, D], f32)
        base_y = sb2("base_y", [P, D], f32)
        base_x = sb2("base_x", [P, D], f32)
        o_sb = sb2("o_sb", [P, D], f32)

        k_split = [t[:, :, :, :].rearrange("p h c n -> p (h c n)").rearrange("p (c n) -> p c n", c=KH) for t in p_t]

        ps_h = ctx.enter_context(nc.psum_tensor("ps_h", [P, BANKS * 512], f32))
        ps_y = [ctx.enter_context(nc.psum_tensor(f"ps_y{a}", [P, 512], f32)) for a in range(2)]
        ps_t = ctx.enter_context(nc.psum_tensor("ps_t", [P, 1024], f32))
        tr16 = ps_t[:, 0:512].bitcast(f16)
        key_banks = [ps_h[:, b * 512:(b + 1) * 512].bitcast(f16) for b in range(BANKS)]
        misc = ps_t[:, 512:1024]
        lg_ps = misc[:, 0:SUB * 2 * EXPERTS]
        rk_ps = misc[:, 32:32 + SUB * EXPERTS]
        cn_ps = misc[:, 48:48 + EXPERTS]
        bt_ps = misc[:, 128:128 + EXPERTS * HC + HC]

        s_const = sem("s_const")
        s_bias_in = sem("s_bias_in")
        s_wr_in = sem("s_wr_in")
        s_bpj_in = sem("s_bpj_in")
        s_x_in = sem2("s_x_in")
        s_row_out = sem2("s_row_out")
        s_xt_out = sem2("s_xt_out")
        s_w_in = sem2("s_w_in")
        s_w_out = sem2("s_w_out")
        s_bt_out = sem("s_bt_out")
        s_scat = sem2("s_scat")
        s_y_out = sem2("s_y_out")
        s_pad = sem("s_pad")
        s_xs_in = sem2("s_xs_in")
        s_wfc_in = sem2("s_wfc_in")
        s_bfc_in = sem2("s_bfc_in")
        s_wpj_in = sem2("s_wpj_in")
        s_bpjx_in = sem2("s_bpjx_in")
        s_kv_in = sem2("s_kv_in")
        s_q_in = sem2("s_q_in")
        s_sc_in = sem2("s_sc_in")
        s_by_in = sem2("s_by_in")
        s_bx_in = sem2("s_bx_in")
        s_gat = sem2("s_gat")
        s_out = sem2("s_out")
        s_iota = sem("s_iota")
        s_bt_tr = sem("s_bt_tr")
        s_bt = sem("s_bt")
        s_wr = sem("s_wr")
        s_w0_in = sem2("s_w0_in")
        s_w0_sc = sem("s_w0_sc")
        s_w0_hi = sem2("s_w0_hi")
        s_w0_lo = sem2("s_w0_lo")
        s_warm = sem("s_warm")
        s_wlast_in = sem("s_wlast_in")
        s_wlast_hi = sem("s_wlast_hi")
        s_wlast_lo = sem("s_wlast_lo")
        s_wlast_out = sem("s_wlast_out")
        s_lna = sem("s_lna")
        s_rstd = sem("s_rstd")
        s_lnb = sem("s_lnb")
        s_tr = sem("s_tr")
        s_xt = sem("s_xt")
        s_logit = sem("s_logit")
        s_ra = sem("s_ra")
        s_rank = sem("s_rank")
        s_rb = sem("s_rb")
        s_msum0 = sem("s_msum0")
        s_count = sem("s_count")
        s_table = sem("s_table")
        s_y_rows = sem("s_y_rows")
        s_wsc = sem("s_wsc")
        s_whi = sem("s_whi")
        s_wlo = sem("s_wlo")
        s_mm1 = sem("s_mm1")
        s_gelu = sem("s_gelu")
        s_hhi = sem("s_hhi")
        s_hlo = sem("s_hlo")
        s_mm2 = sem("s_mm2")
        s_ev = sem("s_ev")
        s_kv_hi = sem("s_kv_hi")
        s_kv_lo = sem("s_kv_lo")
        s_k_tr = sem("s_k_tr")
        s_k_t = sem("s_k_t")
        s_gexp = sem("s_gexp")
        s_gate = sem("s_gate")
        s_qk = sem("s_qk")
        s_mul = sem("s_mul")
        s_nm = sem("s_nm")
        s_exp = sem("s_exp")
        s_inv = sem("s_inv")
        s_pt = sem("s_pt")
        s_phi = sem("s_phi")
        s_plo = sem("s_plo")
        s_pv = sem("s_pv")
        s_meta = sem("s_meta")
        s_base = sem("s_base")
        s_gated = sem("s_gated")
        s_fin = sem("s_fin")

        LNA, LNB, RA, RB, TABLE, Y_ROWS = 5, 4, 10, 7, 32, 9
        CONSTS = 14
        PAD_ROWS, STEP_E = 2, TABLE - 7

        def chain(eng, s, start):
            at = [start]

            def settle():
                wait_ge(eng, s, at[0])

            def link(ins, wait=False):
                ins.then_inc(s, 1)
                at[0] = at[0] + 1
                if wait:
                    settle()
            return link, settle

        def wait_ge(eng, s, value):
            eng.wait_ge(s, value)
            eng.nop(nofuse=True)

        @contextmanager
        def pairs(eng, first, end):
            with eng.Fori(0, (end - first) // 2) as m:
                yield eng.snap(m * 2 + first)

        def nth(n, par, each=16):
            return (n - par) * (each // 2) + each

        def rows(ap, first, n):
            return ap[ds(first, n), :].rearrange("(a p) d -> p a d", p=P)

        def pad_experts(eng, experts):
            wait_ge(eng, s_table, PAD_ROWS)
            for e in experts:
                first_pad = eng.value_load(tab_pad[0:1, e:e + 1], min_val=0, max_val=SPARE - P)
                eng.dma_start(rows(slots_x, first_pad, P), zeros[:, 0:1, :]).then_inc(s_pad, 16)

        block = ctx.enter_context(nc.Block())

        @block.sync
        def _(sp):
            def load_x(i, par, first=False):
                if not first:
                    wait_ge(sp, s_lnb, (i - 1) * LNB)
                sp.dma_start(x_in[par][:, :, :], rows(x_rows, i * TILE, TILE)).then_inc(s_x_in[par], 16)

            def load_expert(i, par, fc):
                if isinstance(i, int) and i == 0:
                    for c in range(DC):
                        wait_ge(sp, s_w0_lo[c], 1)
                else:
                    wait_ge(sp, s_wlo, 2 * i)
                if fc:
                    src = wfc_rows[ds(i * D, D), :].rearrange("(c p) n -> p c n", p=P)
                else:
                    src = wproj_rows[ds((i - EXPERTS) * HID, HID), :].rearrange("(c p) n -> p c n", p=P)
                sp.dma_start(w_stage[par][:, :].rearrange("p (c n) -> p c n", c=DC if fc else HC), src
                             ).then_inc(s_w_in[par], 16)

            def store_w(i, par, fc):
                wait_ge(sp, s_wlo, 2 * (i + 2))
                if fc:
                    dst = wpack[ds(i * P, P), 0:4096]
                else:
                    dst = wpack[ds((i - EXPERTS) * P, P), 4096:8192]
                sp.dma_start(dst, w_split[par][:, :]).then_inc(s_w_out[par], 16)

            def store_row(i, par):
                wait_ge(sp, s_lnb, i * LNB + 2)
                sp.dma_start(key_scale[ds(i, 1), :], xn[par][0:1, :, :].rearrange("p a d -> p (a d)")
                             ).then_inc(s_row_out[par], 16)

            def store_xt(i, par):
                wait_ge(sp, s_xt, i + 1)
                sp.dma_start(xt_d[ds(i * P, P), :], x_t[par][:, :, :].rearrange("p c n -> p (c n)")
                             ).then_inc(s_xt_out[par], 16)

            def store_shared(i, par):
                wait_ge(sp, s_ev, 2 * i + 2)
                sp.dma_start(rows(shared_y, i * TILE, TILE), y_sb[par][:, :, :]).then_inc(s_y_out[par], 16)

            load_x(0, 0, first=True)
            for c in range(DC):
                sp.dma_start(w_stage[0][:, c * HID:(c + 1) * HID], wfc_s[c * P:(c + 1) * P, :]).then_inc(s_w0_in[c], 16)
            sp.dma_start(wr32[:, :, :], wr.rearrange("(c p) e -> p c e", p=P)).then_inc(s_wr_in, 16)
            sp.dma_start(b_rows[0:EXPERTS * HC, :], bfc_rows).then_inc(s_bias_in, 16)
            sp.dma_start(b_rows[EXPERTS * HC:, :], bfc_s_rows).then_inc(s_bias_in, 16)
            load_x(1, 1, first=True)
            sp.dma_start(w_stage[1][:, :].rearrange("p (c n) -> p c n", c=HC),
                         wproj_s.rearrange("(c p) n -> p c n", p=P)).then_inc(s_w_in[1], 16)
            sp.dma_start(b_pj_s[:, :], bproj_s.partition_broadcast(P)).then_inc(s_bpj_in, 16)
            wait_ge(sp, s_const, CONSTS)
            sp.dma_start(rows(slots_x, SPARE, TILE), zeros[:, :, :]).then_inc(s_pad, 16)
            store_row(0, 0)
            store_xt(0, 0)
            load_x(2, 0)
            load_expert(0, 0, True)
            for n in range(2):
                sp.dma_start(prob[n][:, :].rearrange("p (c n) -> p c n", c=KH), rows(k_rows, n * KH * P, KH * P)
                             ).then_inc(s_kv_in[0], 16)
            store_row(1, 1)
            wait_ge(sp, s_bt, 1)
            sp.dma_start(bfct_d, b_t[:, 0:EXPERTS * HC]).then_inc(s_bt_out, 16)
            store_xt(1, 1)
            load_expert(1, 1, True)

            def body1(i, par, next_fc, done_fc, last=False, last_half=False):
                if not last:
                    load_x(i + 2, par)
                store_row(i + 1, 1 - par)
                if last_half:
                    for n in range(2):
                        sp.dma_start(scale_b[n][:, :].rearrange("p (c n) -> p c n", c=HC // 2),
                                     rows(wproj_rows, EXPERTS * HID - (2 - n) * (HID // 2), HID // 2)
                                     ).then_inc(s_wlast_in, 16)
                if not last:
                    load_expert(i + 1, 1 - par, next_fc)
                store_w(i - 1, 1 - par, done_fc)
                store_xt(i + 1, 1 - par)
                store_shared(i - 1, 1 - par)

            body1(1, 1, True, True, last_half=True)
            body1(2, 0, True, True)
            with pairs(sp, 3, EXPERTS - 1) as i:
                body1(i, 1, True, True)
                body1(i + 1, 0, True, True)
            body1(EXPERTS - 1, 1, False, True)
            body1(EXPERTS, 0, False, True)
            with pairs(sp, EXPERTS + 1, SHARED - 3) as i:
                body1(i, 1, False, False)
                body1(i + 1, 0, False, False)
            body1(SHARED - 3, 1, False, False)
            wait_ge(sp, s_wlast_lo, 2)
            sp.dma_start(wpack[(EXPERTS - 1) * P:, 4096:8192], w_pj[1][:, :]).then_inc(s_wlast_out, 16)
            body1(SHARED - 2, 0, False, False, last=True)
            pad_experts(sp, range(EXPERTS // 2))
            wait_ge(sp, s_w_out[0], 8 * EXPERTS)
            wait_ge(sp, s_w_out[1], 8 * EXPERTS)
            wait_ge(sp, s_bt_out, 16)
            wait_ge(sp, s_table, STEP_E)

            def expert_of(j):
                return sp.value_load(tab_e[0:1, ds(j, 1)], min_val=0, max_val=EXPERTS - 1)

            def load_weights(j, e, dst, first_col, loaded, always):
                def load():
                    sp.dma_start(dst[:, :], wpack[ds(e * P, P), first_col:first_col + 4096]).then_inc(loaded, 16)
                if always:
                    load()
                else:
                    before = expert_of(j - 2)
                    with sp.If(e != before):
                        load()
                    with sp.Else():
                        sp.sem_inc(loaded, 16)

            def load_fc(j, par, first=False):
                if not first:
                    wait_ge(sp, s_mm1, BANKS * (SHARED + j - 1))
                e = expert_of(j)
                load_weights(j, e, w_fc[par], 0, s_wfc_in[par], first)
                if not first:
                    wait_ge(sp, s_gelu, BANKS * (SHARED + j - 1))
                sp.dma_start(b_fc[par][:, :], bfct_d[:, ds(e * HC, HC)]).then_inc(s_bfc_in[par], 16)

            def load_pj(j, par, first=False):
                if not first:
                    wait_ge(sp, s_mm2, 2 * (SHARED + j - 1))
                e = expert_of(j)
                load_weights(j, e, w_pj[par], 4096, s_wpj_in[par], first)
                if not first:
                    wait_ge(sp, s_ev, 2 * (SHARED + j - 1))
                sp.dma_start(b_pj[par][:, :], bproj[ds(e, 1), :].rearrange("e n -> (e n)").partition_broadcast(P)
                             ).then_inc(s_bpjx_in[par], 16)

            def load_slots(j, par, half):
                wait_ge(sp, s_tr, SHARED + j - 1)
                r = sp.value_load(tab_x[0:1, ds(j, 1)], min_val=0, max_val=SPARE)
                if half:
                    src, dst = rows(slots_x, r, P), x_split[par][:, 0:1, :]
                else:
                    src, dst = rows(slots_x, r, TILE), x_split[par][:, :, :]
                sp.dma_start(dst, src).then_inc(s_xs_in[par], 16)

            def store_slots(j, par, half, mixed):
                wait_ge(sp, s_ev, 2 * (SHARED + j) + 2)
                if half:
                    dst, src = rows(slots_y, (j - 1) * (P // 2) + FULLS * TILE, P), y_sb[par][:, 0:1, :]
                elif mixed:
                    dst, src = rows(slots_y, j * (TILE // 2), TILE), y_sb[par][:, :, :]
                else:
                    dst, src = rows(slots_y, (j - HALVES) * TILE, TILE), y_sb[par][:, :, :]
                sp.dma_start(dst, src).then_inc(s_y_out[par], 16)

            load_fc(0, 0, first=True)
            wait_ge(sp, s_table, TABLE)
            wait_ge(sp, s_scat[0], 32 * SHARED)
            wait_ge(sp, s_scat[1], 32 * SHARED)
            wait_ge(sp, s_pad, 16 * (EXPERTS + 1))
            load_slots(0, 0, False)
            load_slots(1, 1, True)
            store_w(SHARED - 2, 0, False)
            load_fc(1, 1, first=True)
            load_slots(2, 0, is_half(2))
            wait_ge(sp, s_w_out[0], 8 * SHARED)
            wait_ge(sp, s_w_out[1], 8 * SHARED - 16)
            wait_ge(sp, s_wlast_out, 16)
            load_pj(0, 0, first=True)
            store_shared(SHARED - 2, 0)
            store_shared(SHARED - 1, 1)

            def body2(j, par, slots=None, out=None, last=False):
                if not last:
                    load_fc(j + 1, 1 - par)
                if slots is not None:
                    load_slots(j + 2, par, *slots)
                load_pj(j, par, first=isinstance(j, int) and j == 1)
                if out is not None:
                    store_slots(j - 2, par, *out)

            body2(1, 1, slots=(is_half(3),))
            body2(2, 0, slots=(is_half(4),), out=(is_half(0), True))
            with pairs(sp, 3, MIXED - 3) as j:
                body2(j, 1, slots=(True,), out=(True, True))
                body2(j + 1, 0, slots=(False,), out=(False, True))
            for n in range(2):
                sp.dma_start(scale_b[n][:, :].rearrange("p (c n) -> p c n", c=KH), rows(v_rows, n * KH * P, KH * P)
                             ).then_inc(s_kv_in[1], 16)
            for j in range(MIXED - 3, MIXED + 2):
                body2(j, j % 2, slots=(is_half(j + 2),), out=(is_half(j - 2), j - 2 < MIXED))
            with pairs(sp, MIXED + 2, ROUTED - 2) as j:
                body2(j, 0, slots=(False,), out=(False, False))
                body2(j + 1, 1, slots=(False,), out=(False, False))
            body2(ROUTED - 2, 0, out=(False, False))
            body2(ROUTED - 1, 1, out=(False, False), last=True)

            def load_q(m, par, first=False):
                if not first:
                    wait_ge(sp, s_qk, 2 * m - 2)
                sp.dma_start(q_t[par][:, :, :].rearrange("p c n -> p (c n)"), xt_d[ds(m * P, P), :]
                             ).then_inc(s_q_in[par], 16)

            def load_scale(b, par, first=False):
                if not first:
                    wait_ge(sp, s_mul, 4 * (b - 1))
                src = key_scale[ds(b * 2, 2), :].rearrange("r n -> (r n)")
                sp.dma_start(scale_b[par][:, :], src.partition_broadcast(P)).then_inc(s_sc_in[par], 16)

            def load_base(u, par, first=False):
                if not first:
                    wait_ge(sp, s_base, u - 1)
                sp.dma_start(base_y[par][:, :], shared_y[ds(u * P, P), :]).then_inc(s_by_in[par], 16)
                if not first:
                    wait_ge(sp, s_gated, 2 * u - 3)
                sp.dma_start(base_x[par][:, :], x_rows[ds(u * P, P), :]).then_inc(s_bx_in[par], 16)

            def store_out(u, par):
                wait_ge(sp, s_fin, u + 1)
                sp.dma_start(out_rows[ds(u * P, P), :], o_sb[par][:, :]).then_inc(s_out[par], 16)

            for par in range(2):
                wait_ge(sp, s_xt_out[par], 8 * SHARED)
                wait_ge(sp, s_row_out[par], 8 * SHARED)
                wait_ge(sp, s_y_out[par], 8 * SHARED)
            wait_ge(sp, s_kv_lo, 4)
            load_q(0, 0, first=True)
            load_scale(0, 0, first=True)
            store_slots(ROUTED - 2, 0, False, False)
            load_q(1, 1, first=True)
            load_base(0, 0, first=True)
            store_slots(ROUTED - 1, 1, False, False)
            load_base(1, 1, first=True)
            load_scale(1, 1, first=True)

            def body3(u0, first=False, last=False):
                for s in range(8):
                    u = u0 + s
                    if s % 2 == 1 and not (last and s > 3):
                        m = u0 // 2 if isinstance(u0, int) else None
                        pair = (m if m is not None else half(u0)) + s // 2 + 2
                        load_q(pair, (s // 2) % 2)
                    if s == 2 and not last:
                        load_scale(quarter(u0) + 2, 0)
                    if s == 6 and not last:
                        load_scale(quarter(u0) + 3, 1)
                    if not (first and s == 0):
                        store_out(u - 1, (s + 1) % 2)
                    if not (first and s == 0) and not (last and s == 7):
                        load_base(u + 1, (s + 1) % 2)

            def half(u0):
                return u0 // 2 if isinstance(u0, int) else g8 * 4

            def quarter(u0):
                return u0 // 4 if isinstance(u0, int) else g8 * 2

            body3(0, first=True)
            with sp.Fori(1, QT // 8 - 1) as g:
                g8 = sp.snap(g)
                body3(g8 * 8)
            body3(QT - 8, last=True)
            store_out(QT - 1, 1)
            wait_ge(sp, s_out[0], 8 * QT)
            wait_ge(sp, s_out[1], 8 * QT)

        @block.gpsimd
        def _(pool):
            g = nc.gpsimd
            g.memset(ident_h[:, :], 0.0).then_inc(s_iota, 1)
            g.memset(ident_f[:, :], 0.0).then_inc(s_iota, 1)
            g.memset(before[:, :], 1.0).then_inc(s_iota, 1)
            wait_ge(pool, s_iota, 3)
            for t in (ident_h, ident_f):
                g.affine_select(out=t[:, :], in_=t[:, :], compare_op=ALU.not_equal, fill=1.0, base=0,
                                pattern=[[-1, P]], channel_multiplier=1).then_inc(s_const, 1)
            g.affine_select(out=before[:, :], in_=before[:, :], compare_op=ALU.is_gt, fill=0.0, base=0,
                            pattern=[[1, P]], channel_multiplier=-1).then_inc(s_const, 1)
            g.memset(ones_h[:, :], 1.0).then_inc(s_const, 1)
            g.iota(iota_e[:, :], pattern=[[1, EXPERTS]], base=0, channel_multiplier=0,
                   allow_small_or_imprecise_dtypes=True).then_inc(s_const, 1)
            g.iota(region[:, :], pattern=[[CAP, EXPERTS]], base=0, channel_multiplier=0,
                   allow_small_or_imprecise_dtypes=True).then_inc(s_const, 1)
            for t, full_each, half_each in ((step_no, 1, 1), (step_at, TILE, P)):
                g.iota(t[:, 0:FULLS], pattern=[[full_each, FULLS]], base=0, channel_multiplier=0,
                       allow_small_or_imprecise_dtypes=True).then_inc(s_const, 1)
                g.iota(t[:, FULLS:], pattern=[[half_each, HALVES]], base=0, channel_multiplier=0,
                       allow_small_or_imprecise_dtypes=True).then_inc(s_const, 1)
            g.memset(neg_half[:, :], -0.5).then_inc(s_const, 1)
            g.memset(zeros[:, :, :], 0.0).then_inc(s_const, 1)
            g.memset(one_row[:, :], 1.0).then_inc(s_const, 1)
            g.memset(ends[:, :, :], 0.0).then_inc(s_const, 1)
            wait_ge(pool, s_const, CONSTS)

            def inv_std(i, par):
                wait_ge(pool, s_lna, (i + 1) * LNA)
                g.tensor_tensor(rstd[par][:, :], var_eps[par][:, :], neg_half[:, :], ALU.pow).then_inc(s_rstd, 1)

            def split_w_lo(n, par, dst, piece):
                if piece == 0:
                    wait_ge(pool, s_whi, n)
                at = piece * 1024
                g.tensor_tensor(dst[:, 2048 + at:3072 + at], w_stage[par][:, at:at + 1024], dst[:, at:at + 1024],
                                ALU.subtract).then_inc(s_wlo, 1)

            def scatter(i, par):
                wait_ge(pool, s_rb, i * RB + 6)
                for a in range(SUB):
                    for kk in range(TOP):
                        c = a * TOP + kk
                        g.indirect_dma_start(slots_x, bass.IndirectOffsetOnAxis(ap=pos_i[par][:, c:c + 1], axis=0),
                                             x_split[par][:, a, :], None).then_inc(s_scat[par], 16)

            def body1(i, par):
                inv_std(i + 1, 1 - par)
                split_w_lo(i + 1, 1 - par, w_split[1 - par], 0)
                scatter(i, par)
                split_w_lo(i + 1, 1 - par, w_split[1 - par], 1)

            inv_std(0, 0)
            wait_ge(pool, s_w0_hi[1], 1)
            g.tensor_tensor(w_shared[0][:, 2048 + HID:], w_stage[0][:, HID:], w_shared[0][:, HID:2 * HID],
                            ALU.subtract).then_inc(s_w0_lo[1], 1)
            inv_std(1, 1)
            split_w_lo(1, 1, w_shared[1], 0)
            split_w_lo(1, 1, w_shared[1], 1)
            scatter(0, 0)
            with pairs(pool, 1, SHARED - 1) as i:
                body1(i, 1)
                body1(i + 1, 0)
            split_w_lo(SHARED, 0, w_split[0], 0)
            split_w_lo(SHARED, 0, w_split[0], 1)
            scatter(SHARED - 1, 1)

            def gather(u, par, first=False):
                if not first:
                    wait_ge(pool, s_gated, 2 * u - 2)
                g.tensor_copy(pos_u[par][:, :], y_row_all[:, ds(u * TOP, TOP)]).then_inc(s_meta, 1)
                g.tensor_copy(gate_u[par][:, :], gates[:, ds(u, 1), :].rearrange("p o k -> p (o k)")).then_inc(s_meta, 1)
                wait_ge(pool, s_meta, 2 * u + 1)
                for kk in range(TOP):
                    g.indirect_dma_start(y_rows[par][:, kk, :], None, slots_y,
                                         bass.IndirectOffsetOnAxis(ap=pos_u[par][:, kk:kk + 1], axis=0)
                                         ).then_inc(s_gat[par], 16)

            def add_base(u, par):
                wait_ge(pool, s_by_in[par], nth(u, par))
                wait_ge(pool, s_bx_in[par], nth(u, par))
                g.tensor_tensor(base_x[par][:, :], base_x[par][:, :], base_y[par][:, :], ALU.add).then_inc(s_base, 1)

            wait_ge(pool, s_gate, 3)
            wait_ge(pool, s_y_rows, Y_ROWS)
            for par in range(2):
                wait_ge(pool, s_y_out[par], 16 * ((SHARED + ROUTED + 1 - par) // 2))
            gather(0, 0, first=True)
            add_base(0, 0)
            gather(1, 1, first=True)
            add_base(1, 1)
            with pairs(pool, 2, QT) as u:
                gather(u, 0)
                add_base(u, 0)
                gather(u + 1, 1)
                add_base(u + 1, 1)

        @block.scalar
        def _(act):
            def split_w_hi(n, par, dst, stored):
                act.wait_ge(s_w_in[par], nth(n, par) - (16 if par == 0 else 0))
                nc.scalar.mul(w_stage[par][:, :], w_stage[par][:, :], WS).then_inc(s_wsc, 1)
                act.wait_ge(s_wsc, n)
                if stored is not None:
                    act.wait_ge(s_w_out[par], stored)
                nc.scalar.copy(dst[:, 0:2048], w_stage[par][:, :]).then_inc(s_whi, 1)

            def gelu(t, par, bias, first=False, n=TILE):
                for b in range(BANKS):
                    act.wait_ge(s_mm1, BANKS * t + b + 1)
                    if not first:
                        act.wait_ge(s_hlo, BANKS * (t - 1) + b + 1)
                    for half in range(2):
                        hc = 2 * b + half
                        ins = nc.scalar.activation(h32[:, hc, 0:n], ps_h[:, hc * TILE:hc * TILE + n],
                                                   ACT.Gelu_apprx_tanh, bias=bias[:, hc:hc + 1], scale=1.0 / WS)
                    ins.then_inc(s_gelu, 1)
                    if b == 0 and not (isinstance(t, int) and t < 2):
                        act.wait_ge(s_mm2, 2 * (t - 1))
                    act.wait_ge(s_gelu, BANKS * t + b + 1)
                    nc.scalar.copy(h_split[par][:, 0, 2 * b:2 * b + 2, 0:n], h32[:, 2 * b:2 * b + 2, 0:n]).then_inc(s_hhi, 1)

            b_s = b_t[:, EXPERTS * HC:EXPERTS * HC + HC]
            act.wait_ge(s_const, CONSTS)
            nc.scalar.activation(gap_exp[:, 0:SUB], neg_half[:, :], ACT.Gelu_apprx_tanh).then_inc(s_warm, 1)
            act.wait_ge(s_w0_in[0], 16)
            nc.scalar.mul(w_shared[0][:, 0:HID], w_stage[0][:, 0:HID], WS).then_inc(s_w0_hi[0], 1)
            act.wait_ge(s_w0_in[1], 16)
            nc.scalar.mul(w_stage[0][:, HID:], w_stage[0][:, HID:], WS).then_inc(s_w0_sc, 1)
            act.wait_ge(s_w0_sc, 1)
            nc.scalar.copy(w_shared[0][:, HID:2 * HID], w_stage[0][:, HID:]).then_inc(s_w0_hi[1], 1)
            split_w_hi(1, 1, w_shared[1], None)
            act.wait_ge(s_bt, 1)
            gelu(0, 0, b_s, first=True)
            split_w_hi(2, 0, w_split[0], None)
            gelu(1, 1, b_s)
            split_w_hi(3, 1, w_split[1], None)
            act.wait_ge(s_kv_in[0], 32)
            for h in range(2):
                nc.scalar.copy(k_split[h][:, :, 0:D], prob[h][:, :].rearrange("p (c n) -> p c n", c=KH)).then_inc(s_kv_hi, 1)
            act.wait_ge(s_wlast_in, 32)
            for n in range(2):
                nc.scalar.mul(w_pj[1][:, n * KEYS:(n + 1) * KEYS], scale_b[n][:, :], WS).then_inc(s_wlast_hi, 1)
            with pairs(act, 2, SHARED - 2) as i:
                gelu(i, 0, b_s)
                split_w_hi(i + 2, 0, w_split[0], i * 8)
                gelu(i + 1, 1, b_s)
                split_w_hi(i + 3, 1, w_split[1], i * 8)
            gelu(SHARED - 2, 0, b_s)
            split_w_hi(SHARED, 0, w_split[0], (SHARED - 2) * 8)
            gelu(SHARED - 1, 1, b_s)
            pad_experts(act, range(EXPERTS // 2, EXPERTS))

            def step2(j, par, half=False):
                act.wait_ge(s_bfc_in[par], nth(j, par))
                gelu(SHARED + j, par, b_fc[par], n=P if half else TILE)

            step2(0, 0)
            with pairs(act, 1, MIXED + 1) as j:
                step2(j, 1, half=True)
                step2(j + 1, 0)
            act.wait_ge(s_kv_in[1], 32)
            for h in range(2):
                nc.scalar.copy(v_split[:, 0, h * KH:(h + 1) * KH, :], scale_b[h][:, :].rearrange("p (c n) -> p c n", c=KH)
                               ).then_inc(s_kv_hi, 1)
            with pairs(act, MIXED + 1, ROUTED - 1) as j:
                step2(j, 1)
                step2(j + 1, 0)
            step2(ROUTED - 1, 1)

            act.wait_ge(s_warm, 1)
            nc.scalar.activation(gap_exp[:, :], gap_all[:, :], ACT.Exp, scale=1.0 / WS).then_inc(s_gexp, 1)

            def exp(u, par, first=False):
                act.wait_ge(s_nm, u + 1)
                if not first:
                    act.wait_ge(s_inv, u - 1)
                nc.scalar.activation(prob[par][:, :], prob[par][:, :], ACT.Exp, bias=neg_max[par][:, 0:1],
                                     accum_out=row_sum[par][:, 0:1]).then_inc(s_exp, 1)

            def p_hi(u, par, first=False):
                for kk in range(2):
                    act.wait_ge(s_pt, 2 * u + kk + 1)
                    if kk == 0 and not first:
                        act.wait_ge(s_pv, u - 1)
                    nc.scalar.copy(p_t[par][:, 0, 4 * kk:4 * kk + 4, :],
                                   ps_t[:, kk * 512:(kk + 1) * 512].rearrange("p (c n) -> p c n", n=P)).then_inc(s_phi, 1)

            exp(0, 0, first=True)
            p_hi(0, 0, first=True)
            exp(1, 1, first=True)
            exp(2, 0)
            p_hi(1, 1, first=True)
            exp(3, 1)
            with pairs(act, 2, QT - 2) as u:
                p_hi(u, 0)
                exp(u + 2, 0)
                p_hi(u + 1, 1)
                exp(u + 3, 1)
            p_hi(QT - 2, 0)
            p_hi(QT - 1, 1)

        @block.vector
        def _(dve):
            ve = nc.vector

            def copy_xt(t, par, stored=None, n=TILE):
                dve.wait_ge(s_tr, t + 1)
                if not (isinstance(t, int) and t < 2):
                    dve.wait_ge(s_mm1, BANKS * (t - 1))
                if stored is not None:
                    dve.wait_ge(s_xt_out[par], stored)
                ve.tensor_copy(x_t[par][:, :, 0:n], tr16[:, :].rearrange("p (c n) -> p c n", n=TILE)[:, :, 0:n]).then_inc(s_xt, 1)

            def front_a(stat=None, route=None):
                if stat is not None:
                    i, par = stat
                    lna, lna_settle = chain(dve, s_lna, i * LNA)
                    dve.wait_ge(s_x_in[par], nth(i, par))
                    dve.nop(nofuse=True)
                    lna(ve.bn_stats(stats[:, 0, :], x_in[par][:, 0, :]))
                if route is not None:
                    r, rpar = route
                    ra, ra_settle = chain(dve, s_ra, r * RA)
                    dve.wait_ge(s_logit, r + 1)
                    ra(ve.tensor_reduce(logits[:, :, :], lg_ps.rearrange("p (a h e) -> p a e h", a=SUB, h=2), AX, ALU.add))
                if stat is not None:
                    lna(ve.bn_stats(stats[:, 1, :], x_in[par][:, 1, :]))
                if route is not None:
                    ra_settle()
                    for a in range(SUB):
                        ra(ve.max(top_v[:, a, :], logits[:, a, :]))
                    ra_settle()
                    for a in range(SUB):
                        ra(ve.max_index(top_i[:, a, :], top_v[:, a, :], logits[:, a, :]))
                if stat is not None:
                    lna_settle()
                    for a in range(SUB):
                        lna(ve.bn_aggr(mean_var[par][:, a, :], stats[:, a, :]))
                if route is not None:
                    ra_settle()
                    ra(ve.tensor_copy(top_f[:, :, :], top_i[:, :, 0:TOP]))
                if stat is not None:
                    lna_settle()
                    lna(ve.tensor_scalar(var_eps[par][:, :], mean_var[par][:, :, 1], EPS, None, ALU.add))
                if route is not None:
                    ra_settle()
                    top_flat = top_f[:, :, :].rearrange("p a k -> p (a k)")
                    ra(ve.tensor_tensor(chosen[:, :, :, :].rearrange("p a k e -> p (a k) e"),
                                        top_flat.unsqueeze(2).to_broadcast([P, SUB * TOP, EXPERTS]),
                                        iota_e[:, :].unsqueeze(1).to_broadcast([P, SUB * TOP, EXPERTS]), ALU.is_equal))
                    ra(ve.tensor_copy(exp_all[:, ds(r * SUB * TOP, SUB * TOP)], top_flat))
                    ra(ve.tensor_tensor(gap_all[:, ds(r * SUB, SUB)], top_v[:, :, 1], top_v[:, :, 0], ALU.subtract))
                    ra_settle()
                    ra(ve.tensor_tensor(mask[rpar][:, :, :], chosen[:, :, 0, :], chosen[:, :, 1, :], ALU.add))

            def front_b(norm=None, route=None):
                if norm is not None:
                    i, par = norm
                    lnb, lnb_settle = chain(dve, s_lnb, i * LNB)
                    dve.wait_ge(s_rstd, i + 1)
                    if not (isinstance(i, int) and i < 2):
                        dve.wait_ge(s_row_out[par], (i - par) * 8)
                        dve.wait_ge(s_scat[par], (i - par) * 32)
                        dve.wait_ge(s_tr, i - 1)
                    for a in range(SUB):
                        lnb(ve.tensor_scalar(xn[par][:, a, :], x_in[par][:, a, :], mean_var[par][:, a, 0:1],
                                             rstd[par][:, a:a + 1], ALU.subtract, ALU.mult))
                    lnb_settle()
                    lnb(ve.tensor_copy(x_split[par][:, :, 0:D], xn[par][:, :, :]))
                if route is not None:
                    r, rpar = route
                    rb, rb_settle = chain(dve, s_rb, r * RB)
                    dve.wait_ge(s_rank, r + 1)
                    if not (isinstance(r, int) and r < 2):
                        dve.wait_ge(s_scat[rpar], (r - rpar) * 32)
                    rb(ve.tensor_tensor(mask_sum[:, :], mask_sum[:, :], mask[rpar][:, 0, :], ALU.add))
                    rb(ve.tensor_tensor(slot_of[:, :, :], rk_ps.rearrange("p (a e) -> p a e", a=SUB),
                                        region[:, :].unsqueeze(1).to_broadcast([P, SUB, EXPERTS]), ALU.add))
                if norm is not None:
                    lnb_settle()
                    lnb(ve.tensor_tensor(x_split[par][:, :, D:ROW], xn[par][:, :, :], x_split[par][:, :, 0:D],
                                         ALU.subtract))
                if route is not None:
                    rb_settle()
                    rb(ve.tensor_tensor(mask_sum[:, :], mask_sum[:, :], mask[rpar][:, 1, :], ALU.add))
                    rb(ve.tensor_tensor(picked[:, :, :, :], chosen[:, :, :, :],
                                        slot_of[:, :, :].unsqueeze(2).to_broadcast([P, SUB, TOP, EXPERTS]), ALU.mult))
                    rb_settle()
                    rb(ve.tensor_reduce(pos_f[:, :], picked[:, :, :, :].rearrange("p a k e -> p (a k) e"), AX, ALU.add))
                    rb_settle()
                    rb(ve.tensor_copy(pos_i[rpar][:, :], pos_f[:, :]))
                    rb(ve.tensor_copy(pos_all[:, ds(r * SUB * TOP, SUB * TOP)], pos_f[:, :]))

            def split_h(t, par, n=TILE, banks=range(BANKS)):
                for b in banks:
                    dve.wait_ge(s_hhi, BANKS * t + b + 1)
                    ve.tensor_tensor(h_split[par][:, 1, 2 * b:2 * b + 2, 0:n], h32[:, 2 * b:2 * b + 2, 0:n],
                                     h_split[par][:, 0, 2 * b:2 * b + 2, 0:n], ALU.subtract).then_inc(s_hlo, 1)

            def evict(t, par, bias, subs=SUB, part=None):
                if not (isinstance(t, int) and t < 2):
                    dve.wait_ge(s_y_out[par], (t - par) * 8)
                for a in range(subs) if part is None else (part,):
                    dve.wait_ge(s_mm2, 2 * t + a + 3 - subs)
                    ve.scalar_tensor_tensor(out=y_sb[par][:, a, :], in0=ps_y[a][:, 0:D], scalar=1.0 / WS,
                                            in1=bias[:, :], op0=ALU.mult, op1=ALU.add).then_inc(s_ev, SUB // subs)

            front_a(stat=(0, 0))
            front_b(norm=(0, 0))
            dve.wait_ge(s_w0_hi[0], 1)
            ve.scalar_tensor_tensor(out=w_shared[0][:, 2048:2048 + HID], in0=w_stage[0][:, 0:HID], scalar=WS,
                                    in1=w_shared[0][:, 0:HID], op0=ALU.mult, op1=ALU.subtract).then_inc(s_w0_lo[0], 1)
            copy_xt(0, 0)
            dve.wait_ge(s_wr_in, 16)
            link, _ = chain(dve, s_wr, 0)
            link(ve.tensor_scalar(wr32[:, :, :], wr32[:, :, :], WS, None, ALU.mult), wait=True)
            link(ve.tensor_copy(wr_s[:, :, 0:EXPERTS], wr32[:, :, :]), wait=True)
            link(ve.tensor_tensor(wr_s[:, :, EXPERTS:], wr32[:, :, :], wr_s[:, :, 0:EXPERTS], ALU.subtract))
            ve.memset(mask_sum[:, :], 0.0).then_inc(s_msum0, 1)
            dve.wait_ge(s_bt_tr, 1)
            ve.tensor_copy(b_t[:, :], bt_ps).then_inc(s_bt, 1)
            dve.wait_ge(s_const, CONSTS)
            dve.wait_ge(s_msum0, 1)
            front_a(stat=(1, 1), route=(0, 0))
            front_b(norm=(1, 1), route=(0, 0))
            copy_xt(1, 1)
            split_h(0, 0)
            dve.wait_ge(s_bpj_in, 16)

            def body1(i, par):
                front_a(stat=(i + 1, 1 - par), route=(i, par))
                front_b(norm=(i + 1, 1 - par), route=(i, par))
                split_h(i, par, banks=(0, 1))
                copy_xt(i + 1, 1 - par, stored=(i + 1 - (1 - par)) * 8)
                split_h(i, par, banks=(2, 3))
                evict(i - 1, 1 - par, b_pj_s)

            def split_key_lo(h):
                dve.wait_ge(s_kv_hi, 1 + h)
                ve.tensor_tensor(k_split[h][:, :, D:ROW], prob[h][:, :].rearrange("p (c n) -> p c n", c=KH),
                                 k_split[h][:, :, 0:D], ALU.subtract).then_inc(s_kv_lo, 1)

            body1(1, 1)
            split_key_lo(0)
            body1(2, 0)
            split_key_lo(1)
            def split_last_lo(n):
                dve.wait_ge(s_wlast_hi, n + 1)
                ve.scalar_tensor_tensor(out=w_pj[1][:, 2048 + n * KEYS:2048 + (n + 1) * KEYS], in0=scale_b[n][:, :], scalar=WS,
                                        in1=w_pj[1][:, n * KEYS:(n + 1) * KEYS],
                                        op0=ALU.mult, op1=ALU.subtract).then_inc(s_wlast_lo, 1)

            body1(3, 1)
            split_last_lo(0)
            body1(4, 0)
            split_last_lo(1)
            with pairs(dve, 5, SHARED - 1) as i:
                body1(i, 1)
                body1(i + 1, 0)
            front_a(route=(SHARED - 1, 1))
            front_b(route=(SHARED - 1, 1))

            dve.wait_ge(s_count, 1)
            link, settle = chain(dve, s_table, 0)
            link(ve.tensor_copy(cnt[:, :], cn_ps), wait=True)
            link(ve.tensor_tensor(tab_pad[:, :], cnt[0:1, :], region[0:1, :], ALU.add))
            link(ve.tensor_scalar(cnt_i[:, :], cnt[:, :], float(P - 1), None, ALU.add))
            split_h(SHARED - 1, 1, banks=(0,))
            settle()
            link(ve.tensor_scalar(pair_i[:, :], cnt_i[:, :], BLK_SHIFT + 1, None, ALU.arith_shift_right))
            link(ve.tensor_scalar(blk_i[:, :], cnt_i[:, :], BLK_SHIFT, None, ALU.arith_shift_right), wait=True)
            link(ve.tensor_copy(pair[:, :], pair_i[:, :]))
            link(ve.tensor_copy(blk[:, :], blk_i[:, :]), wait=True)
            full_end, half_end = ends[:, 0, 1:], ends[:, 1, 1:]
            link(ve.tensor_tensor_scan(full_end, one_row[:, :], pair[:, :], 0.0, ALU.mult, ALU.add))
            split_h(SHARED - 1, 1, banks=(1,))
            settle()
            link(ve.tensor_scalar(full_end, full_end, float(FULLS), None, ALU.min), wait=True)
            link(ve.tensor_tensor(full[:, :], full_end, ends[:, 0, 0:EXPERTS], ALU.subtract))
            split_h(SHARED - 1, 1, banks=(2,))
            settle()
            link(ve.scalar_tensor_tensor(out=odd[:, :], in0=full[:, :], scalar=-2.0, in1=blk[:, :],
                                         op0=ALU.mult, op1=ALU.add))
            link(ve.scalar_tensor_tensor(out=half_from[:, :], in0=full[:, :], scalar=float(TILE), in1=region[:, :],
                                         op0=ALU.mult, op1=ALU.add))
            evict(SHARED - 2, 0, b_pj_s, part=0)
            settle()
            link(ve.tensor_tensor_scan(half_end, one_row[:, :], odd[:, :], 0.0, ALU.mult, ALU.add))
            split_h(SHARED - 1, 1, banks=(3,))
            settle()
            kinds = ((0, 0, FULLS), (1, FULLS, ROUTED))
            for kind, lo, hi in kinds:
                each = [1, hi - lo, EXPERTS]
                link(ve.tensor_tensor(past[:, lo:hi, :], step_no[:, lo:hi].unsqueeze(2).to_broadcast(each),
                                      ends[0:1, kind, 1:].unsqueeze(1).to_broadcast(each), ALU.is_ge))
            link(ve.scalar_tensor_tensor(out=base[:, 0, :], in0=ends[:, 0, 0:EXPERTS], scalar=-float(TILE), in1=region[:, :],
                                         op0=ALU.mult, op1=ALU.add))
            link(ve.scalar_tensor_tensor(out=base[:, 1, :], in0=ends[:, 1, 0:EXPERTS], scalar=-float(P), in1=half_from[:, :],
                                         op0=ALU.mult, op1=ALU.add))
            settle()
            link(ve.tensor_reduce(step_e[:, :], past[:, :, :], AX, ALU.add))
            link(ve.tensor_copy(step_b[:, 0:FULLS], step_at[:, 0:FULLS]))
            link(ve.tensor_scalar(step_b[:, FULLS:], step_at[:, FULLS:], base[0:1, 1, 0:1], None, ALU.add))
            link(ve.memset(base_up[:, :, EXPERTS - 1:], float(SPARE)))
            link(ve.tensor_tensor(base_up[:, :, 0:EXPERTS - 1], base[:, :, 1:], base[:, :, 0:EXPERTS - 1], ALU.subtract))
            settle()

            def in_order(tab, src, top):
                turns = tab[:, 0:MIXED].rearrange("o (n k) -> o k n", k=2)
                link(ve.tensor_scalar(turns[:, 0, :], src[:, 0:HALVES], float(top), None, ALU.min))
                link(ve.tensor_scalar(turns[:, 1, :], src[:, FULLS:], float(top), None, ALU.min))
                link(ve.tensor_scalar(tab[:, MIXED:], src[:, HALVES:FULLS], float(top), None, ALU.min))

            in_order(tab_e, step_e, EXPERTS - 1)
            evict(SHARED - 2, 0, b_pj_s, part=1)
            for kind, lo, hi in kinds:
                link(ve.tensor_tensor(past_up[:, lo:hi, :], past[:, lo:hi, :],
                                      base_up[0:1, kind, :].unsqueeze(1).to_broadcast([1, hi - lo, EXPERTS]), ALU.mult))
            settle()
            link(ve.tensor_reduce(step_r[:, :], past_up[:, :, :], AX, ALU.add), wait=True)
            link(ve.tensor_tensor(step_r[:, :], step_r[:, :], step_b[:, :], ALU.add), wait=True)
            in_order(tab_x, step_r, SPARE)

            evict(SHARED - 1, 1, b_pj_s)
            for m in range(KC // 2):
                dve.wait_ge(s_k_tr, m + 1)
                ve.tensor_copy(k_t[:, :, m * TILE:(m + 1) * TILE], key_banks[m].rearrange("p (c n) -> p c n", n=TILE)
                               ).then_inc(s_k_t, 1)
            copy_xt(SHARED, 0, stored=8 * SHARED)
            split_h(SHARED, 0, banks=(0, 1))
            copy_xt(SHARED + 1, 1, stored=8 * SHARED, n=P)
            split_h(SHARED, 0, banks=(2, 3))

            def evict2(j, par, half=False):
                dve.wait_ge(s_bpjx_in[par], nth(j, par))
                evict(SHARED + j, par, b_pj[par], 1 if half else SUB)

            def body2(j, par, prev=False, this=False, following=False):
                n = P if this else TILE
                split_h(SHARED + j, par, n, banks=(0, 1, 2))
                copy_xt(SHARED + j + 1, 1 - par, n=P if following else TILE)
                split_h(SHARED + j, par, n, banks=(3,))
                evict2(j - 1, 1 - par, prev)

            with pairs(dve, 1, MIXED - 1) as j:
                body2(j, 1, this=True)
                body2(j + 1, 0, prev=True, following=True)
            body2(MIXED - 1, 1, this=True)
            link, _ = chain(dve, s_y_rows, 0)
            every = [P, QT * TOP, EXPERTS]
            link(ve.tensor_tensor(half_shift[:, :], base[:, 0, :], base[:, 1, :], ALU.subtract))
            link(ve.tensor_tensor(match_e[:, :, :], exp_all[:, :].unsqueeze(2).to_broadcast(every),
                                  iota_e[:, :].unsqueeze(1).to_broadcast(every), ALU.is_equal))
            link(ve.tensor_tensor(past_e[:, :, :], pos_all[:, :].unsqueeze(2).to_broadcast(every),
                                  half_from[:, :].unsqueeze(1).to_broadcast(every), ALU.is_ge), wait=True)
            link(ve.tensor_scalar(half_shift[:, :], half_shift[:, :], float(FULLS * TILE), None, ALU.add), wait=True)
            link(ve.tensor_tensor(past_e[:, :, :], past_e[:, :, :], half_shift[:, :].unsqueeze(1).to_broadcast(every),
                                  ALU.mult))
            body2(MIXED, 0, prev=True)
            dve.wait_ge(s_y_rows, 5)
            link(ve.tensor_tensor(past_e[:, :, :], past_e[:, :, :], base[:, 0, :].unsqueeze(1).to_broadcast(every),
                                  ALU.subtract), wait=True)
            link(ve.tensor_tensor(match_e[:, :, :], match_e[:, :, :], past_e[:, :, :], ALU.mult), wait=True)
            link(ve.tensor_reduce(shift_t[:, :], match_e[:, :, :], AX, ALU.add), wait=True)
            link(ve.tensor_tensor(y_row_all[:, :], pos_all[:, :], shift_t[:, :], ALU.add))
            for h in range(2):
                dve.wait_ge(s_kv_hi, 3 + h)
                half = slice(h * KH, (h + 1) * KH)
                ve.tensor_tensor(v_split[:, 1, half, :], scale_b[h][:, :].rearrange("p (c n) -> p c n", c=KH),
                                 v_split[:, 0, half, :], ALU.subtract).then_inc(s_kv_lo, 1)
            with pairs(dve, MIXED + 1, ROUTED - 1) as j:
                body2(j, 1)
                body2(j + 1, 0)
            split_h(SHARED + ROUTED - 1, 1)
            evict2(ROUTED - 2, 0)

            def scale_scores(u, par, bpar, loaded, first=False):
                dve.wait_ge(s_qk, u + 1)
                if loaded is not None:
                    dve.wait_ge(s_sc_in[bpar], loaded)
                if not first:
                    dve.wait_ge(s_pt, 2 * (u - 1))
                dve.nop(nofuse=True)
                ve.tensor_tensor_reduce(out=prob[par][:, :], in0=ps_h[:, par * KEYS:(par + 1) * KEYS], in1=scale_b[bpar][:, :],
                                        scale=1.0, scalar=-3.0e38, op0=ALU.mult, op1=ALU.max,
                                        accum_out=row_max[par][:, 0:1]).then_inc(s_mul, 1)
                dve.wait_ge(s_mul, u + 1)
                ve.tensor_scalar(neg_max[par][:, :], row_max[par][:, :], -1.0, None, ALU.mult).then_inc(s_nm, 1)

            def p_lo(u, par, first=False):
                dve.wait_ge(s_exp, u + 1)
                if not first:
                    dve.wait_ge(s_fin, u - 1)
                ve.reciprocal(inv_sum[par][:, :], row_sum[par][:, :]).then_inc(s_inv, 1)
                for kk in range(2):
                    dve.wait_ge(s_phi, 2 * u + kk + 1)
                    ve.tensor_tensor(p_t[par][:, 1, 4 * kk:4 * kk + 4, :],
                                     ps_t[:, kk * 512:(kk + 1) * 512].rearrange("p (c n) -> p c n", n=P),
                                     p_t[par][:, 0, 4 * kk:4 * kk + 4, :], ALU.subtract).then_inc(s_plo, 1)

            def add_routed(u, par, first=False):
                dve.wait_ge(s_base, u + 1)
                dve.wait_ge(s_meta, 2 * u + 2)
                dve.wait_ge(s_gat[par], nth(u, par, 32))
                if not first:
                    dve.wait_ge(s_out[par], (u - par) * 8)
                for kk in range(TOP):
                    if kk:
                        dve.wait_ge(s_gated, 2 * u + 1)
                    ve.scalar_tensor_tensor(out=o_sb[par][:, :], in0=y_rows[par][:, kk, :], scalar=gate_u[par][:, kk:kk + 1],
                                            in1=o_sb[par][:, :] if kk else base_x[par][:, :], op0=ALU.mult, op1=ALU.add
                                            ).then_inc(s_gated, 1)

            def finish(u, par):
                dve.wait_ge(s_gated, 2 * u + 2)
                dve.wait_ge(s_inv, u + 1)
                dve.wait_ge(s_pv, u + 1)
                ve.scalar_tensor_tensor(out=o_sb[par][:, :], in0=ps_y[par][:, 0:D], scalar=inv_sum[par][:, 0:1],
                                        in1=o_sb[par][:, :], op0=ALU.mult, op1=ALU.add).then_inc(s_fin, 1)

            def body3(u0, g8, first=False, last=False):
                for s in range(8):
                    u, par = u0 + s, s % 2
                    if not (first and s == 0):
                        p_lo(u, par, first=first and s < 2)
                    if not (last and s >= 6):
                        n = s + 2
                        loaded = None
                        if n % 4 == 0:
                            loaded = (g8 + n // 8) * 16 + 16
                        scale_scores(u + 2, par, (n // 4) % 2, loaded)
                    if not (first and s == 0):
                        finish(u - 1, 1 - par)
                    add_routed(u, par, first=first and s < 2)

            dve.wait_ge(s_gexp, 1)
            link, _ = chain(dve, s_gate, 0)
            link(ve.tensor_scalar(gap_den[:, :], gap_exp[:, :], 1.0, None, ALU.add), wait=True)
            link(ve.reciprocal(gates[:, :, 0], gap_den[:, :]), wait=True)
            link(ve.tensor_tensor(gates[:, :, 1], gap_exp[:, :], gates[:, :, 0], ALU.mult))
            scale_scores(0, 0, 0, 16, first=True)
            evict2(ROUTED - 1, 1)
            p_lo(0, 0, first=True)
            scale_scores(1, 1, 0, None, first=True)

            body3(0, 0, first=True)
            with dve.Fori(1, QT // 8 - 1) as g3:
                g = dve.snap(g3)
                body3(g * 8, g)
            body3(QT - 8, QT // 8 - 1, last=True)
            finish(QT - 1, 1)

        @block.tensor
        def _(pe):
            mm = nc.tensor.matmul
            TERMS = ((0, 0), (0, 1), (1, 0))

            def transpose_rows(src, subs=SUB, out=tr16):
                for hl in range(2):
                    for c in range(DC):
                        for a in range(subs):
                            n = (hl * DC + c) * TILE + a * P
                            o = hl * D + c * P
                            ins = nc.tensor.transpose(out[:, n:n + P], src[:, a, o:o + P], ident_h[:, :])
                return ins

            def tr1(i, par):
                pe.wait_ge(s_lnb, (i + 1) * LNB)
                if not (isinstance(i, int) and i == 0):
                    pe.wait_ge(s_xt, i)
                transpose_rows(x_split[par]).then_inc(s_tr, 1)

            def tr2(j, par, half=False):
                pe.wait_ge(s_xs_in[par], nth(j, par))
                pe.wait_ge(s_xt, SHARED + j)
                transpose_rows(x_split[par], 1 if half else SUB).then_inc(s_tr, 1)

            def router(i, par):
                pe.wait_ge(s_xt, i + 1)
                if not (isinstance(i, int) and i == 0):
                    pe.wait_ge(s_rb, i * RB)
                for a in range(SUB):
                    for n in range(2 * DC):
                        ins = mm(lg_ps[:, a * 16:(a + 1) * 16], x_t[par][:, n, a * P:(a + 1) * P], wr_s[:, n % DC, :],
                                 start=n == 0, stop=n == 2 * DC - 1)
                ins.then_inc(s_logit, 1)

            def rank(i, par):
                pe.wait_ge(s_ra, (i + 1) * RA)
                for a in range(SUB):
                    o = rk_ps[:, a * EXPERTS:(a + 1) * EXPERTS]
                    mm(o, before[:, :], mask[par][:, a, :], start=True, stop=False)
                    if a == 1:
                        mm(o, ones_h[:, :], mask[par][:, 0, :], start=False, stop=False)
                    ins = mm(o, ones_h[:, :], mask_sum[:, :], start=False, stop=True)
                ins.then_inc(s_rank, 1)

            def up(t, par, w, banks=range(BANKS), cols=TILE):
                pe.wait_ge(s_xt, t + 1)
                wv = w[:, :].rearrange("p (h c n) -> p h c n", h=2, c=DC)
                for b in banks:
                    if not (isinstance(t, int) and t == 0):
                        pe.wait_ge(s_gelu, BANKS * (t - 1) + b + 1)
                    for hc in (2 * b, 2 * b + 1):
                        n = 0
                        for wl, xl in TERMS:
                            for c in range(DC):
                                ins = mm(ps_h[:, hc * TILE:hc * TILE + cols], wv[:, wl, c, hc * P:(hc + 1) * P],
                                         x_t[par][:, xl * DC + c, 0:cols], start=n == 0, stop=n == 3 * DC - 1)
                                n += 1
                    ins.then_inc(s_mm1, 1)

            def down(t, par, w, subs=range(SUB), each=1):
                pe.wait_ge(s_hlo, BANKS * (t + 1))
                wv = w[:, :].rearrange("p (h c n) -> p h c n", h=2, c=HC)
                for a in subs:
                    if not (isinstance(t, int) and t == 0):
                        pe.wait_ge(s_ev, 2 * (t - 1) + a + 1)
                    n = 0
                    for wl, xl in TERMS:
                        for c in range(HC):
                            ins = mm(ps_y[a][:, 0:D], h_split[par][:, xl, c, a * P:(a + 1) * P], wv[:, wl, c, :],
                                     start=n == 0, stop=n == 3 * HC - 1)
                            n += 1
                    ins.then_inc(s_mm2, each)

            pe.wait_ge(s_const, CONSTS)
            pe.wait_ge(s_bias_in, 32)
            nb = EXPERTS * HC + HC
            nc.tensor.transpose(bt_ps, b_rows[:, :], ident_f[0:nb, 0:nb]).then_inc(s_bt_tr, 1)
            tr1(0, 0)
            pe.wait_ge(s_wr, 3)
            pe.wait_ge(s_bt, 1)
            router(0, 0)
            for c in range(DC):
                pe.wait_ge(s_w0_lo[c], 1)
            up(0, 0, w_shared[0], (0, 1, 2))
            rank(0, 0)
            up(0, 0, w_shared[0], (3,))
            tr1(1, 1)
            router(1, 1)
            pe.wait_ge(s_wlo, 2)

            def body1(i, par):
                up(i, par, w_shared[0], (0, 1, 2))
                rank(i, par)
                up(i, par, w_shared[0], (3,))
                down(i - 1, 1 - par, w_shared[1], (0,))
                tr1(i + 1, 1 - par)
                down(i - 1, 1 - par, w_shared[1], (1,))
                router(i + 1, 1 - par)

            body1(1, 1)
            body1(2, 0)
            with pairs(pe, 3, SHARED - 1) as i:
                body1(i, 1)
                body1(i + 1, 0)
            up(SHARED - 1, 1, w_shared[0], (0, 1))
            rank(SHARED - 1, 1)
            up(SHARED - 1, 1, w_shared[0], (2, 3))
            pe.wait_ge(s_rb, SHARED * RB)
            mm(cn_ps, ones_h[:, :], mask_sum[:, :], start=True, stop=True).then_inc(s_count, 1)
            down(SHARED - 2, 0, w_shared[1])
            down(SHARED - 1, 1, w_shared[1])
            for m in range(KC // 2):
                pe.wait_ge(s_kv_lo, m // 2 + 1)
                pe.wait_ge(s_gelu, BANKS * (SHARED - 1) + m + 1)
                transpose_rows(k_split[m // 2][:, 2 * (m % 2):2 * (m % 2) + 2, :], out=key_banks[m]).then_inc(s_k_tr, 1)

            def up2(j, par, half=False):
                pe.wait_ge(s_wfc_in[par], nth(j, par))
                up(SHARED + j, par, w_fc[par], cols=P if half else TILE)

            def down2(j, par, half=False):
                pe.wait_ge(s_wpj_in[par], nth(j, par))
                if half:
                    down(SHARED + j, par, w_pj[par], subs=(0,), each=SUB)
                else:
                    down(SHARED + j, par, w_pj[par])

            def body2(j, par, prev=False, this=False, following=False):
                up2(j, par, this)
                tr2(j + 1, 1 - par, following)
                down2(j - 1, 1 - par, prev)

            tr2(0, 0)
            pe.wait_ge(s_k_t, KC // 2)
            up2(0, 0)
            tr2(1, 1, True)
            with pairs(pe, 1, MIXED - 1) as j:
                body2(j, 1, this=True)
                body2(j + 1, 0, prev=True, following=True)
            body2(MIXED - 1, 1, this=True)
            body2(MIXED, 0, prev=True)
            with pairs(pe, MIXED + 1, ROUTED - 1) as j:
                body2(j, 1)
                body2(j + 1, 0)
            up2(ROUTED - 1, 1)
            down2(ROUTED - 2, 0)

            def scores(u, par, mpar, loaded, first=False):
                if loaded is not None:
                    pe.wait_ge(s_q_in[mpar], loaded)
                if not first:
                    pe.wait_ge(s_mul, u - 1)
                for half in range(2):
                    n = 0
                    for kl, ql in TERMS:
                        for c in range(DC):
                            lo = par * KEYS + half * 512
                            ins = mm(ps_h[:, lo:lo + 512], q_t[mpar][:, ql * DC + c, par * P:(par + 1) * P],
                                     k_t[:, kl * DC + c, half * 512:(half + 1) * 512], start=n == 0, stop=n == 3 * DC - 1)
                            n += 1
                ins.then_inc(s_qk, 1)

            def transpose_probs(u, par, first=False):
                pe.wait_ge(s_exp, u + 1)
                for kk in range(2):
                    if not first:
                        pe.wait_ge(s_plo, 2 * (u - 1) + kk + 1)
                    for c in range(4 * kk, 4 * kk + 4):
                        ins = nc.tensor.transpose(ps_t[:, c * P:(c + 1) * P], prob[par][:, c * P:(c + 1) * P], ident_f[:, :])
                    ins.then_inc(s_pt, 1)

            def values(u, par, first=False):
                if first:
                    pe.wait_ge(s_ev, 2 * (SHARED + ROUTED - 1) + par + 1)
                else:
                    pe.wait_ge(s_fin, u - 1)
                n = 0
                for kk in range(2):
                    pe.wait_ge(s_plo, 2 * u + kk + 1)
                    for vl, pl in TERMS:
                        for c in range(4 * kk, 4 * kk + 4):
                            ins = mm(ps_y[par][:, 0:D], p_t[par][:, pl, c, :], v_split[:, vl, c, :],
                                     start=n == 0, stop=n == 3 * KC - 1)
                            n += 1
                ins.then_inc(s_pv, 1)

            def body3(u0, g8, first=False, last=False):
                for s in range(8):
                    u, par = u0 + s, s % 2
                    if not (first and s == 0) and not (last and s == 7):
                        transpose_probs(u, par)
                    if last and s == 6:
                        transpose_probs(u + 1, 1)
                    if not (last and s >= 6):
                        n = s + 2
                        loaded = None
                        if n % 2 == 0:
                            loaded = g8 * 32 + (n // 4) * 16 + 16
                        scores(u + 2, par, (n // 2) % 2, loaded)
                    values(u, par, first=first and s < 2)

            for b in range(BANKS):
                pe.wait_ge(s_gelu, BANKS * (SHARED + ROUTED - 1) + b + 1)
            pe.wait_ge(s_kv_lo, 4)
            scores(0, 0, 0, 16, first=True)
            down2(ROUTED - 1, 1)
            transpose_probs(0, 0, first=True)
            scores(1, 1, 0, None, first=True)
            body3(0, 0, first=True)
            with pe.Fori(1, QT // 8 - 1) as g3:
                g = pe.snap(g3)
                body3(g * 8, g)
            body3(QT - 8, QT // 8 - 1, last=True)


_INS = ["L0_attn_q", "L0_attn_k", "L0_attn_v", "L0_ffn_Wfc_s", "L0_ffn_bfc_s", "L0_ffn_Wproj_s", "L0_ffn_bproj_s",
        "L0_ffn_Wr", "L0_ffn_Wfc", "L0_ffn_bfc", "L0_ffn_Wproj", "L0_ffn_bproj"]
_OUTS = [((8, 512, 256), "float32")]


def kernel(**inputs):
    import numpy as _np
    import concourse.bacc as _bacc
    from concourse import mybir as _mybir
    from concourse.bass_utils import run_bass_kernel_spmd as _run

    nc = _bacc.Bacc("TRN2", target_bir_lowering=False, num_devices=1)
    arrays, args = {}, []
    for name in _INS:
        a = _np.ascontiguousarray(inputs[name])
        arrays[f"in_{name}_dram"] = a
        args.append(nc.dram_tensor(f"in_{name}_dram", a.shape, _mybir.dt.from_np(a.dtype), kind="ExternalInput").ap())
    for n, (shape, dtype) in enumerate(_OUTS):
        dt = _mybir.dt.from_np(_np.dtype(dtype))
        args.append(nc.dram_tensor(f"out_{n}_dram", shape, dt, kind="ExternalOutput").ap())
    moe_attention_block(nc, *args)
    r = _run(nc, [arrays], core_ids=[0])
    return r.results[0]["out_0_dram"]
```
